# Optimizing a Trainium2 kernel written in Bass

```python
import numpy as np
import jax
import jax.numpy as jnp

def _softmax(x, axis=-1):
    return jax.nn.softmax(x, axis=axis)

def _gelu(x):
    return jax.nn.gelu(x, approximate=True)

def _silu(x):
    return jax.nn.silu(x)

def _sigmoid(x):
    return jax.nn.sigmoid(x)

def _layernorm(x, axis=-1, eps=1e-05):
    m = jnp.mean(x, axis=axis, keepdims=True)
    v = jnp.var(x, axis=axis, keepdims=True)
    return (x - m) / jnp.sqrt(v + eps)

def _scatter_add(tgt, idx, src, axis=0):
    return tgt.at[idx].add(src)

def _segment_sum(src, seg, n):
    return jax.ops.segment_sum(src, seg, n)
kernel_name = 'mk_early_fusion_embed_d1_tok_img1024_r4_edacca'

def setup_inputs(seed: int=0):
    np.random.seed(seed)
    _w = jnp.asarray

    def _rec_inputs():
        import jax
        import jax.numpy as jnp
        _rk = jax.random.key(seed)
        x = 7.22013e-05 + 1.00017 * jax.random.normal(jax.random.fold_in(_rk, 1), (8, 64, 256, 4), jnp.float32)
        x_txt = jax.random.randint(jax.random.fold_in(_rk, 51), (8, 77), 0, 12564, jnp.int32)
        return (x, x_txt)
    x, x_txt = _rec_inputs()

    def _L0_tok_setup():
        import jax, jax.numpy as jnp
        import numpy as np
        B, F, L, H, D = (8, 64, 256, 4, 64)
        MODEL = H * F
        WIN = 128

        def _local_mask():
            m = np.ones((L, L), dtype=bool)
            m = np.tril(m, WIN - 1)
            m = np.triu(m, -(WIN - 1))
            return jnp.asarray(m)

        def _flatten(y):
            n = y.shape[0]
            return y.transpose(0, 2, 3, 1).reshape(n, L, -1)
        key = jax.random.key(seed)
        ks = jax.random.split(key, 12)
        s = lambda n: 1.0 / np.sqrt(n)
        xav = np.sqrt(6.0 / (L + L))
        return {'x': jax.random.normal(ks[0], (B, F, L, H), jnp.float32), 'Wq_w': jax.random.normal(ks[1], (D, F), jnp.float32) * s(F), 'Wq_b': jnp.zeros((D,), jnp.float32), 'Wk_w': jax.random.normal(ks[2], (D, F), jnp.float32) * s(F), 'Wk_b': jnp.zeros((D,), jnp.float32), 'Wv_w': jax.random.normal(ks[3], (D, F), jnp.float32) * s(F), 'Wv_b': jnp.zeros((D,), jnp.float32), 'w_bias': jax.random.uniform(ks[4], (L, L), jnp.float32, -xav, xav), 'out_w': jax.random.normal(ks[5], (H * D, MODEL), jnp.float32) * s(H * D), 'out_b': jnp.zeros((MODEL,), jnp.float32), 'ln_g': jnp.ones((MODEL,), jnp.float32), 'ln_b': jnp.zeros((MODEL,), jnp.float32), 'local_mask': _local_mask()}
    _L0_tok_all = _L0_tok_setup()
    _L0_tok_in = {k: v for k, v in _L0_tok_all.items() if k in ('Wq_w', 'Wq_b', 'Wk_w', 'Wk_b', 'Wv_w', 'Wv_b', 'w_bias', 'out_w', 'out_b', 'ln_g', 'ln_b', 'local_mask')}
    del _L0_tok_all

    def _L0_txt_setup():
        import jax, jax.numpy as jnp
        import numpy as np
        EMBD_D = 64
        LOCAL_D = 64
        VOCAB = 50257
        BATCH, SEQ = (8, 1024)

        def positional_encoding(max_len, d_model):
            depth = d_model // 2
            positions = jnp.arange(max_len, dtype=jnp.float32)[:, None]
            depths = jnp.arange(depth, dtype=jnp.float32)[None, :] / depth
            angle_rads = positions * (1.0 / 2500 ** depths)
            return jnp.concatenate([jnp.sin(angle_rads), jnp.cos(angle_rads)], axis=-1)

        def causal_conv1d(x, w, b, dilation):
            pad = (w.shape[0] - 1) * dilation
            y = jax.lax.conv_general_dilated(x, w, window_strides=(1,), padding=[(pad, 0)], rhs_dilation=(dilation,), dimension_numbers=('NWC', 'WIO', 'NWC'))
            return y + b

        def softpos(x, spos, n_subpos):
            sel = jax.nn.softmax(x[..., :n_subpos], axis=-1)
            return jnp.concatenate([x, jnp.einsum('bsn,nd->bsd', sel, spos)], axis=-1)
        key = jax.random.key(seed)
        k1, k2, k3, k4, k5 = jax.random.split(key, 5)
        return {'tokens': jax.random.randint(k1, (BATCH, SEQ), 0, VOCAB, dtype=jnp.int32), 'emb_table': jax.random.normal(k2, (VOCAB, EMBD_D), dtype=jnp.float32) * 0.02, 'conv_w': jax.random.normal(k3, (3, EMBD_D, LOCAL_D), dtype=jnp.float32) * 0.05, 'conv_b': jnp.zeros((LOCAL_D,), dtype=jnp.float32), 'spos0': jax.random.normal(k4, (LOCAL_D, LOCAL_D), dtype=jnp.float32) * 0.05, 'spos1': jax.random.normal(k5, (LOCAL_D, LOCAL_D), dtype=jnp.float32) * 0.05}
    _L0_txt_all = _L0_txt_setup()
    _L0_txt_in = {k: v for k, v in _L0_txt_all.items() if k in ('emb_table', 'conv_w', 'conv_b', 'spos0', 'spos1')}
    del _L0_txt_all

    def _L0_attn_setup():
        import jax, jax.numpy as jnp
        import numpy as np
        key = jax.random.key(seed)
        ks = jax.random.split(key, 5)
        B, S, D = (2, 512, 256)
        scale = 0.02
        return {'x': jax.random.normal(ks[0], (B, S, D), dtype=jnp.float32), 'q_proj_weight': jax.random.normal(ks[1], (D, D), dtype=jnp.float32) * scale, 'k_proj_weight': jax.random.normal(ks[2], (D, D), dtype=jnp.float32) * scale, 'v_proj_weight': jax.random.normal(ks[3], (D, D), dtype=jnp.float32) * scale, 'o_proj_weight': jax.random.normal(ks[4], (D, D), dtype=jnp.float32) * scale}
    _L0_attn_all = _L0_attn_setup()
    _L0_attn_in = {k: v for k, v in _L0_attn_all.items() if k in ('q_proj_weight', 'k_proj_weight', 'v_proj_weight', 'o_proj_weight')}
    del _L0_attn_all

    def _L0_ffn_setup():
        import jax, jax.numpy as jnp
        import numpy as np
        DIM = 256
        HIDDEN = 768
        SCALE = 1.0 / 127.0

        def _dequant(w_int, dtype):
            return w_int.astype(dtype) * jnp.asarray(SCALE, dtype)
        key = jax.random.key(seed)
        k_x, k_g, k_u, k_d = jax.random.split(key, 4)
        x = jax.random.normal(k_x, (4, 512, DIM), dtype=jnp.float32)
        w_gate = jax.random.randint(k_g, (HIDDEN, DIM), -127, 128, dtype=jnp.int32)
        w_up = jax.random.randint(k_u, (HIDDEN, DIM), -127, 128, dtype=jnp.int32)
        w_down = jax.random.randint(k_d, (DIM, HIDDEN), -127, 128, dtype=jnp.int32)
        return {'x': x, 'w_gate': w_gate, 'w_up': w_up, 'w_down': w_down}
    _L0_ffn_all = _L0_ffn_setup()
    _L0_ffn_in = {k: v for k, v in _L0_ffn_all.items() if k in ('w_gate', 'w_up', 'w_down')}
    del _L0_ffn_all
    return {'x': x, 'x_txt': x_txt, 'L0_tok_Wq_w': _L0_tok_in['Wq_w'], 'L0_tok_Wq_b': _L0_tok_in['Wq_b'], 'L0_tok_Wk_w': _L0_tok_in['Wk_w'], 'L0_tok_Wk_b': _L0_tok_in['Wk_b'], 'L0_tok_Wv_w': _L0_tok_in['Wv_w'], 'L0_tok_Wv_b': _L0_tok_in['Wv_b'], 'L0_tok_w_bias': _L0_tok_in['w_bias'], 'L0_tok_out_w': _L0_tok_in['out_w'], 'L0_tok_out_b': _L0_tok_in['out_b'], 'L0_tok_ln_g': _L0_tok_in['ln_g'], 'L0_tok_ln_b': _L0_tok_in['ln_b'], 'L0_tok_local_mask': _L0_tok_in['local_mask'], 'L0_txt_emb_table': _L0_txt_in['emb_table'], 'L0_txt_conv_w': _L0_txt_in['conv_w'], 'L0_txt_conv_b': _L0_txt_in['conv_b'], 'L0_txt_spos0': _L0_txt_in['spos0'], 'L0_txt_spos1': _L0_txt_in['spos1'], 'L0_attn_q_proj_weight': _L0_attn_in['q_proj_weight'], 'L0_attn_k_proj_weight': _L0_attn_in['k_proj_weight'], 'L0_attn_v_proj_weight': _L0_attn_in['v_proj_weight'], 'L0_attn_o_proj_weight': _L0_attn_in['o_proj_weight'], 'L0_ffn_w_gate': _L0_ffn_in['w_gate'], 'L0_ffn_w_up': _L0_ffn_in['w_up'], 'L0_ffn_w_down': _L0_ffn_in['w_down']}

def reference(x, x_txt, L0_tok_Wq_w, L0_tok_Wq_b, L0_tok_Wk_w, L0_tok_Wk_b, L0_tok_Wv_w, L0_tok_Wv_b, L0_tok_w_bias, L0_tok_out_w, L0_tok_out_b, L0_tok_ln_g, L0_tok_ln_b, L0_tok_local_mask, L0_txt_emb_table, L0_txt_conv_w, L0_txt_conv_b, L0_txt_spos0, L0_txt_spos1, L0_attn_q_proj_weight, L0_attn_k_proj_weight, L0_attn_v_proj_weight, L0_attn_o_proj_weight, L0_ffn_w_gate, L0_ffn_w_up, L0_ffn_w_down):
    import jax
    import jax.numpy as jnp

    def _L0_tok_ref(x, Wq_w, Wq_b, Wk_w, Wk_b, Wv_w, Wv_b, w_bias, out_w, out_b, ln_g, ln_b, local_mask):
        import jax, jax.numpy as jnp
        import numpy as np
        B, F, L, H, D = (8, 64, 256, 4, 64)
        MODEL = H * F
        WIN = 128

        def _local_mask():
            m = np.ones((L, L), dtype=bool)
            m = np.tril(m, WIN - 1)
            m = np.triu(m, -(WIN - 1))
            return jnp.asarray(m)

        def _flatten(y):
            n = y.shape[0]
            return y.transpose(0, 2, 3, 1).reshape(n, L, -1)

        def proj(w, b):
            y = jnp.einsum('nclh,dc->ndlh', x, w) + b[None, :, None, None]
            return _flatten(y)
        q = proj(Wq_w, Wq_b)
        k = proj(Wk_w, Wk_b)
        v = proj(Wv_w, Wv_b)
        wb = w_bias * local_mask.astype(w_bias.dtype)
        ew = jnp.exp(wb)
        ek = jnp.exp(k)
        num = jnp.einsum('ts,nsd->ntd', ew, ek * v)
        den = jnp.einsum('ts,nsd->ntd', ew, ek)
        y = jax.nn.sigmoid(q) * num / den
        h = y @ out_w + out_b + _flatten(x)
        mu = jnp.mean(h, axis=-1, keepdims=True)
        var = jnp.mean(jnp.square(h - mu), axis=-1, keepdims=True)
        return (h - mu) * jax.lax.rsqrt(var + 1e-05) * ln_g + ln_b

    def _L0_txt_ref(tokens, emb_table, conv_w, conv_b, spos0, spos1):
        import jax, jax.numpy as jnp
        import numpy as np
        EMBD_D = 64
        LOCAL_D = 64
        VOCAB = 50257
        BATCH, SEQ = (8, 1024)

        def positional_encoding(max_len, d_model):
            depth = d_model // 2
            positions = jnp.arange(max_len, dtype=jnp.float32)[:, None]
            depths = jnp.arange(depth, dtype=jnp.float32)[None, :] / depth
            angle_rads = positions * (1.0 / 2500 ** depths)
            return jnp.concatenate([jnp.sin(angle_rads), jnp.cos(angle_rads)], axis=-1)

        def causal_conv1d(x, w, b, dilation):
            pad = (w.shape[0] - 1) * dilation
            y = jax.lax.conv_general_dilated(x, w, window_strides=(1,), padding=[(pad, 0)], rhs_dilation=(dilation,), dimension_numbers=('NWC', 'WIO', 'NWC'))
            return y + b

        def softpos(x, spos, n_subpos):
            sel = jax.nn.softmax(x[..., :n_subpos], axis=-1)
            return jnp.concatenate([x, jnp.einsum('bsn,nd->bsd', sel, spos)], axis=-1)
        seq = tokens.shape[1]
        x = emb_table[tokens] * jnp.sqrt(jnp.float32(EMBD_D)) + positional_encoding(seq, EMBD_D)
        x1 = causal_conv1d(x, conv_w, conv_b, dilation=1)
        y0 = softpos(x, spos0, LOCAL_D)
        y1 = softpos(x1, spos1, LOCAL_D)
        return jnp.concatenate([y0, y1], axis=-1)

    def _L0_attn_ref(x, q_proj_weight, k_proj_weight, v_proj_weight, o_proj_weight):
        import jax, jax.numpy as jnp
        import numpy as np
        num_heads = 16
        B, S, d_in = x.shape
        d_k = q_proj_weight.shape[0]
        head_size = d_k // num_heads

        def split_heads(t):
            return t.reshape(B, S, num_heads, head_size).transpose(0, 2, 1, 3)
        q = split_heads(jnp.einsum('bsd,kd->bsk', x, q_proj_weight))
        k = split_heads(jnp.einsum('bsd,kd->bsk', x, k_proj_weight))
        v = split_heads(jnp.einsum('bsd,kd->bsk', x, v_proj_weight))
        scale = jnp.float32(head_size) ** (-0.5)
        scores = jnp.einsum('bhtc,bhkc->bhtk', q, k) * scale
        causal = jnp.tril(jnp.ones((S, S), dtype=bool))
        scores = jnp.where(causal, scores, -jnp.inf)
        attn = jax.nn.softmax(scores, axis=-1)
        out = jnp.einsum('bhtk,bhkc->bhtc', attn, v)
        out = out.transpose(0, 2, 1, 3).reshape(B, S, d_k)
        return jnp.einsum('bsv,dv->bsd', out, o_proj_weight)

    def _L0_ffn_ref(x, w_gate, w_up, w_down):
        import jax, jax.numpy as jnp
        import numpy as np
        DIM = 256
        HIDDEN = 768
        SCALE = 1.0 / 127.0

        def _dequant(w_int, dtype):
            return w_int.astype(dtype) * jnp.asarray(SCALE, dtype)
        wg = _dequant(w_gate, x.dtype)
        wu = _dequant(w_up, x.dtype)
        wd = _dequant(w_down, x.dtype)
        gate = jnp.einsum('bsd,hd->bsh', x, wg)
        up = jnp.einsum('bsd,hd->bsh', x, wu)
        h = jax.nn.silu(gate) * up
        return jnp.einsum('bsh,dh->bsd', h, wd)
    h = _L0_tok_ref(x, L0_tok_Wq_w, L0_tok_Wq_b, L0_tok_Wk_w, L0_tok_Wk_b, L0_tok_Wv_w, L0_tok_Wv_b, L0_tok_w_bias, L0_tok_out_w, L0_tok_out_b, L0_tok_ln_g, L0_tok_ln_b, L0_tok_local_mask)
    h = jnp.concatenate([h, _L0_txt_ref(x_txt, L0_txt_emb_table, L0_txt_conv_w, L0_txt_conv_b, L0_txt_spos0, L0_txt_spos1)], axis=1)
    h = h + _L0_attn_ref(_layernorm(h, axis=-1), L0_attn_q_proj_weight, L0_attn_k_proj_weight, L0_attn_v_proj_weight, L0_attn_o_proj_weight)
    h = h + _L0_ffn_ref(_layernorm(h, axis=-1), L0_ffn_w_gate, L0_ffn_w_up, L0_ffn_w_down)
    return h

_drawn_inputs = setup_inputs


def setup_inputs(seed=0):
    import zlib

    import numpy as np

    out = dict(_drawn_inputs(seed))
    spreads = {'L0_tok_Wq_b': (0.0, 0.8),
     'L0_tok_Wk_b': (0.0, 0.8),
     'L0_tok_Wv_b': (0.0, 0.1),
     'L0_tok_out_b': (0.0, 0.1),
     'L0_tok_ln_g': (1.0, 0.2),
     'L0_tok_ln_b': (0.0, 0.1),
     'L0_txt_conv_b': (0.0, 0.1)}
    factors = {'L0_tok_w_bias': 8.0,
     'L0_txt_spos0': 8.0,
     'L0_txt_spos1': 8.0,
     'L0_attn_q_proj_weight': 8.0,
     'L0_attn_k_proj_weight': 8.0}
    for name, (base, spread) in spreads.items():
        noise = np.random.default_rng([zlib.crc32(name.encode()), seed]).standard_normal(out[name].shape)
        drawn = base * np.exp(spread * noise) if base else spread * noise
        out[name] = jnp.asarray(drawn.astype(out[name].dtype))
    for name, factor in factors.items():
        out[name] = (out[name] * factor).astype(out[name].dtype)
    return out
```

```python
from contextlib import ExitStack

import concourse.bass as bass
from concourse import mybir

B, F, L, H4, D = 8, 64, 256, 4, 64
MODEL = H4 * F
T = 77
S = L + T
HEADS, HD = 16, 16
HIDDEN = 768
P = 128
TILES = [(0, P), (P, P), (2 * P, T)]
KEND = [P, 2 * P, S]
QW = [S, S - P, T]
QOFF = [0, S, 2 * S - P]
PW = sum(QW)
CH = MODEL // P
HC = HIDDEN // P
SB = -(-S // 32)
EPS = 1e-5
PARTS_Q = [0, 1, 2, 0, 1, 0]
PARTS_K = [0, 0, 0, 1, 1, 2]
STK = HD * len(PARTS_Q)
MASKED = -1e30
HSCALE = 2.0 ** -4
MIX_DVE = 12
LN_STEPS = 10

SM = [(0, 8 * u, 8, 4) for u in range(2)] + [(1, 4 * u, 4, 2) for u in range(4)] + \
     [(2, 2 * u, 2, 1) for u in range(8)]


def build(nc, x_mix, x_flat, tokens, pos, wkv, wq, bq, ebk_in, bv_in, wbt, maskt, outw, rows3,
          emb, convw, spos, wqkv_t, wo_t, wgu, wd, out):
    f32, bf16, f16 = mybir.dt.float32, mybir.dt.bfloat16, mybir.dt.float16
    i32, u8 = mybir.dt.int32, mybir.dt.uint8
    ALU, ACT, AX = mybir.AluOpType, mybir.ActivationFunctionType, mybir.AxisListType

    ctx = ExitStack()
    with ctx:
        def sb(name, shape, dt=f32):
            return ctx.enter_context(nc.sbuf_tensor(name, shape, dt))

        def sem(name):
            return ctx.enter_context(nc.semaphore(name))

        resid = sb("resid", [P, B, 3, MODEL])
        ident = sb("ident", [P, P])
        identb = sb("identb", [P, P], bf16)
        causal = sb("causal", [P, P], bf16)
        tok_sb = sb("tok_sb", [T, B], i32)
        pos_sb = sb("pos_sb", [T, F])
        emb_sb = sb("emb_sb", [T, B, F])
        conv_sb = sb("conv_sb", [F + 1, 3, F])
        spos_sb = sb("spos_sb", [F, 2, F])
        xcT = sb("xcT", [F + 1, B, T + 2])
        selx = sb("selx", [T, 2, B, F])
        smx = sb("smx", [T, 2, B])
        ssum = sb("ssum", [T, 2, B])
        srec = sb("srec", [T, 2, B])
        selT = sb("selT", [F, 2, B, T])
        wkv_sb = sb("wkv_sb", [P, 4 * F])
        wq_sb = sb("wq_sb", [P, P])
        bq_sb = sb("bq_sb", [P, 1])
        bqh = sb("bqh", [P, 1])
        bk_sb = sb("bk_sb", [P, 1])
        ebk = sb("ebk", [P, 1])
        ebk2 = sb("ebk2", [P, 1])
        bv_sb = sb("bv_sb", [P, 1])
        bvh = sb("bvh", [P, 1])
        wb_sb = sb("wb_sb", [P, 2, L])
        mask_sb = sb("mask_sb", [P, 2, L], u8)
        wbm = sb("wbm", [P, 2, L])
        ew = sb("ew", [P, 2, L])
        outw_sb = sb("outw_sb", [P, CH, MODEL])
        rows_sb = sb("rows_sb", [P, 3, MODEL])
        xs = sb("xs", [P, 2, L])
        xf = sb("xf", [P, 2, MODEL])
        xfb = sb("xfb", [P, 2, MODEL])
        ekv = sb("ekv", [P, 2, 2, MODEL])
        tq = sb("tq", [P, CH, L])
        sg = sb("sg", [P, CH, L])
        rden = sb("rden", [P, CH, L])
        yr = sb("yr", [P, CH, L])
        yT = sb("yT", [P, CH, L])
        hpre = sb("hpre", [P, 2, MODEL])
        hn = sb("hn", [P, 2, MODEL])
        hg = sb("hg", [P, 2, MODEL])
        st_m = sb("st_m", [P, 2, 6])
        mv_m = sb("mv_m", [P, 2, 2])
        ve_m = sb("ve_m", [P, 2])
        rs_m = sb("rs_m", [P, 2])
        nhalf = sb("nhalf", [P, 3])
        wqkv_sb = sb("wqkv_sb", [P, 3, CH, MODEL])
        wo_sb = sb("wo_sb", [P, 4, MODEL])
        st_a = sb("st_a", [P, 3, 6])
        mv_a = sb("mv_a", [P, 3, 2])
        ve_a = sb("ve_a", [P, 3])
        rs_a = sb("rs_a", [P, 3])
        xln = sb("xln", [P, 3, MODEL])
        xlnT = sb("xlnT", [P, CH, S])
        parts = sb("parts", [P, 3, 4, S], bf16)
        rest = sb("rest", [P, 4, S])
        qstack = [sb(f"qstack{p}", [P, HEADS * S], bf16) for p in range(2)]
        kstack = [sb(f"kstack{p}", [P, HEADS * S], bf16) for p in range(2)]
        QS, KS = ([x[:, :].rearrange("p (h t) -> p h t", h=HEADS) for x in xs2] for xs2 in (qstack, kstack))
        V = [sb(f"V{p}", [P, 3, HEADS, 32]) for p in range(2)]
        mx = sb("mx", [P, 3, HEADS])
        mhl = sb("mhl", [P, 3, 2, HEADS], bf16)
        mT = sb("mT", [2 * HEADS, S], bf16)
        probs = sb("probs", [P, 4, 2, PW])
        denT = sb("denT", [P, SB * 32])
        denr = sb("denr", [P, SB])
        scale = sb("scale", [P, SB * 32])
        OT = sb("OT", [P, 4, S])
        st_f = sb("st_f", [P, 3, 6])
        mv_f = sb("mv_f", [P, 3, 2])
        ve_f = sb("ve_f", [P, 3])
        rs_f = sb("rs_f", [P, 3])
        wgu_sb = sb("wgu_sb", [P, 2, CH, HIDDEN], f16)
        wd_sb = sb("wd_sb", [P, HC, MODEL], f16)
        ost = sb("ost", [P, 3, MODEL])
        q16 = qstack[0][:, :].bitcast(f16)
        xfh, xfl, hTh, hTl = (q16[:, a * S:b * S].rearrange("p (c t) -> p c t", t=S)
                              for a, b in ((0, 2), (2, 4), (4, 4 + HC), (4 + HC, 4 + 2 * HC)))
        k32 = kstack[0][:, :].bitcast(f32)
        tg, ag, hh = (k32[:, a * S:(a + 2) * S].rearrange("p (c t) -> p c t", t=S) for a in (0, 2, 4))
        stage = probs[:, :, :, :].rearrange("p a b c -> p (a b c)")
        stage_gu = stage[:, 0:2 * CH * HIDDEN].bitcast(i32).rearrange("p (a c n) -> p a c n", a=2, c=CH)
        stage_d = stage[:, 2 * CH * HIDDEN:2 * CH * HIDDEN + HC * MODEL].bitcast(i32) \
            .rearrange("p (c n) -> p c n", c=HC)

        bank = [ctx.enter_context(nc.psum_tensor(f"bank{i}", [P, 1024], f32)) for i in range(4)]
        half = [bank[0], bank[1]]
        PB = [bank[2][:, 0:512], bank[2][:, 512:1024]]
        OB, MB = bank[3][:, 0:512], bank[3][:, 512:1024]

        qk_dram = [nc.dram_tensor(f"qk_parts{p}", [2, 3, MODEL, S], bf16).ap() for p in range(2)]
        m_dram = [nc.dram_tensor(f"max_rows{p}", [2 * HEADS, S], bf16).ap() for p in range(2)]

        names = """loaded_text loaded_mixw loaded_wb loaded_rows loaded_attw loaded_ffw consts_ready gathered
        text_dve text_tr text_act text_mm ffw_cast mix_consts ew_ready
        x_loaded xf_loaded xfb_ready kv_mm q_mm ek_ready tq_ready ekv_ready sg_ready nd_mm
        mixout_mm mix_dve mix_rstd att_rstd ffn_rstd hg_ready resid_ready
        att_ln xt_tr xt_copied qk_mm part1 rest_ready part2 part3 v_mm v_copied stack_ones
        parts_stored stacked0 stacked1 row_max_mm row_max maxima_ready mt_tr mt_copied m_stored m_loaded
        st_mm exp_done selected pv_mm norm_steps normed oproj_mm attn_added
        ffn_ln fxt_tr fx_hi fx_lo gu_mm tanh_done a_ready h_ready h_hi h_lo down_mm final_ready
        out_stored held_pool held_dve""".split()
        s = {n: sem(n) for n in names}

        block = ctx.enter_context(nc.Block())

        def head_rows(h):
            return h * HD

        @block.sync
        def _(sp):
            def load(dst, src, name):
                sp.dma_start(dst, src).then_inc(s[name], 16)

            load(tok_sb[:, :], tokens, "loaded_text")
            load(pos_sb[:, :], pos, "loaded_text")
            load(conv_sb[:, :, :], convw, "loaded_text")
            load(spos_sb[:, :, :], spos, "loaded_text")
            load(wkv_sb[:, :], wkv, "loaded_mixw")
            load(wq_sb[:, :], wq, "loaded_mixw")
            load(bq_sb[:, :], bq, "loaded_mixw")
            load(bk_sb[:, :], ebk_in, "loaded_mixw")
            load(bv_sb[:, :], bv_in, "loaded_mixw")
            load(outw_sb[:, :, :], outw, "loaded_mixw")
            load(wb_sb[:, :, :], wbt, "loaded_wb")
            load(mask_sb[:, :, :], maskt, "loaded_wb")
            load(rows_sb[:, :, :], rows3, "loaded_rows")

            def load_x(n):
                load(xs[:, :, :], x_mix[bass.ds(n, 1)].rearrange("a p h l -> (a p) h l"), "x_loaded")

            def load_xf(n):
                load(xf[:, :, :], x_flat[bass.ds(n, 1)].rearrange("a p t m -> (a p) t m"), "xf_loaded")

            load_x(0)
            load_xf(0)
            load(wqkv_sb[:, :, :, :], wqkv_t, "loaded_attw")
            load(wo_sb[:, :, :], wo_t, "loaded_attw")
            load(stage_gu, wgu, "loaded_ffw")
            load(stage_d, wd, "loaded_ffw")
            with sp.Fori(1, B) as n:
                sp.wait_ge(s["q_mm"], n)
                load_x(n)
                sp.wait_ge(s["xfb_ready"], n)
                load_xf(n)

            def store_parts(n, par):
                sp.wait_ge(s["part3"], 4 * n + 4)
                sp.wait_ge(s["part2"], 4 * n + 4)
                for qk in range(2):
                    for part in range(3):
                        sp.dma_start(qk_dram[par][qk, part].rearrange("(c p) t -> p c t", p=P),
                                     parts[:, part, 2 * qk:2 * qk + 2, :]).then_inc(s["parts_stored"], 16)

            def load_stacks(n, par, reused=True):
                sp.wait_ge(s["parts_stored"], 96 * (n + 1))
                if reused:
                    sp.wait_ge(s["st_mm"], 16 * (n - 1))
                for qk, (dst, order) in enumerate([(QS[par], PARTS_Q), (KS[par], PARTS_K)]):
                    for r, part in enumerate(order):
                        sp.dma_start(dst[HD * r:HD * r + HD, :, :],
                                     qk_dram[par][qk, part].rearrange("(h i) t -> i h t", i=HD)) \
                            .then_inc(s[f"stacked{par}"], 16)

            def max_rows(n, par):
                sp.wait_ge(s["mt_copied"], n + 1)
                sp.dma_start(m_dram[par], mT[:, :]).then_inc(s["m_stored"], 16)
                sp.wait_ge(s["m_stored"], 16 * (n + 1))
                sp.dma_start(QS[par][STK:STK + 2, :, :], m_dram[par].rearrange("(r h) t -> r h t", r=2)) \
                    .then_inc(s["m_loaded"], 16)

            def step(n, par, reused=True):
                store_parts(n + 1, 1 - par)
                max_rows(n, par)
                load_stacks(n + 1, 1 - par, reused)

            store_parts(0, 0)
            load_stacks(0, 0, False)
            step(0, 0, False)
            with sp.Fori(0, (B - 2) // 2) as i:
                step(2 * i + 1, 1)
                step(2 * i + 2, 0)
            max_rows(B - 1, 1)

            def store_out(n):
                sp.wait_ge(s["final_ready"], 3 * n + 3)
                for dst, src in ((out[bass.ds(n, 1), 0:L, :].rearrange("a (t p) m -> p (a t) m", p=P),
                                  ost[:, 0:2, :]),
                                 (out[bass.ds(n, 1), L:S, :].rearrange("a p m -> (a p) m"), ost[0:T, 2, :])):
                    sp.dma_start(dst, src).then_inc(s["out_stored"], 16)

            with sp.Fori(0, B) as n:
                store_out(n)
            sp.wait_ge(s["out_stored"], 32 * B)
            sp.wait_ge(s["m_loaded"], 16 * B)

        @block.gpsimd
        def _(pool):
            g = nc.gpsimd
            g.memset(ident[:, :], 0.0).then_inc(s["consts_ready"], 1)
            g.memset(identb[:, :], 0.0).then_inc(s["consts_ready"], 1)
            g.memset(causal[:, :], 0.0).then_inc(s["consts_ready"], 1)
            g.memset(nhalf[:, :], -0.5).then_inc(s["consts_ready"], 1)
            pool.wait_ge(s["consts_ready"], 4)
            for m in (ident, identb):
                g.affine_select(out=m[:, :], in_=m[:, :], compare_op=ALU.not_equal, fill=1.0, base=0,
                                pattern=[[-1, P]], channel_multiplier=1).then_inc(s["consts_ready"], 1)
            g.affine_select(out=causal[:, :], in_=causal[:, :], compare_op=ALU.is_ge, fill=MASKED, base=0,
                            pattern=[[-1, P]], channel_multiplier=1).then_inc(s["consts_ready"], 1)
            pool.wait_ge(s["loaded_text"], 64)
            for n in range(B):
                g.indirect_dma_start(emb_sb[:, n, :], None, emb,
                                     bass.IndirectOffsetOnAxis(tok_sb[:, n:n + 1], 0)) \
                    .then_inc(s["gathered"], 16)
            for p in range(2):
                g.memset(V[p][:, :, :, HD:32], 0.0).then_inc(s["stack_ones"], 1)
            for p in range(2):
                pool.wait_ge(s["stack_ones"], 2 + p)
                g.memset(KS[p][STK:P, :, :], 1.0).then_inc(s["stack_ones"], 1)
            pool.wait_ge(s["stack_ones"], 4)
            for p in range(2):
                g.memset(V[p][:, :, :, HD:HD + 1], 1.0).then_inc(s["stack_ones"], 1)

            pool.wait_ge(s["loaded_rows"], 16)
            bias_row, gain_row, shift_row = (rows_sb[:, r:r + 1, :].to_broadcast([P, 2, MODEL]) for r in range(3))

            def residual_in(n):
                pool.wait_ge(s["xf_loaded"], 16 * (n + 1))
                if not (isinstance(n, int) and n == 0):
                    pool.wait_ge(s["mix_dve"], MIX_DVE * (n - 1) + 5)
                g.tensor_tensor(xfb[:, :, :], xf[:, :, :], bias_row, ALU.add).then_inc(s["xfb_ready"], 1)

            def inverse_root(n, counted, count, dst, src, done):
                pool.wait_ge(s[counted], count)
                g.tensor_tensor(dst[:, :], src[:, :], nhalf[:, 0:src.shape[1]], ALU.pow).then_inc(s[done], 1)

            def gain(n):
                inverse_root(n, "mix_dve", MIX_DVE * n + 10, rs_m, ve_m, "mix_rstd")
                pool.wait_ge(s["mix_dve"], MIX_DVE * (n + 1))
                g.tensor_tensor(hg[:, :, :], hn[:, :, :], gain_row, ALU.mult).then_inc(s["hg_ready"], 1)
                pool.wait_ge(s["hg_ready"], n + 1)
                g.tensor_tensor(resid[:, bass.ds(n, 1), 0:2, :].rearrange("p a t m -> p (a t) m"), hg[:, :, :],
                                shift_row, ALU.add).then_inc(s["resid_ready"], 1)

            residual_in(0)
            with pool.Fori(1, B) as n:
                residual_in(n)
                gain(n - 1)
            gain(B - 1)

            def third_parts(n):
                for c in range(4):
                    pool.wait_ge(s["part2"], 4 * n + c + 1)
                    g.tensor_tensor(parts[:, 2, c, :], rest[:, c, :], parts[:, 1, c, :], ALU.subtract) \
                        .then_inc(s["part3"], 1)

            def keep_past(n):
                for k in range(8):
                    for kt, (_, rows) in enumerate(TILES):
                        pool.wait_ge(s["exp_done"], 24 * n + 3 * k + kt + 1)
                        pool.sem_inc(s["held_pool"], 1)
                        blk = probs[0:rows, k % 4, :, QOFF[kt]:QOFF[kt] + rows]
                        g.affine_select(out=blk, in_=blk, compare_op=ALU.is_ge, fill=0.0, base=0,
                                        pattern=[[0, 2], [1, rows]], channel_multiplier=-1) \
                            .then_inc(s["selected"], 1)

            def att_inverse_root(n):
                inverse_root(n, "att_ln", LN_STEPS * n + 7, rs_a, ve_a, "att_rstd")

            att_inverse_root(0)
            third_parts(0)
            with pool.Fori(0, B - 1) as n:
                att_inverse_root(n + 1)
                pool.wait_ge(s["parts_stored"], 96 * (n + 1))
                third_parts(n + 1)
                keep_past(n)
            keep_past(B - 1)

            def low_halves(n):
                for c in range(HC):
                    pool.wait_ge(s["h_hi"], HC * n + c + 1)
                    g.tensor_tensor(hTl[:, c, :], hh[:, c % 2, :], hTh[:, c, :], ALU.subtract) \
                        .then_inc(s["h_lo"], 1)

            with pool.Fori(0, B) as n:
                inverse_root(n, "ffn_ln", LN_STEPS * n + 7, rs_f, ve_f, "ffn_rstd")
                low_halves(n)

        @block.scalar
        def _(act):
            a = nc.scalar
            act.wait_ge(s["text_dve"], 10)
            a.activation(selx[:, :, :, :], selx[:, :, :, :], ACT.Exp).then_inc(s["text_act"], 1)
            act.wait_ge(s["mix_consts"], 1)
            a.activation(ew[:, :, :], wbm[:, :, :], ACT.Exp).then_inc(s["ew_ready"], 1)
            act.wait_ge(s["loaded_mixw"], 96)
            a.activation(ebk[:, :], bk_sb[:, :], ACT.Exp).then_inc(s["ew_ready"], 1)
            a.mul(bqh[:, :], bq_sb[:, :], 0.5).then_inc(s["ew_ready"], 1)
            act.wait_ge(s["ew_ready"], 3)
            a.mul(ebk2[:, :], ebk[:, :], 2.0).then_inc(s["ew_ready"], 1)

            def mixer_exps(n):
                first = isinstance(n, int) and n == 0
                for t in range(2):
                    act.wait_ge(s["kv_mm"], 2 * n + t + 1)
                    if not first and t == 0:
                        act.wait_ge(s["nd_mm"], n)
                    kv = half[0][:, 512 * t:512 * t + 512].rearrange("p (h w) -> p h w", h=2)
                    a.activation(ekv[:, t, 1, :].rearrange("p (h w) -> p h w", h=2), kv[:, :, 0:P], ACT.Exp) \
                        .then_inc(s["ek_ready"], 1)
                act.wait_ge(s["q_mm"], n + 1)
                if not first:
                    act.wait_ge(s["sg_ready"], n)
                a.activation(tq[:, :, :], PB[0].rearrange("p (c l) -> p c l", c=CH), ACT.Tanh, scale=0.5,
                             bias=bqh[:, 0:1]).then_inc(s["tq_ready"], 1)

            mixer_exps(0)
            with act.Fori(1, B) as n:
                mixer_exps(n)

            def xt_copy(n):
                act.wait_ge(s["xt_tr"], n + 1)
                if not (isinstance(n, int) and n == 0):
                    act.wait_ge(s["v_mm"], 3 * n)
                a.copy(xlnT[:, :, :], bank[2][:, :].rearrange("p (c w) -> p c w", c=2)[:, :, 0:S]) \
                    .then_inc(s["xt_copied"], 1)

            def first_parts(n, c):
                act.wait_ge(s["qk_mm"], 4 * n + c + 1)
                if not (isinstance(n, int) and n == 0) and c == 0:
                    act.wait_ge(s["parts_stored"], 96 * n)
                a.copy(parts[:, 0, c, :], PB[c % 2][:, 0:S]).then_inc(s["part1"], 1)

            def second_parts(n, c):
                act.wait_ge(s["rest_ready"], 4 * n + c + 1)
                a.copy(parts[:, 1, c, :], rest[:, c, :]).then_inc(s["part2"], 1)

            def v_copy(n, par, t):
                r = TILES[t][1]
                act.wait_ge(s["v_mm"], 3 * n + t + 1)
                if not (isinstance(n, int) and n < 2) and t == 0:
                    act.wait_ge(s["pv_mm"], 4 * (n - 1))
                a.copy(V[par][0:r, t, :, 0:HD], PB[t % 2][0:r, 0:MODEL].rearrange("p (h w) -> p h w", h=HEADS)) \
                    .then_inc(s["v_copied"], 1)

            def chunks(n):
                for c in range(4):
                    first_parts(n, c)
                    second_parts(n, c)

            def mt_copy(n):
                act.wait_ge(s["mt_tr"], n + 1)
                if not (isinstance(n, int) and n == 0):
                    act.wait_ge(s["m_stored"], 16 * n)
                a.copy(mT[:, :], OB[0:2 * HEADS, :].bitcast(bf16)[:, 0:S]).then_inc(s["mt_copied"], 1)

            def exps(n):
                first = isinstance(n, int) and n == 0
                for k in range(8):
                    if not (first and k < 4):
                        act.wait_ge(s["pv_mm"], 4 * n + k // 2 - 1)
                    for kt, (_, rows) in enumerate(TILES):
                        act.wait_ge(s["st_mm"], 16 * n + 2 * k + (1 if kt == 0 else 2))
                        off = 0 if kt < 2 else QW[1]
                        src = half[min(kt, 1)][0:rows, :].rearrange("p (h w) -> p h w", h=2)[:, :, off:off + QW[kt]]
                        a.activation(probs[0:rows, k % 4, :, QOFF[kt]:QOFF[kt] + QW[kt]], src, ACT.Exp,
                                     scale=HD ** -0.5).then_inc(s["exp_done"], 1)

            def att_step(n, par):
                xt_copy(n + 1)
                chunks(n + 1)
                mt_copy(n)
                for t in range(3):
                    v_copy(n + 1, 1 - par, t)
                exps(n)

            xt_copy(0)
            chunks(0)
            act.wait_ge(s["stack_ones"], 6)
            for t in range(3):
                v_copy(0, 0, t)
            act.wait_ge(s["ffw_cast"], 2)
            att_step(0, 0)
            with act.Fori(0, (B - 2) // 2) as i:
                att_step(2 * i + 1, 1)
                att_step(2 * i + 2, 0)
            mt_copy(B - 1)
            exps(B - 1)

            def fx_high(n):
                act.wait_ge(s["fxt_tr"], n + 1)
                if not (isinstance(n, int) and n == 0):
                    act.wait_ge(s["gu_mm"], HC * n)
                a.copy(xfh[:, :, :], bank[2][:, :].rearrange("p (c w) -> p c w", c=2)[:, :, 0:S]) \
                    .then_inc(s["fx_hi"], 1)

            def gate_tanh(n, c):
                act.wait_ge(s["gu_mm"], HC * n + c + 1)
                if not (isinstance(n, int) and n == 0 and c < 2):
                    act.wait_ge(s["a_ready"], HC * n + c - 1)
                a.activation(tg[:, c % 2, :], half[c % 2][:, 0:S], ACT.Tanh, scale=0.5 / 127.0) \
                    .then_inc(s["tanh_done"], 1)

            def h_high(n, c):
                act.wait_ge(s["h_ready"], HC * n + c + 1)
                if not (isinstance(n, int) and n == 0) and c == 0:
                    act.wait_ge(s["down_mm"], 3 * n)
                a.copy(hTh[:, c, :], hh[:, c % 2, :]).then_inc(s["h_hi"], 1)

            def gates(n):
                gate_tanh(n, 0)
                for c in range(HC):
                    if c + 1 < HC:
                        gate_tanh(n, c + 1)
                    h_high(n, c)

            for n in range(1):
                fx_high(n)
                gates(n)
            with act.Fori(1, B) as n:
                fx_high(n)
                gates(n)

        @block.vector
        def _(dve):
            v = nc.vector
            v.memset(resid[:, :, 2, :], 0.0).then_inc(s["text_dve"], 1)
            v.memset(xcT[0:F, :, 0:2], 0.0).then_inc(s["text_dve"], 1)
            v.memset(xcT[F:F + 1, :, :], 1.0).then_inc(s["text_dve"], 1)
            dve.wait_ge(s["loaded_wb"], 32)
            v.tensor_tensor(wbm[:, :, :], wb_sb[:, :, :], mask_sb[:, :, :], ALU.mult).then_inc(s["mix_consts"], 1)
            dve.wait_ge(s["gathered"], 16 * B)
            dve.wait_ge(s["text_dve"], 3)
            xe = resid[0:T, :, 2, 0:F]
            x1 = resid[0:T, :, 2, 2 * F:3 * F]
            v.scalar_tensor_tensor(out=xe, in0=emb_sb[:, :, :], scalar=float(F) ** 0.5,
                                   in1=pos_sb[:, :].unsqueeze(1).to_broadcast([T, B, F]),
                                   op0=ALU.mult, op1=ALU.add).then_inc(s["text_dve"], 1)
            dve.wait_ge(s["text_tr"], 1)
            v.tensor_copy(xcT[0:F, :, 2:T + 2].rearrange("f (a b) t -> f a b t", a=2),
                          half[0][0:F, :].rearrange("p (a w) -> p a w", a=2)[:, :, 0:4 * T]
                          .rearrange("p a (b t) -> p a b t", b=4)).then_inc(s["text_dve"], 1)
            dve.wait_ge(s["text_mm"], 1)
            v.tensor_copy(x1, PB[0][0:T, :].rearrange("p (n f) -> p n f", n=B)).then_inc(s["text_dve"], 1)
            dve.wait_ge(s["text_dve"], 6)
            for k, src in enumerate((xe, x1)):
                v.tensor_reduce(smx[:, k, :], src, axis=AX.X, op=ALU.max).then_inc(s["text_dve"], 1)
            dve.wait_ge(s["text_dve"], 8)
            for k, src in enumerate((xe, x1)):
                v.tensor_tensor(selx[:, k, :, :], src, smx[:, k, :].unsqueeze(2).to_broadcast([T, B, F]),
                                ALU.subtract).then_inc(s["text_dve"], 1)
            dve.wait_ge(s["text_act"], 1)
            v.tensor_reduce(ssum[:, :, :], selx[:, :, :, :], axis=AX.X, op=ALU.add).then_inc(s["text_dve"], 1)
            dve.wait_ge(s["text_dve"], 11)
            v.reciprocal(srec[:, :, :], ssum[:, :, :]).then_inc(s["text_dve"], 1)
            dve.wait_ge(s["text_dve"], 12)
            v.tensor_tensor(selx[:, :, :, :], selx[:, :, :, :],
                            srec[:, :, :].unsqueeze(3).to_broadcast([T, 2, B, F]), ALU.mult) \
                .then_inc(s["text_dve"], 1)
            for k in range(2):
                dve.wait_ge(s["text_tr"], 2 + k)
                v.tensor_copy(selT[:, k, :, :].rearrange("f (a b) t -> f a b t", a=2),
                              half[k][0:F, :].rearrange("p (a w) -> p a w", a=2)[:, :, 0:4 * T]
                              .rearrange("p a (b t) -> p a b t", b=4)).then_inc(s["text_dve"], 1)
            for k in range(2):
                dve.wait_ge(s["text_mm"], 2 + k)
                v.tensor_copy(resid[0:T, :, 2, (2 * k + 1) * F:(2 * k + 2) * F],
                              PB[k][0:T, :].rearrange("p (n f) -> p n f", n=B)).then_inc(s["text_dve"], 1)
            dve.wait_ge(s["loaded_ffw"], 32)
            v.tensor_copy(wgu_sb[:, :, :, :], stage_gu).then_inc(s["ffw_cast"], 1)
            v.tensor_copy(wd_sb[:, :, :], stage_d).then_inc(s["ffw_cast"], 1)

            dve.wait_ge(s["ew_ready"], 4)

            def mix_kv(n):
                for t in range(2):
                    dve.wait_ge(s["ek_ready"], 2 * n + t + 1)
                    kv = half[0][:, 512 * t:512 * t + 512].rearrange("p (h w) -> p h w", h=2)
                    v.tensor_tensor(ekv[:, t, 0, :].rearrange("p (h w) -> p h w", h=2),
                                    ekv[:, t, 1, :].rearrange("p (h w) -> p h w", h=2), kv[:, :, P:2 * P],
                                    ALU.mult).then_inc(s["ekv_ready"], 1)

            def mix_gate(n):
                dve.wait_ge(s["tq_ready"], n + 1)
                v.tensor_scalar(sg[:, :, :], tq[:, :, :], 1.0, None, ALU.add).then_inc(s["sg_ready"], 1)

            def mix_average(n):
                num = half[1][:, 0:512].rearrange("p (c l) -> p c l", c=CH)
                den = half[1][:, 512:1024].rearrange("p (c l) -> p c l", c=CH)
                dve.wait_ge(s["nd_mm"], n + 1)
                v.tensor_scalar(rden[:, :, :], den, ebk2[:, 0:1], None, ALU.mult).then_inc(s["mix_dve"], 1)
                dve.wait_ge(s["mix_dve"], MIX_DVE * n + 1)
                v.reciprocal(rden[:, :, :], rden[:, :, :]).then_inc(s["mix_dve"], 1)
                dve.wait_ge(s["mix_dve"], MIX_DVE * n + 2)
                v.scalar_tensor_tensor(out=yr[:, :, :], in0=rden[:, :, :], scalar=ebk[:, 0:1], in1=num,
                                       op0=ALU.mult, op1=ALU.mult).then_inc(s["mix_dve"], 1)
                dve.wait_ge(s["mix_dve"], MIX_DVE * n + 3)
                dve.wait_ge(s["sg_ready"], n + 1)
                v.scalar_tensor_tensor(out=yT[:, :, :], in0=yr[:, :, :], scalar=bvh[:, 0:1], in1=sg[:, :, :],
                                       op0=ALU.add, op1=ALU.mult).then_inc(s["mix_dve"], 1)

            def mix_norm(n):
                dve.wait_ge(s["mixout_mm"], n + 1)
                dve.wait_ge(s["xfb_ready"], n + 1)
                v.tensor_tensor(hpre[:, :, :], OB.rearrange("p (t m) -> p t m", t=2), xfb[:, :, :], ALU.add) \
                    .then_inc(s["mix_dve"], 1)
                dve.wait_ge(s["mix_dve"], MIX_DVE * n + 5)
                for t in range(2):
                    v.bn_stats(st_m[:, t, :], hpre[:, t, :]).then_inc(s["mix_dve"], 1)
                dve.wait_ge(s["mix_dve"], MIX_DVE * n + 7)
                dve.sem_inc(s["held_dve"], 1)
                for t in range(2):
                    v.bn_aggr(mv_m[:, t, :], st_m[:, t, :]).then_inc(s["mix_dve"], 1)
                dve.wait_ge(s["mix_dve"], MIX_DVE * n + 9)
                v.tensor_scalar(ve_m[:, :], mv_m[:, :, 1], EPS, None, ALU.add).then_inc(s["mix_dve"], 1)
                dve.wait_ge(s["mix_rstd"], n + 1)
                if not (isinstance(n, int) and n == 0):
                    dve.wait_ge(s["hg_ready"], n)
                for t in range(2):
                    v.tensor_scalar(hn[:, t, :], hpre[:, t, :], mv_m[:, t, 0:1], rs_m[:, t:t + 1],
                                    ALU.subtract, ALU.mult).then_inc(s["mix_dve"], 1)

            dve.wait_ge(s["loaded_mixw"], 96)
            v.tensor_scalar(bvh[:, :], bv_sb[:, :], 0.5, None, ALU.mult).then_inc(s["mix_consts"], 1)
            v.memset(mx[:, :, :], 0.0).then_inc(s["mix_consts"], 1)
            v.memset(MB[:, S:32 * SB], 1.0).then_inc(s["mix_consts"], 1)
            dve.wait_ge(s["mix_consts"], 4)
            mix_kv(0)
            mix_gate(0)
            with dve.Fori(0, B - 1) as n:
                mix_average(n)
                mix_kv(n + 1)
                mix_norm(n)
                mix_gate(n + 1)
            mix_average(B - 1)
            mix_norm(B - 1)

            def layer_norm(n, name, stats, mv, ve, rs, rstd):
                base = LN_STEPS * n
                for t in range(3):
                    v.bn_stats(stats[:, t, :], resid[:, bass.ds(n, 1), t, :].rearrange("p a m -> p (a m)")) \
                        .then_inc(s[name], 1)
                dve.wait_ge(s[name], base + 3)
                dve.sem_inc(s["held_dve"], 1)
                for t in range(3):
                    v.bn_aggr(mv[:, t, :], stats[:, t, :]).then_inc(s[name], 1)
                dve.wait_ge(s[name], base + 6)
                v.tensor_scalar(ve[:, :], mv[:, :, 1], EPS, None, ALU.add).then_inc(s[name], 1)
                dve.wait_ge(s[rstd], n + 1)
                for t in range(3):
                    v.tensor_scalar(xln[:, t, :], resid[:, bass.ds(n, 1), t, :].rearrange("p a m -> p (a m)"),
                                    mv[:, t, 0:1], rs[:, t:t + 1], ALU.subtract, ALU.mult).then_inc(s[name], 1)

            def att_norm(n):
                dve.wait_ge(s["resid_ready"], n + 1)
                if not (isinstance(n, int) and n == 0):
                    dve.wait_ge(s["xt_tr"], n)
                layer_norm(n, "att_ln", st_a, mv_a, ve_a, rs_a, "att_rstd")

            def take_rest(n, c):
                dve.wait_ge(s["part1"], 4 * n + c + 1)
                if not (isinstance(n, int) and n == 0):
                    dve.wait_ge(s["part3"], 4 * n + c - 3)
                v.tensor_tensor(rest[:, c, :], PB[c % 2][:, 0:S], parts[:, 0, c, :], ALU.subtract) \
                    .then_inc(s["rest_ready"], 1)

            def row_max(n, u):
                t, h0, nh, per = SM[u]
                rows = TILES[t][1]
                dve.wait_ge(s["row_max_mm"], len(SM) * n + u + 1)
                src = half[u % 2][0:rows, :].rearrange("p (h w) -> p h w", h=nh)[:, :, 0:KEND[t]]
                v.tensor_reduce(mx[0:rows, t, h0:h0 + nh], src, axis=AX.X, op=ALU.max).then_inc(s["row_max"], 1)

            def split_max(n):
                dve.wait_ge(s["row_max"], len(SM) * (n + 1))
                if not (isinstance(n, int) and n == 0):
                    dve.wait_ge(s["mt_tr"], n)
                v.tensor_scalar(mhl[:, :, 0, :], mx[:, :, :], -1.0, None, ALU.mult).then_inc(s["maxima_ready"], 1)
                dve.wait_ge(s["maxima_ready"], 2 * n + 1)
                v.scalar_tensor_tensor(out=mhl[:, :, 1, :], in0=mx[:, :, :], scalar=-1.0, in1=mhl[:, :, 0, :],
                                       op0=ALU.mult, op1=ALU.subtract).then_inc(s["maxima_ready"], 1)

            def add_attention(n):
                for t, (_, rows) in enumerate(TILES):
                    dve.wait_ge(s["oproj_mm"], 3 * n + (2 if t < 2 else 3))
                    src = (MB[:, 0:MODEL], MB[:, MODEL:2 * MODEL], OB[:, 0:MODEL])[t]
                    r = resid[0:rows, bass.ds(n, 1), t, :].rearrange("p a m -> p (a m)")
                    v.tensor_tensor(r, r, src[0:rows, :], ALU.add).then_inc(s["attn_added"], 1)

            def normalise(n, g):
                ob = (OB, MB)[g % 2]
                dve.wait_ge(s["pv_mm"], 4 * n + g + 1)
                v.transpose(denT[:, :], ob[:, 0:32 * SB]).then_inc(s["norm_steps"], 1)
                dve.wait_ge(s["norm_steps"], 12 * n + 3 * g + 1)
                v.reciprocal(denr[:, :], denT[:, :].rearrange("p (b c) -> p b c", c=32)[:, :, HD]) \
                    .then_inc(s["norm_steps"], 1)
                dve.wait_ge(s["norm_steps"], 12 * n + 3 * g + 2)
                v.transpose(scale[:, :], denr[:, :].unsqueeze(2).to_broadcast([P, SB, 32])) \
                    .then_inc(s["norm_steps"], 1)
                dve.wait_ge(s["norm_steps"], 12 * n + 3 * g + 3)
                if not (isinstance(n, int) and n == 0) and g == 0:
                    dve.wait_ge(s["oproj_mm"], 3 * n)
                v.tensor_tensor(OT[:, g, :], scale[:, 0:S], ob[:, 0:S], ALU.mult).then_inc(s["normed"], 1)

            def att_step(n):
                last = isinstance(n, int) and n == B - 1
                row_max(n, 0)
                row_max(n, 1)
                if not last:
                    att_norm(n + 1)
                for u in range(2, len(SM)):
                    row_max(n, u)
                    if not last and u in (6, 8, 10, 12):
                        take_rest(n + 1, (u - 6) // 2)
                split_max(n)
                if not (isinstance(n, int) and n == 0):
                    add_attention(n - 1)
                for g in range(4):
                    normalise(n, g)

            dve.wait_ge(s["text_dve"], 17)
            att_norm(0)
            for c in range(4):
                take_rest(0, c)
            att_step(0)
            with dve.Fori(1, B - 1) as n:
                att_step(n)
            att_step(B - 1)
            add_attention(B - 1)

            def ffn_norm(n):
                if isinstance(n, int) and n == 0:
                    dve.wait_ge(s["attn_added"], 3 * B)
                    dve.wait_ge(s["xt_tr"], B)
                else:
                    dve.wait_ge(s["fxt_tr"], n)
                layer_norm(n, "ffn_ln", st_f, mv_f, ve_f, rs_f, "ffn_rstd")
                dve.wait_ge(s["fx_hi"], n + 1)
                if not (isinstance(n, int) and n == 0):
                    dve.wait_ge(s["gu_mm"], HC * n)
                v.tensor_tensor(xfl[:, :, :], bank[2][:, :].rearrange("p (c w) -> p c w", c=2)[:, :, 0:S],
                                xfh[:, :, :], ALU.subtract).then_inc(s["fx_lo"], 1)

            def hidden(n, c):
                g_ps, u_ps = half[c % 2][:, 0:S], half[c % 2][:, 512:512 + S]
                dve.wait_ge(s["tanh_done"], HC * n + c + 1)
                v.scalar_tensor_tensor(out=ag[:, c % 2, :], in0=tg[:, c % 2, :], scalar=1.0, in1=g_ps,
                                       op0=ALU.add, op1=ALU.mult).then_inc(s["a_ready"], 1)
                dve.wait_ge(s["a_ready"], HC * n + c + 1)
                if not (isinstance(n, int) and n == 0 and c < 2):
                    dve.wait_ge(s["h_lo"], HC * n + c - 1)
                v.scalar_tensor_tensor(out=hh[:, c % 2, :], in0=ag[:, c % 2, :], scalar=HSCALE / (2 * 127.0 ** 2),
                                       in1=u_ps, op0=ALU.mult, op1=ALU.mult).then_inc(s["h_ready"], 1)

            def finish(n):
                if not (isinstance(n, int) and n == 0):
                    dve.wait_ge(s["out_stored"], 32 * n)
                for t, (_, rows) in enumerate(TILES):
                    dve.wait_ge(s["down_mm"], 3 * n + (2 if t < 2 else 3))
                    src = (OB[:, 0:MODEL], OB[:, MODEL:2 * MODEL], MB[:, 0:MODEL])[t]
                    v.scalar_tensor_tensor(out=ost[0:rows, t, :], in0=src[0:rows, :], scalar=1.0 / (127.0 * HSCALE),
                                           in1=resid[0:rows, bass.ds(n, 1), t, :].rearrange("p a m -> p (a m)"),
                                           op0=ALU.mult, op1=ALU.add).then_inc(s["final_ready"], 1)

            ffn_norm(0)
            for c in range(HC):
                hidden(0, c)
            with dve.Fori(1, B) as n:
                ffn_norm(n)
                hidden(n, 0)
                finish(n - 1)
                for c in range(1, HC):
                    hidden(n, c)
            finish(B - 1)

        @block.tensor
        def _(pe):
            mm, tr = nc.tensor.matmul, nc.tensor.transpose
            pe.wait_ge(s["consts_ready"], 7)
            pe.wait_ge(s["text_dve"], 4)
            xe = resid[0:T, :, 2, 0:F]
            for n in range(B):
                o = 512 * (n // 4) + T * (n % 4)
                last = tr(half[0][0:F, o:o + T], xe[:, n, :], ident[0:T, 0:T])
            last.then_inc(s["text_tr"], 1)
            pe.wait_ge(s["text_dve"], 5)
            for n in range(B):
                for tap in range(3):
                    last = mm(PB[0][0:T, n * F:(n + 1) * F], xcT[:, n, tap:tap + T], conv_sb[:, tap, :],
                              start=(tap == 0), stop=(tap == 2))
            last.then_inc(s["text_mm"], 1)
            pe.wait_ge(s["text_dve"], 13)
            for k in range(2):
                for n in range(B):
                    o = 512 * (n // 4) + T * (n % 4)
                    last = tr(half[k][0:F, o:o + T], selx[:, k, n, :], ident[0:T, 0:T])
                last.then_inc(s["text_tr"], 1)
            for k in range(2):
                pe.wait_ge(s["text_dve"], 14 + k)
                for n in range(B):
                    last = mm(PB[k][0:T, n * F:(n + 1) * F], selT[:, k, n, :], spos_sb[:, k, :], start=True, stop=True)
                last.then_inc(s["text_mm"], 1)

            def key_value(n):
                pe.wait_ge(s["x_loaded"], 16 * (n + 1))
                for t in range(2):
                    if not (isinstance(n, int) and n == 0):
                        pe.wait_ge(s["ekv_ready"], 2 * n)
                    for h in range(2):
                        last = mm(half[0][:, 512 * t + 256 * h:512 * t + 256 * h + 256],
                                  xs[:, h, P * t:P * t + P], wkv_sb[:, :], start=True, stop=True)
                    last.then_inc(s["kv_mm"], 1)
                if not (isinstance(n, int) and n == 0):
                    pe.wait_ge(s["tq_ready"], n)
                for h in range(2):
                    last = mm(PB[0][:, L * h:L * h + L], wq_sb[:, :], xs[:, h, :], start=True, stop=True)
                last.then_inc(s["q_mm"], 1)

            def averages(n):
                pe.wait_ge(s["ekv_ready"], 2 * n + 2)
                for c in range(CH):
                    for nd in range(2):
                        for t in range(2):
                            last = mm(half[1][:, 512 * nd + L * c:512 * nd + L * c + L],
                                      ekv[:, t, nd, P * c:P * c + P], ew[:, t, :], start=(t == 0), stop=(t == 1))
                last.then_inc(s["nd_mm"], 1)

            def mix_project(n):
                pe.wait_ge(s["mix_dve"], MIX_DVE * n + 4)
                for t in range(2):
                    for c in range(CH):
                        last = mm(OB[:, MODEL * t:MODEL * t + MODEL], yT[:, c, P * t:P * t + P], outw_sb[:, c, :],
                                  start=(c == 0), stop=(c == CH - 1))
                last.then_inc(s["mixout_mm"], 1)

            pe.wait_ge(s["loaded_mixw"], 96)
            pe.wait_ge(s["text_dve"], 17)
            key_value(0)
            pe.wait_ge(s["ew_ready"], 1)
            with pe.Fori(0, B - 1) as n:
                averages(n)
                key_value(n + 1)
                mix_project(n)
            averages(B - 1)
            mix_project(B - 1)

            def transpose_tokens(name):
                for t, (t0, rows) in enumerate(TILES):
                    for c in range(CH):
                        last = tr(PB[c][:, t0:t0 + rows], xln[0:rows, t, P * c:P * c + P], ident[0:rows, 0:rows])
                last.then_inc(s[name], 1)

            def att_transpose(n):
                pe.wait_ge(s["att_ln"], LN_STEPS * (n + 1))
                if not (isinstance(n, int) and n == 0):
                    pe.wait_ge(s["v_copied"], 3 * n)
                transpose_tokens("xt_tr")

            def query_key(n, c):
                if c < 2:
                    pe.wait_ge(s["xt_copied"], n + 1)
                else:
                    pe.wait_ge(s["rest_ready"], 4 * n + c - 1)
                for kc in range(CH):
                    last = mm(PB[c % 2][:, 0:S], wqkv_sb[:, c // 2, kc, P * (c % 2):P * (c % 2) + P], xlnT[:, kc, :],
                              start=(kc == 0), stop=(kc == CH - 1))
                last.then_inc(s["qk_mm"], 1)

            def values(n, t):
                if t < 2:
                    pe.wait_ge(s["rest_ready"], 4 * n + 3 + t)
                else:
                    pe.wait_ge(s["v_copied"], 3 * n + 1)
                t0, rows = TILES[t]
                for kc in range(CH):
                    last = mm(PB[t % 2][0:rows, 0:MODEL], xlnT[:, kc, t0:t0 + rows], wqkv_sb[:, 2, kc, :],
                              start=(kc == 0), stop=(kc == CH - 1))
                last.then_inc(s["v_mm"], 1)

            def scores_for_max(n, par, u):
                t, h0, nh, per = SM[u]
                t0, rows = TILES[t]
                if u >= 2:
                    pe.wait_ge(s["row_max"], len(SM) * n + u - 1)
                elif not (isinstance(n, int) and n == 0):
                    pe.wait_ge(s["exp_done"], 24 * n - (2 if u == 0 else 0))
                for i in range(nh):
                    h = h0 + i
                    o = 512 * (i // per) + KEND[t] * (i % per)
                    mm(half[u % 2][0:rows, o:o + KEND[t]], QS[par][0:STK, h, t0:t0 + rows], KS[par][0:STK, h, 0:KEND[t]],
                       start=True, stop=False)
                    last = mm(half[u % 2][0:rows, o + t0:o + t0 + rows], identb[:, 0:rows], causal[:, 0:rows],
                              start=False, stop=True)
                last.then_inc(s["row_max_mm"], 1)

            def transpose_max(n):
                pe.wait_ge(s["maxima_ready"], 2 * n + 2)
                for t, (t0, rows) in enumerate(TILES):
                    last = tr(OB[0:2 * HEADS, :].bitcast(bf16)[:, t0:t0 + rows],
                              mhl[0:rows, t, :, :].rearrange("p a h -> p (a h)"), identb[0:rows, 0:rows])
                last.then_inc(s["mt_tr"], 1)

            def scores_transposed(n, par, k):
                for kt, (t0, rows) in enumerate(TILES):
                    if kt < 2:
                        if k == 0:
                            pe.wait_ge(s["row_max"], len(SM) * n + 13 + kt)
                        else:
                            pe.wait_ge(s["exp_done"], 24 * n + 3 * (k - 1) + (1 if kt == 0 else 3))
                    off = 0 if kt < 2 else QW[1]
                    for i in range(2):
                        o = 512 * i + off
                        last = mm(half[min(kt, 1)][0:rows, o:o + QW[kt]], KS[par][0:STK + 2, 2 * k + i, t0:t0 + rows],
                                  QS[par][0:STK + 2, 2 * k + i, t0:S], start=True, stop=True)
                    if kt != 1:
                        last.then_inc(s["st_mm"], 1)

            def weighted_values(n, par, g):
                pe.wait_ge(s["selected"], 24 * n + 6 * (g + 1))
                if g >= 2:
                    pe.wait_ge(s["normed"], 4 * n + g - 1)
                elif not (isinstance(n, int) and n == 0):
                    pe.wait_ge(s["attn_added"], 3 * n)
                for kt, (t0, rows) in enumerate(TILES):
                    for j in range(4):
                        h = 4 * g + j
                        last = mm((OB, MB)[g % 2][32 * j:32 * j + 32, t0:S], V[par][0:rows, kt, h, :],
                                  probs[0:rows, (h // 2) % 4, h % 2, QOFF[kt]:QOFF[kt] + QW[kt]],
                                  start=(kt == 0), stop=(kt == 2))
                last.then_inc(s["pv_mm"], 1)

            def out_project(n, t):
                t0, rows = TILES[t]
                pe.wait_ge(s["normed"], 4 * n + 4)
                dst = (MB[:, 0:MODEL], MB[:, MODEL:2 * MODEL], OB[:, 0:MODEL])[t]
                if t == 2 and not (isinstance(n, int) and n == B - 1):
                    pe.wait_ge(s["mt_copied"], n + 2)
                for g in range(4):
                    last = mm(dst[0:rows, :], OT[:, g, t0:t0 + rows], wo_sb[:, g, :], start=(g == 0), stop=(g == 3))
                last.then_inc(s["oproj_mm"], 1)

            def att_step(n, par, turns):
                last = isinstance(n, int) and n == B - 1
                first = isinstance(n, int) and n == 0
                pe.wait_ge(s[f"stacked{par}"], 192 * turns)
                for u in range(len(SM)):
                    scores_for_max(n, par, u)
                    if not last:
                        if u == 3:
                            att_transpose(n + 1)
                        if u in (5, 7, 9, 11):
                            query_key(n + 1, (u - 5) // 2)
                if not first:
                    out_project(n - 1, 0)
                    out_project(n - 1, 1)
                transpose_max(n)
                if not first:
                    out_project(n - 1, 2)
                if not last:
                    for t in range(3):
                        values(n + 1, t)
                pe.wait_ge(s["m_loaded"], 16 * (n + 1))
                for k in range(8):
                    scores_transposed(n, par, k)
                    if k in (2, 4, 6):
                        weighted_values(n, par, k // 2 - 1)
                weighted_values(n, par, 3)

            pe.wait_ge(s["loaded_attw"], 32)
            pe.wait_ge(s["mix_dve"], MIX_DVE * (B - 1) + 5)
            pe.wait_ge(s["tq_ready"], B)
            att_transpose(0)
            for c in range(4):
                query_key(0, c)
            for t in range(3):
                values(0, t)
            pe.wait_ge(s["stack_ones"], 6)
            att_step(0, 0, 1)
            with pe.Fori(0, (B - 2) // 2) as i:
                att_step(2 * i + 1, 1, i + 1)
                att_step(2 * i + 2, 0, i + 2)
            att_step(B - 1, 1, B // 2)
            for t in range(3):
                out_project(B - 1, t)

            def ffn_transpose(n):
                pe.wait_ge(s["ffn_ln"], LN_STEPS * (n + 1))
                if not (isinstance(n, int) and n == 0):
                    pe.wait_ge(s["fx_lo"], n)
                transpose_tokens("fxt_tr")

            def gate_up(n, c):
                pe.wait_ge(s["fx_lo"], n + 1)
                if not (isinstance(n, int) and n == 0 and c < 2):
                    pe.wait_ge(s["h_ready"], HC * n + c - 1)
                for gu in range(2):
                    for kc in range(CH):
                        for x in (xfh, xfl):
                            last = mm(half[c % 2][:, 512 * gu:512 * gu + S], wgu_sb[:, gu, kc, P * c:P * c + P],
                                      x[:, kc, :], start=(kc == 0 and x is xfh), stop=(kc == CH - 1 and x is xfl))
                last.then_inc(s["gu_mm"], 1)

            def down(n):
                pe.wait_ge(s["h_hi"], HC * (n + 1))
                pe.wait_ge(s["h_lo"], HC * (n + 1))
                if not (isinstance(n, int) and n == 0):
                    pe.wait_ge(s["final_ready"], 3 * n)
                for t, (t0, rows) in enumerate(TILES):
                    dst = (OB[:, 0:MODEL], OB[:, MODEL:2 * MODEL], MB[:, 0:MODEL])[t]
                    for c in range(HC):
                        for x in (hTh, hTl):
                            last = mm(dst[0:rows, :], x[:, c, t0:t0 + rows], wd_sb[:, c, :],
                                      start=(c == 0 and x is hTh), stop=(c == HC - 1 and x is hTl))
                    last.then_inc(s["down_mm"], 1)

            pe.wait_ge(s["attn_added"], 3 * B)
            pe.wait_ge(s["v_copied"], 3 * B)
            pe.wait_ge(s["exp_done"], 24 * B)
            pe.wait_ge(s["ffw_cast"], 2)
            ffn_transpose(0)
            for c in range(HC):
                gate_up(0, c)
            with pe.Fori(1, B) as n:
                ffn_transpose(n)
                gate_up(n, 0)
                down(n - 1)
                for c in range(1, HC):
                    gate_up(n, c)
            down(B - 1)


def kernel(**inputs):
    import numpy as np
    import concourse.bacc as bacc
    from concourse import mybir as mb
    from concourse.bass_utils import run_bass_kernel_spmd

    x = {k: np.asarray(v) for k, v in inputs.items()}
    z = np.zeros((F, F), np.float32)

    def halves(w):
        return w.T.reshape(-1, P, w.shape[0]).transpose(1, 0, 2)

    def two_heads(*ws):
        top = [m for w in ws for m in (w.T, z)]
        low = [m for w in ws for m in (z, w.T)]
        return np.concatenate([np.concatenate(top, 1), np.concatenate(low, 1)], 0)

    def column(b):
        return np.concatenate([b, b]).reshape(P, 1)

    depth = F // 2
    angle = np.arange(T, dtype=np.float32)[:, None] * \
        (np.float32(1.0) / np.float32(2500) ** (np.arange(depth, dtype=np.float32)[None, :] / np.float32(depth)))
    pos = np.concatenate([np.sin(angle), np.cos(angle)], -1).astype(np.float32)

    conv = np.concatenate([x["L0_txt_conv_w"].transpose(1, 0, 2), np.zeros((1, 3, F), np.float32)], 0)
    conv[F, 2, :] = x["L0_txt_conv_b"]
    wo = np.zeros((4, 32, 4, MODEL), np.float32)
    wo[:, :HD] = x["L0_attn_o_proj_weight"].T.reshape(4, 4, HD, MODEL).transpose(1, 2, 0, 3)
    xm = x["x"]
    arrays = dict(
        x_mix=xm.transpose(0, 3, 1, 2).reshape(B, 2, 2, F, L).transpose(0, 2, 3, 1, 4).reshape(B, P, 2, L),
        x_flat=xm.transpose(0, 2, 3, 1).reshape(B, 2, P, MODEL).transpose(0, 2, 1, 3),
        tokens=x["x_txt"].T, pos=pos,
        wkv=two_heads(x["L0_tok_Wk_w"], x["L0_tok_Wv_w"]), wq=two_heads(x["L0_tok_Wq_w"]),
        bq=column(x["L0_tok_Wq_b"]), bk=column(x["L0_tok_Wk_b"]), bv=column(x["L0_tok_Wv_b"]),
        wbt=halves(x["L0_tok_w_bias"]), maskt=halves(x["L0_tok_local_mask"]),
        outw=x["L0_tok_out_w"].reshape(CH, P, MODEL).transpose(1, 0, 2),
        rows3=np.broadcast_to(np.stack([x["L0_tok_out_b"], x["L0_tok_ln_g"], x["L0_tok_ln_b"]])[None],
                              (P, 3, MODEL)),
        emb=x["L0_txt_emb_table"], convw=conv,
        spos=np.stack([x["L0_txt_spos0"], x["L0_txt_spos1"]], 1),
        wqkv=np.stack([halves(x[f"L0_attn_{m}_proj_weight"]) for m in "qkv"], 1),
        wo=wo.reshape(P, 4, MODEL),
        wgu=np.stack([halves(x["L0_ffn_w_gate"]), halves(x["L0_ffn_w_up"])], 1),
        wd=halves(x["L0_ffn_w_down"]),
    )
    nc = bacc.Bacc("TRN2", target_bir_lowering=False, num_devices=1)
    sent, args = {}, []
    for name, a in arrays.items():
        a = np.ascontiguousarray(a)
        sent[f"in_{name}"] = a
        dt = mb.dt.uint8 if a.dtype == bool else mb.dt.from_np(a.dtype)
        args.append(nc.dram_tensor(f"in_{name}", a.shape, dt, kind="ExternalInput").ap())
    args.append(nc.dram_tensor("out", (B, S, MODEL), mb.dt.float32, kind="ExternalOutput").ap())
    build(nc, *args)
    r = run_bass_kernel_spmd(nc, [sent], core_ids=[0])
    return r.results[0]["out"]
```

```python
from contextlib import ExitStack

import numpy as np

import concourse.bass as bass
from concourse import mybir

B, F, L, H4, D = 8, 64, 256, 4, 64
MODEL = H4 * F
T = 77
S = L + T
HEADS, HD = 16, 16
HIDDEN = 768
P = 128
TILES = [(0, P), (P, P), (2 * P, T)]
KEND = [P, 2 * P, S]
QW = [S, S - P, T]
QOFF = [0, S, 2 * S - P]
PW = sum(QW)
CH = MODEL // P
HC = HIDDEN // P
SB = -(-S // 32)
EPS = 1e-5
PARTS_Q = [0, 1, 2, 0, 1, 0]
PARTS_K = [0, 0, 0, 1, 1, 2]
STK = HD * len(PARTS_Q)
MASKED = -1e30
LAST = B - 1
PAIRS = B // 2 - 1
REST_AFTER = [6, 7, 9, 11]
PE_ORDER = "s0 s1 g0 s2 w0 g1 s3 g2 s4 w1 s5 g3 s6 w2 g4 s7 g5 w3".split()
ACT_ORDER = "e0 e1 t0 e2 h0 t1 e3 h1 t2 e4 h2 e5 t3 e6 h3 t4 e7 h4 t5 h5".split()
DVE_ORDER = "h0 n0 h1 h2 n1 h3 n2 h4 h5 n3".split()
POOL_ORDER = "s0 s1 s2 h0 s3 h1 s4 h2 s5 s6 h3 p0 s7 h4 h5 p1".split()
HSCALE = 2.0 ** -4
ARENA = 13700
MIX_AVG, MIX_NORM = 4, 8
LN_STEPS = 10

SM = [(0, 8 * u, 8, 4) for u in range(2)] + [(1, 4 * u, 4, 2) for u in range(4)] + \
     [(2, 2 * u, 2, 1) for u in range(8)]


def build(nc, x_mix, x_flat, tokens, pos, wkv, wq, bq, ebk_in, bv_in, wbt, maskt, outw, rows3,
          emb, convw, spos, wqkv_t, wo_t, rmask, wgu, wd, out):
    f32, bf16, f16 = mybir.dt.float32, mybir.dt.bfloat16, mybir.dt.float16
    i32, u8 = mybir.dt.int32, mybir.dt.uint8
    ALU, ACT, AX = mybir.AluOpType, mybir.ActivationFunctionType, mybir.AxisListType

    ctx = ExitStack()
    with ctx:
        def sb(name, shape, dt=f32):
            return ctx.enter_context(nc.sbuf_tensor(name, shape, dt))

        def sem(name):
            return ctx.enter_context(nc.semaphore(name))

        resid = sb("resid", [P, B, 3, MODEL])
        ident = sb("ident", [P, P])
        identb = sb("identb", [P, P], bf16)
        causal = sb("causal", [P, P], bf16)
        tok_sb = sb("tok_sb", [T, B], i32)
        nhalf = sb("nhalf", [P, 3])
        arena = sb("arena", [P, ARENA])

        def carver():
            at = [0]

            def take(*dims, dt=f32, rows=P):
                words = int(np.prod(dims)) // (1 if dt == f32 else 2)
                part = arena[0:rows, at[0]:at[0] + words]
                at[0] += words
                assert at[0] <= ARENA
                part = part if dt == f32 else part.bitcast(dt)
                names = "abcd"[:len(dims)]
                return part.rearrange(f"p ({' '.join(names)}) -> p {' '.join(names)}", **dict(zip(names, dims)))
            return take

        early, late = carver(), carver()
        pos_sb = early(F, rows=T)
        emb_sb = early(B, F, rows=T)
        conv_sb = early(3, F, rows=F + 1)
        spos_sb = early(2, F)
        xcT = early(B, T + 2, rows=F + 1)
        selx = early(2, B, F, rows=T)
        smx = early(2, B, rows=T)
        ssum = early(2, B, rows=T)
        srec = early(2, B, rows=T)
        selT = early(2, B // 2, T)
        wkv_sb = early(4 * F)
        wq_sb = early(P)
        bq_sb, bqh, bk_sb, ebk, ebk2, bv_sb, bvh = (early(1) for _ in range(7))
        wb_sb = early(2, L)
        wbm = early(2, L)
        ew = early(2, L)
        outw_sb = early(CH, MODEL)
        rows_sb = early(3, MODEL)
        xs = early(2, L)
        xf = early(2, MODEL)
        xfb = early(2, MODEL)
        ekv = early(2, 2, MODEL)
        tq = early(CH, L)
        sg = early(CH, L)
        rden = early(CH, L)
        yr = early(CH, L)
        yT = early(CH, L)
        hpre = early(2, MODEL)
        hn = early(2, MODEL)
        hg = early(2, MODEL)
        st_m = early(2, 6)
        mv_m = early(2, 2)
        ve_m = early(2)
        rs_m = early(2)
        mask_sb = sb("mask_sb", [P, 2, L], u8)
        wqkv_sb = sb("wqkv_sb", [P, 3, CH, MODEL])
        wo_sb = sb("wo_sb", [P, 2, MODEL])
        st_a = sb("st_a", [P, 3, 6])
        mv_a = sb("mv_a", [P, 3, 2])
        ve_a = sb("ve_a", [P, 3])
        rs_a = sb("rs_a", [P, 3])
        xln = sb("xln", [P, 3, MODEL])
        xlnT = sb("xlnT", [P, CH, S])
        parts = sb("parts", [P, 3, 4, S], bf16)
        rest = sb("rest", [P, 4, S])
        qstack = [sb(f"qstack{p}", [P, HEADS * S], bf16) for p in range(2)]
        kstack = [sb(f"kstack{p}", [P, HEADS * S], bf16) for p in range(2)]
        QS, KS = ([x[:, :].rearrange("p (h t) -> p h t", h=HEADS) for x in xs2] for xs2 in (qstack, kstack))
        V = [sb(f"V{p}", [P, 3, HEADS, 32])[:, :, :, :] for p in range(2)]
        mx = sb("mx", [P, 3, HEADS])
        mhl = sb("mhl", [P, 3, 2, HEADS], bf16)
        mT = sb("mT", [2 * HEADS, S], bf16)
        probs = sb("probs", [P, 4, 2, PW])
        denT = sb("denT", [P, SB * 32])
        denr = sb("denr", [P, SB])
        scale = sb("scale", [P, SB * 32])
        oh = sb("oh", [P, 4, S])
        OT = sb("OT", [P, 2, S])
        row_mask = sb("row_mask", [P, 2])
        st_f = sb("st_f", [P, 3, 6])
        mv_f = sb("mv_f", [P, 3, 2])
        ve_f = sb("ve_f", [P, 3])
        rs_f = sb("rs_f", [P, 3])
        xlnf = late(3, MODEL)
        xfh = late(CH, S, dt=f16)
        xfl = late(CH, S, dt=f16)
        tg = late(S)
        ag = late(S)
        hh = late(2, S)
        hTh = late(HC, S, dt=f16)
        hTl = late(HC, S, dt=f16)
        ost = late(3, MODEL)
        wgu_sb = sb("wgu_sb", [P, 2, CH, HIDDEN], f16)
        wd_sb = sb("wd_sb", [P, HC, MODEL], f16)
        stage = probs[:, :, :, :].rearrange("p a b c -> p (a b c)")
        stage_gu = stage[:, 0:2 * CH * HIDDEN].bitcast(i32).rearrange("p (a c n) -> p a c n", a=2, c=CH)
        stage_d = stage[:, 2 * CH * HIDDEN:2 * CH * HIDDEN + HC * MODEL].bitcast(i32) \
            .rearrange("p (c n) -> p c n", c=HC)

        bank = [ctx.enter_context(nc.psum_tensor(f"bank{i}", [P, 1024], f32)) for i in range(4)]
        half = [bank[0], bank[1]]
        PB = [bank[2][:, 0:512], bank[2][:, 512:1024]]
        OB, MB = bank[3][:, 0:512], bank[3][:, 512:1024]

        qk_dram = [nc.dram_tensor(f"qk_parts{p}", [2, 3, MODEL, S], bf16).ap() for p in range(2)]
        m_dram = [nc.dram_tensor(f"max_rows{p}", [2 * HEADS, S], bf16).ap() for p in range(2)]

        names = """loaded_tok loaded_text loaded_mixw loaded_wb loaded_rows loaded_attw loaded_ffw consts_ready gathered
        text_dve text_tr text_act text_mm ffw_cast mix_consts ew_ready
        x_loaded xf_loaded xfb_ready kv_mm q_mm ek_ready tq_ready ekv_ready sg_ready nd_mm
        mixout_mm mix_avg mix_norm mix_rstd att_rstd ffn_rstd hg_ready resid_ready packed
        att_ln xt_tr xt_copied qk_mm part1 rest_ready part2 part3 v_mm v_copied stack_ones
        parts_stored stacked0 stacked1 row_max_mm row_max maxima_ready mt_tr mt_copied m_stored m_loaded
        st_mm exp_done selected pv_mm norm_steps normed oproj_mm attn_added
        ffn_ln fxt_tr fx_hi fx_lo gu_mm tanh_done a_ready h_ready h_hi h_lo down_mm final_ready
        out_stored held_pool held_dve held_sync""".split()
        s = {n: sem(n) for n in names}

        block = ctx.enter_context(nc.Block())
        def since(n, k):
            return not isinstance(n, int) or n >= k

        def before(n, k):
            return not isinstance(n, int) or n < k

        @block.sync
        def _(sp):
            def load(dst, src, name):
                sp.dma_start(dst, src).then_inc(s[name], 16)

            def load_x(n):
                load(xs[:, :, :], x_mix[bass.ds(n, 1)].rearrange("a p h l -> (a p) h l"), "x_loaded")

            def load_xf(n):
                load(xf[:, :, :], x_flat[bass.ds(n, 1)].rearrange("a p t m -> (a p) t m"), "xf_loaded")

            load(tok_sb[:, :], tokens, "loaded_tok")
            load_x(0)
            load(wkv_sb[:, :], wkv, "loaded_mixw")
            load(wq_sb[:, :], wq, "loaded_mixw")
            load(bq_sb[:, :], bq, "loaded_mixw")
            load(bk_sb[:, :], ebk_in, "loaded_mixw")
            load(bv_sb[:, :], bv_in, "loaded_mixw")
            load(wb_sb[:, :, :], wbt, "loaded_wb")
            load(mask_sb[:, :, :], maskt, "loaded_wb")
            load(outw_sb[:, :, :], outw, "loaded_mixw")
            load_xf(0)
            load(rows_sb[:, :, :], rows3, "loaded_rows")
            load(pos_sb[:, :], pos, "loaded_text")
            load(conv_sb[:, :, :], convw, "loaded_text")
            for b in range(2):
                load(spos_sb[F * b:F * b + F, :, :], spos, "loaded_text")
            load(stage_gu, wgu, "loaded_ffw")
            load(stage_d, wd, "loaded_ffw")
            load(wqkv_sb[:, :, :, :], wqkv_t, "loaded_attw")
            load(wo_sb[:, :, :], wo_t, "loaded_attw")
            load(row_mask[:, :], rmask, "loaded_attw")
            with sp.Fori(1, B) as n:
                sp.wait_ge(s["q_mm"], n)
                load_x(n)
                sp.wait_ge(s["xfb_ready"], n)
                load_xf(n)

            def store_parts(n, par):
                sp.wait_ge(s["part3"], 4 * n + 4)
                sp.wait_ge(s["part2"], 4 * n + 4)
                for qk in range(2):
                    for part in range(3):
                        sp.dma_start(qk_dram[par][qk, part].rearrange("(c p) t -> p c t", p=P),
                                     parts[:, part, 2 * qk:2 * qk + 2, :]).then_inc(s["parts_stored"], 16)

            def load_stacks(n, par, reused=True):
                sp.wait_ge(s["parts_stored"], 96 * (n + 1))
                sp.sem_inc(s["held_sync"], 1)
                if reused:
                    sp.wait_ge(s["st_mm"], 16 * (n - 1))
                for qk, (dst, order) in enumerate([(QS[par], PARTS_Q), (KS[par], PARTS_K)]):
                    for r, part in enumerate(order):
                        sp.dma_start(dst[HD * r:HD * r + HD, :, :],
                                     qk_dram[par][qk, part].rearrange("(h i) t -> i h t", i=HD)) \
                            .then_inc(s[f"stacked{par}"], 16)

            def max_rows(n, par):
                sp.wait_ge(s["mt_copied"], n + 1)
                sp.dma_start(m_dram[par], mT[:, :]).then_inc(s["m_stored"], 16)
                sp.wait_ge(s["m_stored"], 16 * (n + 1))
                sp.dma_start(QS[par][STK:STK + 2, :, :], m_dram[par].rearrange("(r h) t -> r h t", r=2)) \
                    .then_inc(s["m_loaded"], 16)

            def store_out(n):
                sp.wait_ge(s["final_ready"], 3 * n + 3)
                sp.sem_inc(s["held_sync"], 1)
                for dst, src in ((out[bass.ds(n, 1), 0:L, :].rearrange("a (t p) m -> p (a t) m", p=P),
                                  ost[:, 0:2, :]),
                                 (out[bass.ds(n, 1), L:S, :].rearrange("a p m -> (a p) m"), ost[0:T, 2, :])):
                    sp.dma_start(dst, src).then_inc(s["out_stored"], 16)

            def step(n, par):
                if before(n, LAST):
                    store_parts(n + 1, 1 - par)
                if since(n, 2):
                    store_out(n - 2)
                max_rows(n, par)
                if before(n, LAST):
                    load_stacks(n + 1, 1 - par, since(n, 1))

            store_parts(0, 0)
            load_stacks(0, 0, False)
            step(0, 0)
            step(1, 1)
            with sp.Fori(1, PAIRS) as i:
                step(2 * i, 0)
                step(2 * i + 1, 1)
            step(B - 2, 0)
            step(LAST, 1)
            store_out(B - 2)
            store_out(B - 1)
            sp.wait_ge(s["out_stored"], 32 * B)
            sp.wait_ge(s["m_loaded"], 16 * B)

        @block.gpsimd
        def _(pool):
            g = nc.gpsimd
            g.memset(ident[:, :], 0.0).then_inc(s["consts_ready"], 1)
            g.memset(identb[:, :], 0.0).then_inc(s["consts_ready"], 1)
            g.memset(causal[:, :], 0.0).then_inc(s["consts_ready"], 1)
            g.memset(nhalf[:, :], -0.5).then_inc(s["consts_ready"], 1)
            pool.wait_ge(s["consts_ready"], 4)
            for m in (ident, identb):
                g.affine_select(out=m[:, :], in_=m[:, :], compare_op=ALU.not_equal, fill=1.0, base=0,
                                pattern=[[-1, P]], channel_multiplier=1).then_inc(s["consts_ready"], 1)
            g.affine_select(out=causal[:, :], in_=causal[:, :], compare_op=ALU.is_ge, fill=MASKED, base=0,
                            pattern=[[-1, P]], channel_multiplier=1).then_inc(s["consts_ready"], 1)
            pool.wait_ge(s["loaded_tok"], 16)
            for n in range(B):
                g.indirect_dma_start(emb_sb[:, n, :], None, emb,
                                     bass.IndirectOffsetOnAxis(tok_sb[:, n:n + 1], 0)) \
                    .then_inc(s["gathered"], 16)
            for p in range(2):
                g.memset(V[p][:, :, :, :], 0.0).then_inc(s["stack_ones"], 1)
            for p in range(2):
                pool.wait_ge(s["stack_ones"], 2 + p)
                g.memset(KS[p][STK:P, :, :], 1.0).then_inc(s["stack_ones"], 1)
            pool.wait_ge(s["stack_ones"], 4)
            for p in range(2):
                for b in range(2):
                    g.memset(V[p].rearrange("p t (c b j) w -> p t c b j w", b=2, j=4)[:, :, :, b, :, HD * (1 - b)],
                             1.0).then_inc(s["stack_ones"], 1)

            pool.wait_ge(s["loaded_rows"], 16)
            bias_row, gain_row, shift_row = (rows_sb[:, r:r + 1, :].to_broadcast([P, 2, MODEL]) for r in range(3))

            def residual_in(n):
                pool.wait_ge(s["xf_loaded"], 16 * (n + 1))
                if since(n, 1):
                    pool.wait_ge(s["mix_norm"], MIX_NORM * (n - 1) + 1)
                g.tensor_tensor(xfb[:, :, :], xf[:, :, :], bias_row, ALU.add).then_inc(s["xfb_ready"], 1)

            def inverse_root(n, counted, count, dst, src, done):
                pool.wait_ge(s[counted], count)
                g.tensor_tensor(dst[:, :], src[:, :], nhalf[:, 0:src.shape[1]], ALU.pow).then_inc(s[done], 1)

            def gain(n):
                inverse_root(n, "mix_norm", MIX_NORM * n + 6, rs_m, ve_m, "mix_rstd")
                pool.wait_ge(s["mix_norm"], MIX_NORM * (n + 1))
                g.tensor_tensor(hg[:, :, :], hn[:, :, :], gain_row, ALU.mult).then_inc(s["hg_ready"], 1)
                pool.wait_ge(s["hg_ready"], n + 1)
                g.tensor_tensor(resid[:, bass.ds(n, 1), 0:2, :].rearrange("p a t m -> p (a t) m"), hg[:, :, :],
                                shift_row, ALU.add).then_inc(s["resid_ready"], 1)

            def att_inverse_root(n):
                inverse_root(n, "att_ln", LN_STEPS * n + 7, rs_a, ve_a, "att_rstd")

            def third_part(n, c):
                pool.wait_ge(s["part2"], 4 * n + c + 1)
                g.tensor_tensor(parts[:, 2, c, :], rest[:, c, :], parts[:, 1, c, :], ALU.subtract) \
                    .then_inc(s["part3"], 1)

            def keep_past(n, k):
                for kt, (_, rows) in enumerate(TILES):
                    pool.wait_ge(s["exp_done"], 24 * n + 3 * k + kt + 1)
                    pool.sem_inc(s["held_pool"], 1)
                    blk = probs[0:rows, k % 4, :, QOFF[kt]:QOFF[kt] + rows]
                    g.affine_select(out=blk, in_=blk, compare_op=ALU.is_ge, fill=0.0, base=0,
                                    pattern=[[0, 2], [1, rows]], channel_multiplier=-1) \
                        .then_inc(s["selected"], 1)

            def pack(n, c):
                pool.wait_ge(s["normed"], 4 * n + 2 * c + 2)
                if since(n, 1) and c == 0:
                    pool.wait_ge(s["oproj_mm"], 3 * n)
                g.tensor_tensor(OT[:, c, :], oh[:, 2 * c, :], oh[:, 2 * c + 1, :], ALU.add) \
                    .then_inc(s["packed"], 1)

            def low_half(n, c):
                pool.wait_ge(s["h_hi"], HC * n + c + 1)
                g.tensor_tensor(hTl[:, c, :], hh[:, c % 2, :], hTh[:, c, :], ALU.subtract) \
                    .then_inc(s["h_lo"], 1)

            def ffn_inverse_root(n):
                inverse_root(n, "ffn_ln", LN_STEPS * n + 7, rs_f, ve_f, "ffn_rstd")

            residual_in(0)
            with pool.Fori(1, B - 1) as n:
                residual_in(n)
                gain(n - 1)
            att_inverse_root(0)
            residual_in(LAST)
            third_part(0, 0)
            third_part(0, 1)
            gain(B - 2)
            third_part(0, 2)
            third_part(0, 3)
            gain(LAST)

            def step(n):
                if before(n, LAST):
                    att_inverse_root(n + 1)
                if since(n, 1):
                    ffn_inverse_root(n - 1)
                if before(n, LAST):
                    pool.wait_ge(s["parts_stored"], 96 * (n + 1))
                    for c in range(4):
                        third_part(n + 1, c)
                for item in POOL_ORDER:
                    kind, k = item[0], int(item[1])
                    if kind == "s":
                        keep_past(n, k)
                    elif kind == "p":
                        pack(n, k)
                    elif since(n, 1):
                        low_half(n - 1, k)

            step(0)
            step(1)
            with pool.Fori(2, B - 2) as n:
                step(n)
            step(B - 2)
            step(LAST)
            ffn_inverse_root(LAST)
            for c in range(HC):
                low_half(LAST, c)

        @block.scalar
        def _(act):
            a = nc.scalar
            act.wait_ge(s["loaded_mixw"], 96)
            a.activation(ebk[:, :], bk_sb[:, :], ACT.Exp).then_inc(s["ew_ready"], 1)
            a.mul(bqh[:, :], bq_sb[:, :], 0.5).then_inc(s["ew_ready"], 1)
            act.wait_ge(s["mix_consts"], 1)
            a.activation(ew[:, :, :], wbm[:, :, :], ACT.Exp).then_inc(s["ew_ready"], 1)
            act.wait_ge(s["ew_ready"], 3)
            a.mul(ebk2[:, :], ebk[:, :], 2.0).then_inc(s["ew_ready"], 1)

            def mixer_exps(n):
                first = isinstance(n, int) and n == 0
                for t in range(2):
                    act.wait_ge(s["kv_mm"], 2 * n + t + 1)
                    if not first and t == 0:
                        act.wait_ge(s["nd_mm"], n)
                    kv = half[0][:, 512 * t:512 * t + 512].rearrange("p (h w) -> p h w", h=2)
                    a.activation(ekv[:, t, 1, :].rearrange("p (h w) -> p h w", h=2), kv[:, :, 0:P], ACT.Exp) \
                        .then_inc(s["ek_ready"], 1)
                act.wait_ge(s["q_mm"], n + 1)
                if not first:
                    act.wait_ge(s["sg_ready"], n)
                a.activation(tq[:, :, :], PB[0].rearrange("p (c l) -> p c l", c=CH), ACT.Tanh, scale=0.5,
                             bias=bqh[:, 0:1]).then_inc(s["tq_ready"], 1)

            for n in range(3):
                mixer_exps(n)
            act.wait_ge(s["text_dve"], 11)
            a.activation(selx[:, :, :, :], selx[:, :, :, :], ACT.Exp).then_inc(s["text_act"], 1)
            with act.Fori(3, B) as n:
                mixer_exps(n)

            def xt_copy(n):
                act.wait_ge(s["xt_tr"], n + 1)
                if since(n, 1):
                    act.wait_ge(s["v_mm"], 3 * n)
                a.copy(xlnT[:, :, :], bank[2][:, :].rearrange("p (c w) -> p c w", c=2)[:, :, 0:S]) \
                    .then_inc(s["xt_copied"], 1)

            def first_parts(n, c):
                act.wait_ge(s["qk_mm"], 4 * n + c + 1)
                if since(n, 1) and c == 0:
                    act.wait_ge(s["parts_stored"], 96 * n)
                a.copy(parts[:, 0, c, :], PB[c % 2][:, 0:S]).then_inc(s["part1"], 1)

            def second_parts(n, c):
                act.wait_ge(s["rest_ready"], 4 * n + c + 1)
                a.copy(parts[:, 1, c, :], rest[:, c, :]).then_inc(s["part2"], 1)

            def v_copy(n, par, t):
                r = TILES[t][1]
                act.wait_ge(s["v_mm"], 3 * n + t + 1)
                if since(n, 2) and t == 0:
                    act.wait_ge(s["pv_mm"], 4 * (n - 1))
                for b in range(2):
                    a.copy(V[par].rearrange("p t (c b j) w -> p t c b j w", b=2, j=4)
                           [0:r, t, :, b, :, HD * b:HD * b + HD],
                           PB[t % 2][0:r, 0:MODEL].rearrange("p (c b j w) -> p c b j w", c=2, b=2, j=4)[:, :, b]) \
                        .then_inc(s["v_copied"], 1)

            def chunks(n):
                for c in range(4):
                    first_parts(n, c)
                    second_parts(n, c)

            def mt_copy(n):
                act.wait_ge(s["mt_tr"], n + 1)
                if since(n, 1):
                    act.wait_ge(s["m_stored"], 16 * n)
                a.copy(mT[:, :], OB[0:2 * HEADS, :].bitcast(bf16)[:, 0:S]).then_inc(s["mt_copied"], 1)

            def exps(n, k):
                if since(n, 1) or k >= 4:
                    act.wait_ge(s["pv_mm"], 4 * n + k // 2 - 1)
                for kt, (_, rows) in enumerate(TILES):
                    act.wait_ge(s["st_mm"], 16 * n + 2 * k + (1 if kt == 0 else 2))
                    off = 0 if kt < 2 else QW[1]
                    src = half[min(kt, 1)][0:rows, :].rearrange("p (h w) -> p h w", h=2)[:, :, off:off + QW[kt]]
                    a.activation(probs[0:rows, k % 4, :, QOFF[kt]:QOFF[kt] + QW[kt]], src, ACT.Exp,
                                 scale=HD ** -0.5).then_inc(s["exp_done"], 1)

            def fx_high(n):
                act.wait_ge(s["fxt_tr"], n + 1)
                if since(n, 1):
                    act.wait_ge(s["gu_mm"], HC * n)
                a.copy(xfh[:, :, :], bank[2][:, :].rearrange("p (c w) -> p c w", c=2)[:, :, 0:S]) \
                    .then_inc(s["fx_hi"], 1)

            def gate_tanh(n, c):
                act.wait_ge(s["gu_mm"], HC * n + c + 1)
                if since(n, 1) or c >= 1:
                    act.wait_ge(s["a_ready"], HC * n + c)
                a.activation(tg[:, :], PB[0][:, 0:S], ACT.Tanh, scale=0.5 / 127.0).then_inc(s["tanh_done"], 1)

            def h_high(n, c):
                act.wait_ge(s["h_ready"], HC * n + c + 1)
                if since(n, 1) and c == 0:
                    act.wait_ge(s["down_mm"], 3 * n)
                a.copy(hTh[:, c, :], hh[:, c % 2, :]).then_inc(s["h_hi"], 1)

            def step(n, par):
                if before(n, LAST):
                    xt_copy(n + 1)
                    chunks(n + 1)
                    v_copy(n + 1, 1 - par, 0)
                mt_copy(n)
                if before(n, LAST):
                    v_copy(n + 1, 1 - par, 1)
                    v_copy(n + 1, 1 - par, 2)
                if since(n, 1):
                    fx_high(n - 1)
                for item in ACT_ORDER:
                    kind, k = item[0], int(item[1])
                    if kind == "e":
                        exps(n, k)
                    elif since(n, 1):
                        (gate_tanh if kind == "t" else h_high)(n - 1, k)

            xt_copy(0)
            chunks(0)
            act.wait_ge(s["stack_ones"], 8)
            for t in range(3):
                v_copy(0, 0, t)
            act.wait_ge(s["ffw_cast"], 2)
            step(0, 0)
            step(1, 1)
            with act.Fori(1, PAIRS) as i:
                step(2 * i, 0)
                step(2 * i + 1, 1)
            step(B - 2, 0)
            step(LAST, 1)
            fx_high(LAST)
            for item in ACT_ORDER:
                if item[0] != "e":
                    (gate_tanh if item[0] == "t" else h_high)(LAST, int(item[1]))

        @block.vector
        def _(dve):
            v = nc.vector
            v.memset(resid[:, :, 2, :], 0.0).then_inc(s["text_dve"], 1)
            v.memset(xcT[0:F, :, 0:2], 0.0).then_inc(s["text_dve"], 1)
            v.memset(xcT[F:F + 1, :, :], 1.0).then_inc(s["text_dve"], 1)
            dve.wait_ge(s["loaded_wb"], 32)
            v.tensor_tensor(wbm[:, :, :], wb_sb[:, :, :], mask_sb[:, :, :], ALU.mult).then_inc(s["mix_consts"], 1)
            xe = resid[0:T, :, 2, 0:F]
            x1 = resid[0:T, :, 2, 2 * F:3 * F]

            def text_embed():
                dve.wait_ge(s["loaded_text"], 64)
                dve.wait_ge(s["gathered"], 16 * B)
                dve.wait_ge(s["text_dve"], 3)
                v.scalar_tensor_tensor(out=xe, in0=emb_sb[:, :, :], scalar=float(F) ** 0.5,
                                       in1=pos_sb[:, :].unsqueeze(1).to_broadcast([T, B, F]),
                                       op0=ALU.mult, op1=ALU.add).then_inc(s["text_dve"], 1)

            def text_columns():
                dve.wait_ge(s["text_tr"], 1)
                for k, b in enumerate((PB[1], MB)):
                    v.tensor_copy(xcT[0:F, 4 * k:4 * k + 4, 2:T + 2],
                                  b[0:F, 0:4 * T].rearrange("p (b t) -> p b t", b=4)) \
                        .then_inc(s["text_dve"], 1)

            def text_softmax_in():
                dve.wait_ge(s["text_mm"], 1)
                v.tensor_copy(x1, PB[1][0:T, :].rearrange("p (n f) -> p n f", n=B)).then_inc(s["text_dve"], 1)
                dve.wait_ge(s["text_dve"], 7)
                v.tensor_reduce(smx[:, 0, :], xe, axis=AX.X, op=ALU.max).then_inc(s["text_dve"], 1)
                v.tensor_reduce(smx[:, 1, :], x1, axis=AX.X, op=ALU.max).then_inc(s["text_dve"], 1)
                dve.wait_ge(s["text_dve"], 9)
                for k, src in enumerate((xe, x1)):
                    v.tensor_tensor(selx[:, k, :, :], src, smx[:, k, :].unsqueeze(2).to_broadcast([T, B, F]),
                                    ALU.subtract).then_inc(s["text_dve"], 1)

            def text_softmax_out():
                dve.wait_ge(s["text_act"], 1)
                v.tensor_reduce(ssum[:, :, :], selx[:, :, :, :], axis=AX.X, op=ALU.add) \
                    .then_inc(s["text_dve"], 1)
                dve.wait_ge(s["text_dve"], 12)
                v.reciprocal(srec[:, :, :], ssum[:, :, :]).then_inc(s["text_dve"], 1)
                dve.wait_ge(s["text_dve"], 13)
                v.tensor_tensor(selx[:, :, :, :], selx[:, :, :, :],
                                srec[:, :, :].unsqueeze(3).to_broadcast([T, 2, B, F]), ALU.mult) \
                    .then_inc(s["text_dve"], 1)

            def text_selectors():
                for k, b in enumerate((PB[1], MB)):
                    dve.wait_ge(s["text_tr"], 2 + k)
                    v.tensor_copy(selT[:, k, :, :], b[:, 0:4 * T].rearrange("p (b t) -> p b t", b=4)) \
                        .then_inc(s["text_dve"], 1)

            def text_positions():
                for odd, bank_ in enumerate((PB[1], MB)):
                    dve.wait_ge(s["text_mm"], 2 + odd)
                    v.tensor_copy(resid[0:T, :, 2, :].rearrange("p (m o) (k w f) -> p o k m w f", o=2, k=2, w=2)
                                  [:, odd, :, :, 1, :],
                                  bank_[0:T, :].rearrange("p (k m f) -> p k m f", k=2, m=B // 2)) \
                        .then_inc(s["text_dve"], 1)

            def cast_ffn_weights():
                dve.wait_ge(s["loaded_ffw"], 32)
                v.tensor_copy(wgu_sb[:, :, :, :], stage_gu).then_inc(s["ffw_cast"], 1)
                v.tensor_copy(wd_sb[:, :, :], stage_d).then_inc(s["ffw_cast"], 1)

            def mix_kv(n):
                for t in range(2):
                    dve.wait_ge(s["ek_ready"], 2 * n + t + 1)
                    kv = half[0][:, 512 * t:512 * t + 512].rearrange("p (h w) -> p h w", h=2)
                    v.tensor_tensor(ekv[:, t, 0, :].rearrange("p (h w) -> p h w", h=2),
                                    ekv[:, t, 1, :].rearrange("p (h w) -> p h w", h=2), kv[:, :, P:2 * P],
                                    ALU.mult).then_inc(s["ekv_ready"], 1)

            def mix_gate(n):
                dve.wait_ge(s["tq_ready"], n + 1)
                if since(n, 1):
                    dve.wait_ge(s["mix_avg"], MIX_AVG * n)
                v.tensor_scalar(sg[:, :, :], tq[:, :, :], 1.0, None, ALU.add).then_inc(s["sg_ready"], 1)

            def mix_divide(n):
                den = half[1][:, 512:1024].rearrange("p (c l) -> p c l", c=CH)
                dve.wait_ge(s["nd_mm"], n + 1)
                v.tensor_scalar(rden[:, :, :], den, ebk2[:, 0:1], None, ALU.mult).then_inc(s["mix_avg"], 1)
                dve.wait_ge(s["mix_avg"], MIX_AVG * n + 1)
                v.reciprocal(rden[:, :, :], rden[:, :, :]).then_inc(s["mix_avg"], 1)

            def mix_average(n):
                num = half[1][:, 0:512].rearrange("p (c l) -> p c l", c=CH)
                dve.wait_ge(s["mix_avg"], MIX_AVG * n + 2)
                v.scalar_tensor_tensor(out=yr[:, :, :], in0=rden[:, :, :], scalar=ebk[:, 0:1], in1=num,
                                       op0=ALU.mult, op1=ALU.mult).then_inc(s["mix_avg"], 1)
                dve.wait_ge(s["mix_avg"], MIX_AVG * n + 3)
                dve.wait_ge(s["sg_ready"], n + 1)
                if since(n, 1):
                    dve.wait_ge(s["mixout_mm"], n)
                v.scalar_tensor_tensor(out=yT[:, :, :], in0=yr[:, :, :], scalar=bvh[:, 0:1], in1=sg[:, :, :],
                                       op0=ALU.add, op1=ALU.mult).then_inc(s["mix_avg"], 1)

            def mix_norm(n):
                dve.wait_ge(s["mixout_mm"], n + 1)
                dve.wait_ge(s["xfb_ready"], n + 1)
                v.tensor_tensor(hpre[:, :, :], OB.rearrange("p (t m) -> p t m", t=2), xfb[:, :, :], ALU.add) \
                    .then_inc(s["mix_norm"], 1)
                dve.wait_ge(s["mix_norm"], MIX_NORM * n + 1)
                for t in range(2):
                    v.bn_stats(st_m[:, t, :], hpre[:, t, :]).then_inc(s["mix_norm"], 1)
                dve.wait_ge(s["mix_norm"], MIX_NORM * n + 3)
                dve.sem_inc(s["held_dve"], 1)
                for t in range(2):
                    v.bn_aggr(mv_m[:, t, :], st_m[:, t, :]).then_inc(s["mix_norm"], 1)
                dve.wait_ge(s["mix_norm"], MIX_NORM * n + 5)
                v.tensor_scalar(ve_m[:, :], mv_m[:, :, 1], EPS, None, ALU.add).then_inc(s["mix_norm"], 1)
                dve.wait_ge(s["mix_rstd"], n + 1)
                if since(n, 1):
                    dve.wait_ge(s["hg_ready"], n)
                for t in range(2):
                    v.tensor_scalar(hn[:, t, :], hpre[:, t, :], mv_m[:, t, 0:1], rs_m[:, t:t + 1],
                                    ALU.subtract, ALU.mult).then_inc(s["mix_norm"], 1)

            dve.wait_ge(s["loaded_mixw"], 96)
            v.tensor_scalar(bvh[:, :], bv_sb[:, :], 0.5, None, ALU.mult).then_inc(s["mix_consts"], 1)
            v.memset(mx[:, :, :], 0.0).then_inc(s["mix_consts"], 1)
            v.memset(MB[:, S:32 * SB], 1.0).then_inc(s["mix_consts"], 1)
            dve.wait_ge(s["mix_consts"], 4)
            dve.wait_ge(s["ew_ready"], 4)

            def mix_step(n, text_first=None, text_last=None):
                mix_divide(n)
                mix_kv(n + 1)
                mix_average(n)
                if text_first:
                    text_first()
                if since(n, 1):
                    mix_norm(n - 1)
                mix_gate(n + 1)
                if text_last:
                    text_last()

            mix_kv(0)
            mix_gate(0)
            mix_step(0, text_embed)
            text_columns()
            mix_step(1, None, text_softmax_in)
            text_softmax_out()
            mix_step(2, cast_ffn_weights, text_selectors)
            with dve.Fori(3, B - 1) as n:
                mix_step(n)

            def norm_stats(n, name, stats, mv, ve):
                base = LN_STEPS * n
                for t in range(3):
                    v.bn_stats(stats[:, t, :], resid[:, bass.ds(n, 1), t, :].rearrange("p a m -> p (a m)")) \
                        .then_inc(s[name], 1)
                dve.wait_ge(s[name], base + 3)
                dve.sem_inc(s["held_dve"], 1)
                for t in range(3):
                    v.bn_aggr(mv[:, t, :], stats[:, t, :]).then_inc(s[name], 1)
                dve.wait_ge(s[name], base + 6)
                v.tensor_scalar(ve[:, :], mv[:, :, 1], EPS, None, ALU.add).then_inc(s[name], 1)

            def norm_apply(n, name, mv, rs, rstd, dst):
                dve.wait_ge(s[rstd], n + 1)
                for t in range(3):
                    v.tensor_scalar(dst[:, t, :], resid[:, bass.ds(n, 1), t, :].rearrange("p a m -> p (a m)"),
                                    mv[:, t, 0:1], rs[:, t:t + 1], ALU.subtract, ALU.mult).then_inc(s[name], 1)

            def att_stats(n):
                dve.wait_ge(s["resid_ready"], n + 1)
                dve.sem_inc(s["held_dve"], 1)
                norm_stats(n, "att_ln", st_a, mv_a, ve_a)

            def att_apply(n):
                if since(n, 1):
                    dve.wait_ge(s["xt_tr"], n)
                norm_apply(n, "att_ln", mv_a, rs_a, "att_rstd", xln)

            def take_rest(n, c):
                dve.wait_ge(s["part1"], 4 * n + c + 1)
                if since(n, 1):
                    dve.wait_ge(s["part3"], 4 * n + c - 3)
                v.tensor_tensor(rest[:, c, :], PB[c % 2][:, 0:S], parts[:, 0, c, :], ALU.subtract) \
                    .then_inc(s["rest_ready"], 1)

            def row_max(n, u):
                t, h0, nh, per = SM[u]
                rows = TILES[t][1]
                dve.wait_ge(s["row_max_mm"], len(SM) * n + u + 1)
                src = half[u % 2][0:rows, :].rearrange("p (h w) -> p h w", h=nh)[:, :, 0:KEND[t]]
                v.tensor_reduce(mx[0:rows, t, h0:h0 + nh], src, axis=AX.X, op=ALU.max).then_inc(s["row_max"], 1)

            def split_max(n):
                dve.wait_ge(s["row_max"], len(SM) * (n + 1))
                if since(n, 1):
                    dve.wait_ge(s["mt_tr"], n)
                v.tensor_scalar(mhl[:, :, 0, :], mx[:, :, :], -1.0, None, ALU.mult).then_inc(s["maxima_ready"], 1)
                dve.wait_ge(s["maxima_ready"], 2 * n + 1)
                v.scalar_tensor_tensor(out=mhl[:, :, 1, :], in0=mx[:, :, :], scalar=-1.0, in1=mhl[:, :, 0, :],
                                       op0=ALU.mult, op1=ALU.subtract).then_inc(s["maxima_ready"], 1)

            def add_attention(n, t):
                rows = TILES[t][1]
                dve.wait_ge(s["oproj_mm"], 3 * n + (2 if t < 2 else 3))
                src = (MB[:, 0:MODEL], MB[:, MODEL:2 * MODEL], OB[:, 0:MODEL])[t]
                r = resid[0:rows, bass.ds(n, 1), t, :].rearrange("p a m -> p (a m)")
                v.tensor_tensor(r, r, src[0:rows, :], ALU.add).then_inc(s["attn_added"], 1)

            def normalise(n, g):
                ob = (OB, MB)[g % 2]
                dve.wait_ge(s["pv_mm"], 4 * n + g + 1)
                v.transpose(denT[:, :], ob[:, 0:32 * SB]).then_inc(s["norm_steps"], 1)
                dve.wait_ge(s["norm_steps"], 12 * n + 3 * g + 1)
                v.reciprocal(denr[:, :], denT[:, :].rearrange("p (b c) -> p b c", c=32)[:, :, HD * (1 - g % 2)]) \
                    .then_inc(s["norm_steps"], 1)
                dve.wait_ge(s["norm_steps"], 12 * n + 3 * g + 2)
                v.transpose(scale[:, :], denr[:, :].unsqueeze(2).to_broadcast([P, SB, 32])) \
                    .then_inc(s["norm_steps"], 1)
                dve.wait_ge(s["norm_steps"], 12 * n + 3 * g + 3)
                if since(n, 1):
                    dve.wait_ge(s["packed"], 2 * (n - 1) + g // 2 + 1)
                v.scalar_tensor_tensor(out=oh[:, g, :], in0=scale[:, 0:S], scalar=row_mask[:, g % 2:g % 2 + 1],
                                       in1=ob[:, 0:S], op0=ALU.mult, op1=ALU.mult).then_inc(s["normed"], 1)

            def ffn_apply(n):
                if since(n, 1):
                    dve.wait_ge(s["fxt_tr"], n)
                norm_apply(n, "ffn_ln", mv_f, rs_f, "ffn_rstd", xlnf)

            def ffn_stats(n):
                dve.wait_ge(s["attn_added"], 3 * n + 3)
                dve.sem_inc(s["held_dve"], 1)
                norm_stats(n, "ffn_ln", st_f, mv_f, ve_f)

            def fx_low(n):
                dve.wait_ge(s["fx_hi"], n + 1)
                if since(n, 1):
                    dve.wait_ge(s["gu_mm"], HC * n)
                v.tensor_tensor(xfl[:, :, :], bank[2][:, :].rearrange("p (c w) -> p c w", c=2)[:, :, 0:S],
                                xfh[:, :, :], ALU.subtract).then_inc(s["fx_lo"], 1)

            def hidden(n, c):
                dve.wait_ge(s["tanh_done"], HC * n + c + 1)
                v.scalar_tensor_tensor(out=ag[:, :], in0=tg[:, :], scalar=1.0, in1=PB[0][:, 0:S],
                                       op0=ALU.add, op1=ALU.mult).then_inc(s["a_ready"], 1)
                dve.wait_ge(s["a_ready"], HC * n + c + 1)
                if since(n, 1) or c >= 2:
                    dve.wait_ge(s["h_lo"], HC * n + c - 1)
                v.scalar_tensor_tensor(out=hh[:, c % 2, :], in0=ag[:, :], scalar=HSCALE / (2 * 127.0 ** 2),
                                       in1=PB[1][:, 0:S], op0=ALU.mult, op1=ALU.mult).then_inc(s["h_ready"], 1)

            def finish(n, t):
                if since(n, 1) and t == 0:
                    dve.wait_ge(s["out_stored"], 32 * n)
                rows = TILES[t][1]
                dve.wait_ge(s["down_mm"], 3 * n + (2 if t < 2 else 3))
                src = (OB[:, 0:MODEL], OB[:, MODEL:2 * MODEL], MB[:, 0:MODEL])[t]
                v.scalar_tensor_tensor(out=ost[0:rows, t, :], in0=src[0:rows, :], scalar=1.0 / (127.0 * HSCALE),
                                       in1=resid[0:rows, bass.ds(n, 1), t, :].rearrange("p a m -> p (a m)"),
                                       op0=ALU.mult, op1=ALU.add).then_inc(s["final_ready"], 1)

            def step(n):
                for u in range(len(SM)):
                    row_max(n, u)
                    if before(n, LAST):
                        if u == 0:
                            att_stats(n + 1)
                        if u == 1:
                            att_apply(n + 1)
                        if u in REST_AFTER:
                            take_rest(n + 1, REST_AFTER.index(u))
                    if since(n, 1):
                        if u == 2:
                            add_attention(n - 1, 0)
                            add_attention(n - 1, 1)
                        if u == 4:
                            add_attention(n - 1, 2)
                            ffn_stats(n - 1)
                        if u == 5:
                            ffn_apply(n - 1)
                    if since(n, 2):
                        if u == 10:
                            finish(n - 2, 0)
                            finish(n - 2, 1)
                        if u == 12:
                            finish(n - 2, 2)
                split_max(n)
                if since(n, 1):
                    fx_low(n - 1)
                for item in DVE_ORDER:
                    kind, k = item[0], int(item[1])
                    if kind == "n":
                        normalise(n, k)
                    elif since(n, 1):
                        hidden(n - 1, k)

            text_positions()
            dve.wait_ge(s["text_dve"], 18)
            att_stats(0)
            att_apply(0)
            mix_divide(LAST)
            take_rest(0, 0)
            take_rest(0, 1)
            mix_average(LAST)
            mix_norm(B - 2)
            take_rest(0, 2)
            take_rest(0, 3)
            mix_norm(LAST)
            dve.wait_ge(s["loaded_attw"], 48)
            step(0)
            step(1)
            with dve.Fori(2, B - 2) as n:
                step(n)
            step(B - 2)
            step(LAST)
            for t in range(3):
                add_attention(LAST, t)
            ffn_stats(LAST)
            ffn_apply(LAST)
            for t in range(3):
                finish(B - 2, t)
            fx_low(LAST)
            for c in range(HC):
                hidden(LAST, c)
            for t in range(3):
                finish(LAST, t)

        @block.tensor
        def _(pe):
            mm, tr = nc.tensor.matmul, nc.tensor.transpose
            def text_transpose():
                pe.wait_ge(s["consts_ready"], 7)
                pe.wait_ge(s["text_dve"], 4)
                for n in range(B):
                    last = tr((PB[1], MB)[n // 4][0:F, T * (n % 4):T * (n % 4) + T], resid[0:T, n, 2, 0:F], ident[0:T, 0:T])
                last.then_inc(s["text_tr"], 1)

            def text_convolve():
                pe.wait_ge(s["loaded_text"], 64)
                pe.wait_ge(s["text_dve"], 6)
                for n in range(B):
                    for tap in range(3):
                        last = mm(PB[1][0:T, n * F:(n + 1) * F], xcT[:, n, tap:tap + T], conv_sb[:, tap, :],
                                  start=(tap == 0), stop=(tap == 2))
                last.then_inc(s["text_mm"], 1)

            def text_transpose_selectors():
                pe.wait_ge(s["text_dve"], 14)
                for k, b in enumerate((PB[1], MB)):
                    for m in range(B // 2):
                        last = tr(b[:, T * m:T * m + T], selx[:, k, 2 * m:2 * m + 2, :].rearrange("p n f -> p (n f)"),
                                  ident[0:T, 0:T])
                    last.then_inc(s["text_tr"], 1)

            def text_soft_positions():
                pe.wait_ge(s["text_dve"], 16)
                for odd, bank_ in enumerate((PB[1], MB)):
                    r0 = F * odd
                    for k in range(2):
                        for m in range(B // 2):
                            o = F * (B // 2 * k + m)
                            last = mm(bank_[0:T, o:o + F], selT[r0:r0 + F, k, m, :], spos_sb[r0:r0 + F, k, :],
                                      start=True, stop=True)
                    last.then_inc(s["text_mm"], 1)

            def key_value(n):
                pe.wait_ge(s["x_loaded"], 16 * (n + 1))
                for t in range(2):
                    if since(n, 1):
                        pe.wait_ge(s["ekv_ready"], 2 * n)
                    for h in range(2):
                        last = mm(half[0][:, 512 * t + 256 * h:512 * t + 256 * h + 256],
                                  xs[:, h, P * t:P * t + P], wkv_sb[:, :], start=True, stop=True)
                    last.then_inc(s["kv_mm"], 1)

            def queries(n):
                if since(n, 1):
                    pe.wait_ge(s["tq_ready"], n)
                for h in range(2):
                    last = mm(PB[0][:, L * h:L * h + L], wq_sb[:, :], xs[:, h, :], start=True, stop=True)
                last.then_inc(s["q_mm"], 1)

            def averages(n):
                pe.wait_ge(s["ekv_ready"], 2 * n + 2)
                if since(n, 1):
                    pe.wait_ge(s["mix_avg"], MIX_AVG * (n - 1) + 3)
                for c in range(CH):
                    for nd in range(2):
                        for t in range(2):
                            last = mm(half[1][:, 512 * nd + L * c:512 * nd + L * c + L],
                                      ekv[:, t, nd, P * c:P * c + P], ew[:, t, :], start=(t == 0), stop=(t == 1))
                last.then_inc(s["nd_mm"], 1)

            def mix_project(n):
                pe.wait_ge(s["mix_avg"], MIX_AVG * n + 4)
                if since(n, 1):
                    pe.wait_ge(s["mix_norm"], MIX_NORM * (n - 1) + 1)
                for t in range(2):
                    for c in range(CH):
                        last = mm(OB[:, MODEL * t:MODEL * t + MODEL], yT[:, c, P * t:P * t + P], outw_sb[:, c, :],
                                  start=(c == 0), stop=(c == CH - 1))
                last.then_inc(s["mixout_mm"], 1)

            def mix_step(n):
                averages(n)
                key_value(n + 1)
                if since(n, 1):
                    mix_project(n - 1)
                queries(n + 1)

            pe.wait_ge(s["loaded_mixw"], 96)
            key_value(0)
            queries(0)
            pe.wait_ge(s["ew_ready"], 4)
            mix_step(0)
            text_transpose()
            mix_step(1)
            text_convolve()
            mix_step(2)
            text_transpose_selectors()
            with pe.Fori(3, B - 1) as n:
                mix_step(n)

            def transpose_tokens(src, name):
                for t, (t0, rows) in enumerate(TILES):
                    for c in range(CH):
                        last = tr(PB[c][:, t0:t0 + rows], src[0:rows, t, P * c:P * c + P], ident[0:rows, 0:rows])
                last.then_inc(s[name], 1)

            def att_transpose(n):
                pe.wait_ge(s["att_ln"], LN_STEPS * (n + 1))
                if since(n, 3):
                    pe.wait_ge(s["h_ready"], HC * (n - 2))
                if since(n, 1):
                    pe.wait_ge(s["v_copied"], 6 * n)
                transpose_tokens(xln, "xt_tr")

            def query_key(n, c):
                if c < 2:
                    pe.wait_ge(s["xt_copied"], n + 1)
                else:
                    pe.wait_ge(s["rest_ready"], 4 * n + c - 1)
                for kc in range(CH):
                    last = mm(PB[c % 2][:, 0:S], wqkv_sb[:, c // 2, kc, P * (c % 2):P * (c % 2) + P], xlnT[:, kc, :],
                              start=(kc == 0), stop=(kc == CH - 1))
                last.then_inc(s["qk_mm"], 1)

            def values(n, t):
                if t < 2:
                    pe.wait_ge(s["rest_ready"], 4 * n + 3 + t)
                else:
                    pe.wait_ge(s["v_copied"], 6 * n + 2)
                t0, rows = TILES[t]
                for kc in range(CH):
                    last = mm(PB[t % 2][0:rows, 0:MODEL], xlnT[:, kc, t0:t0 + rows], wqkv_sb[:, 2, kc, :],
                              start=(kc == 0), stop=(kc == CH - 1))
                last.then_inc(s["v_mm"], 1)

            def scores_for_max(n, par, u):
                t, h0, nh, per = SM[u]
                t0, rows = TILES[t]
                if u >= 2:
                    pe.wait_ge(s["row_max"], len(SM) * n + u - 1)
                elif since(n, 1):
                    pe.wait_ge(s["exp_done"], 24 * n - (2 if u == 0 else 0))
                for i in range(nh):
                    h = h0 + i
                    o = 512 * (i // per) + KEND[t] * (i % per)
                    mm(half[u % 2][0:rows, o:o + KEND[t]], QS[par][0:STK, h, t0:t0 + rows], KS[par][0:STK, h, 0:KEND[t]],
                       start=True, stop=False)
                    last = mm(half[u % 2][0:rows, o + t0:o + t0 + rows], identb[:, 0:rows], causal[:, 0:rows],
                              start=False, stop=True)
                last.then_inc(s["row_max_mm"], 1)

            def transpose_max(n):
                pe.wait_ge(s["maxima_ready"], 2 * n + 2)
                if since(n, 1):
                    pe.wait_ge(s["attn_added"], 3 * n)
                if since(n, 2):
                    pe.wait_ge(s["final_ready"], 3 * (n - 1))
                for t, (t0, rows) in enumerate(TILES):
                    last = tr(OB[0:2 * HEADS, :].bitcast(bf16)[:, t0:t0 + rows],
                              mhl[0:rows, t, :, :].rearrange("p a h -> p (a h)"), identb[0:rows, 0:rows])
                last.then_inc(s["mt_tr"], 1)

            def scores_transposed(n, par, k):
                for kt, (t0, rows) in enumerate(TILES):
                    if kt < 2:
                        if k == 0:
                            pe.wait_ge(s["row_max"], len(SM) * n + 13 + kt)
                        else:
                            pe.wait_ge(s["exp_done"], 24 * n + 3 * (k - 1) + (1 if kt == 0 else 3))
                    off = 0 if kt < 2 else QW[1]
                    for i in range(2):
                        o = 512 * i + off
                        last = mm(half[min(kt, 1)][0:rows, o:o + QW[kt]], KS[par][0:STK + 2, 2 * k + i, t0:t0 + rows],
                                  QS[par][0:STK + 2, 2 * k + i, t0:S], start=True, stop=True)
                    if kt != 1:
                        last.then_inc(s["st_mm"], 1)

            def weighted_values(n, par, g):
                pe.wait_ge(s["selected"], 24 * n + 6 * (g + 1))
                if g >= 2:
                    pe.wait_ge(s["normed"], 4 * n + g - 1)
                elif g == 0:
                    pe.wait_ge(s["mt_copied"], n + 1)
                for kt, (t0, rows) in enumerate(TILES):
                    for j in range(4):
                        h = 4 * g + j
                        last = mm((OB, MB)[g % 2][32 * j:32 * j + 32, t0:S], V[par][0:rows, kt, h, :],
                                  probs[0:rows, (h // 2) % 4, h % 2, QOFF[kt]:QOFF[kt] + QW[kt]],
                                  start=(kt == 0), stop=(kt == 2))
                last.then_inc(s["pv_mm"], 1)

            def out_project(n, t):
                t0, rows = TILES[t]
                pe.wait_ge(s["normed"], 4 * n + 4)
                pe.wait_ge(s["packed"], 2 * n + 2)
                dst = (MB[:, 0:MODEL], MB[:, MODEL:2 * MODEL], OB[:, 0:MODEL])[t]
                for c in range(2):
                    last = mm(dst[0:rows, :], OT[:, c, t0:t0 + rows], wo_sb[:, c, :], start=(c == 0), stop=(c == 1))
                last.then_inc(s["oproj_mm"], 1)

            def ffn_transpose(n):
                pe.wait_ge(s["ffn_ln"], LN_STEPS * (n + 1))
                if not before(n, LAST):
                    pe.wait_ge(s["h_ready"], HC * n)
                else:
                    pe.wait_ge(s["v_copied"], 6 * B if isinstance(n, int) and n == B - 2 else 6 * (n + 3))
                transpose_tokens(xlnf, "fxt_tr")

            def gate_up(n, c):
                if c == 0:
                    pe.wait_ge(s["fx_lo"], n + 1)
                else:
                    pe.wait_ge(s["h_ready"], HC * n + c)
                for gu in range(2):
                    for kc in range(CH):
                        for x in (xfh, xfl):
                            last = mm(PB[gu][:, 0:S], wgu_sb[:, gu, kc, P * c:P * c + P],
                                      x[:, kc, :], start=(kc == 0 and x is xfh), stop=(kc == CH - 1 and x is xfl))
                last.then_inc(s["gu_mm"], 1)

            def down(n, t):
                if t == 0:
                    pe.wait_ge(s["h_hi"], HC * (n + 1))
                    pe.wait_ge(s["h_lo"], HC * (n + 1))
                    pe.wait_ge(s["attn_added"], 3 * B if not before(n, LAST) else 3 * (n + 2))
                    if not before(n, LAST):
                        pe.wait_ge(s["final_ready"], 3 * n)
                t0, rows = TILES[t]
                dst = (OB[:, 0:MODEL], OB[:, MODEL:2 * MODEL], MB[:, 0:MODEL])[t]
                for c in range(HC):
                    for x in (hTh, hTl):
                        last = mm(dst[0:rows, :], x[:, c, t0:t0 + rows], wd_sb[:, c, :],
                                  start=(c == 0 and x is hTh), stop=(c == HC - 1 and x is hTl))
                last.then_inc(s["down_mm"], 1)

            def step(n, par, turns):
                pe.wait_ge(s[f"stacked{par}"], 192 * turns)
                for u in range(len(SM)):
                    scores_for_max(n, par, u)
                    if since(n, 1):
                        if u == 1:
                            out_project(n - 1, 0)
                            out_project(n - 1, 1)
                        if u == 3:
                            out_project(n - 1, 2)
                    if before(n, LAST):
                        if u == 4:
                            att_transpose(n + 1)
                        if u in (5, 6, 8, 10):
                            query_key(n + 1, (5, 6, 8, 10).index(u))
                    if since(n, 2) and u in (7, 9, 11):
                        down(n - 2, (u - 7) // 2)
                if before(n, LAST):
                    values(n + 1, 0)
                transpose_max(n)
                if before(n, LAST):
                    values(n + 1, 1)
                    values(n + 1, 2)
                if since(n, 1):
                    ffn_transpose(n - 1)
                pe.wait_ge(s["m_loaded"], 16 * (n + 1))
                for item in PE_ORDER:
                    kind, k = item[0], int(item[1])
                    if kind == "s":
                        scores_transposed(n, par, k)
                    elif kind == "w":
                        weighted_values(n, par, k)
                    elif since(n, 1):
                        gate_up(n - 1, k)

            text_soft_positions()
            averages(LAST)
            pe.wait_ge(s["loaded_attw"], 48)
            pe.wait_ge(s["text_dve"], 18)
            pe.wait_ge(s["tq_ready"], B)
            att_transpose(0)
            query_key(0, 0)
            query_key(0, 1)
            mix_project(B - 2)
            query_key(0, 2)
            query_key(0, 3)
            mix_project(LAST)
            for t in range(3):
                values(0, t)
            pe.wait_ge(s["stack_ones"], 8)
            pe.wait_ge(s["mix_norm"], MIX_NORM * LAST + 1)
            step(0, 0, 1)
            step(1, 1, 1)
            with pe.Fori(1, PAIRS) as i:
                step(2 * i, 0, i + 1)
                step(2 * i + 1, 1, i + 1)
            step(B - 2, 0, B // 2)
            step(LAST, 1, B // 2)
            for t in range(3):
                out_project(LAST, t)
            for t in range(3):
                down(B - 2, t)
            ffn_transpose(LAST)
            for c in range(HC):
                gate_up(LAST, c)
            for t in range(3):
                down(LAST, t)


def kernel(**inputs):
    import concourse.bacc as bacc
    from concourse import mybir as mb
    from concourse.bass_utils import run_bass_kernel_spmd

    x = {k: np.asarray(v) for k, v in inputs.items()}
    z = np.zeros((F, F), np.float32)

    def halves(w):
        return w.T.reshape(-1, P, w.shape[0]).transpose(1, 0, 2)

    def two_heads(*ws):
        top = [m for w in ws for m in (w.T, z)]
        low = [m for w in ws for m in (z, w.T)]
        return np.concatenate([np.concatenate(top, 1), np.concatenate(low, 1)], 0)

    def column(b):
        return np.concatenate([b, b]).reshape(P, 1)

    depth = F // 2
    angle = np.arange(T, dtype=np.float32)[:, None] * \
        (np.float32(1.0) / np.float32(2500) ** (np.arange(depth, dtype=np.float32)[None, :] / np.float32(depth)))
    pos = np.concatenate([np.sin(angle), np.cos(angle)], -1).astype(np.float32)

    conv = np.concatenate([x["L0_txt_conv_w"].transpose(1, 0, 2), np.zeros((1, 3, F), np.float32)], 0)
    conv[F, 2, :] = x["L0_txt_conv_b"]
    wo = x["L0_attn_o_proj_weight"].T.reshape(2, 2, 4, HD, MODEL).transpose(2, 1, 3, 0, 4)
    rmask = (np.arange(P)[:, None] // HD % 2 == np.arange(2)[None, :]).astype(np.float32)
    xm = x["x"]
    arrays = dict(
        x_mix=xm.transpose(0, 3, 1, 2).reshape(B, 2, 2, F, L).transpose(0, 2, 3, 1, 4).reshape(B, P, 2, L),
        x_flat=xm.transpose(0, 2, 3, 1).reshape(B, 2, P, MODEL).transpose(0, 2, 1, 3),
        tokens=x["x_txt"].T, pos=pos,
        wkv=two_heads(x["L0_tok_Wk_w"], x["L0_tok_Wv_w"]), wq=two_heads(x["L0_tok_Wq_w"]),
        bq=column(x["L0_tok_Wq_b"]), bk=column(x["L0_tok_Wk_b"]), bv=column(x["L0_tok_Wv_b"]),
        wbt=halves(x["L0_tok_w_bias"]), maskt=halves(x["L0_tok_local_mask"]),
        outw=x["L0_tok_out_w"].reshape(CH, P, MODEL).transpose(1, 0, 2),
        rows3=np.broadcast_to(np.stack([x["L0_tok_out_b"], x["L0_tok_ln_g"], x["L0_tok_ln_b"]])[None],
                              (P, 3, MODEL)),
        emb=x["L0_txt_emb_table"], convw=conv,
        spos=np.stack([x["L0_txt_spos0"], x["L0_txt_spos1"]], 1),
        wqkv=np.stack([halves(x[f"L0_attn_{m}_proj_weight"]) for m in "qkv"], 1),
        wo=wo.reshape(P, 2, MODEL), rmask=rmask,
        wgu=np.stack([halves(x["L0_ffn_w_gate"]), halves(x["L0_ffn_w_up"])], 1),
        wd=halves(x["L0_ffn_w_down"]),
    )
    nc = bacc.Bacc("TRN2", target_bir_lowering=False, num_devices=1)
    sent, args = {}, []
    for name, a in arrays.items():
        a = np.ascontiguousarray(a)
        sent[f"in_{name}"] = a
        dt = mb.dt.uint8 if a.dtype == bool else mb.dt.from_np(a.dtype)
        args.append(nc.dram_tensor(f"in_{name}", a.shape, dt, kind="ExternalInput").ap())
    args.append(nc.dram_tensor("out", (B, S, MODEL), mb.dt.float32, kind="ExternalOutput").ap())
    build(nc, *args)
    r = run_bass_kernel_spmd(nc, [sent], core_ids=[0])
    return r.results[0]["out"]
```

```python
from contextlib import ExitStack

import numpy as np

import concourse.bass as bass
from concourse import mybir

B, F, L, H4 = 8, 64, 256, 4
MODEL = H4 * F
T = 77
S = L + T
HEADS, HD = 16, 16
HIDDEN = 768
P = 128
TILES = [(0, P), (P, P), (2 * P, T)]
KEND = [P, 2 * P, S]
QW = [S, S - P, T]
QOFF = [0, S, 2 * S - P]
PW = sum(QW)
CH = MODEL // P
HC = HIDDEN // P
SB = -(-S // 32)
EPS = 1e-5
STK_PARTS = 6
RUNS_Q = [(0, 3), (0, 2), (0, 1)]
RUNS_K = [(0, 3), (1, 2), (2, 1)]
STK = HD * STK_PARTS
MASKED = -1e30
LAST = B - 1
PAIRS = B // 2 - 1
PE_MAX_ORDER = "r2 x0 q0 o0 r3 r4 o1 r5 o2 r6 q1 q2 r7 r8 d0 q3 m0 r9 d1 r10 d2 r11 r12 v0 r13 v1 v2 m1 f0".split()
ACT_MAX_ORDER = "x0 q0 q1 w0 q2 m0 q3 v0 v1 v2 m1 f0".split()
DVE_MAX_ORDER = "r2 r3 r4 o0 o1 q0 o2 r5 w0 r6 q1 m0 r7 r8 q2 r9 q3 r10 r11 d0 d1 d2 r12 r13 m1 f0".split()
POOL_MAX_ORDER = "q0 w0 q1 q2 q3".split()
PE_ORDER = "s0 s1 g0 u0 s2 w0 g1 s3 u1 g2 s4 u2 w1 g3 s5 u3 s6 g4 u4 w2 s7 g5 u5 r0 r1 w3".split()
ACT_ORDER = "s0 s1 t0 s2 h0 t1 s3 h1 t2 a0 s4 h2 t3 s5 a1 h3 t4 s6 a2 h4 s7 t5 h5".split()
DVE_ORDER = "a0 h0 h1 n0 h2 n1 h3 h4 n2 r0 h5 n3 r1".split()
POOL_ORDER = "s0 s1 s2 a0 h0 s3 s4 h1 h2 s5 h3 p0 h4 s6 s7 h5 p1".split()
HSCALE = 0.5
ARENA = 14730
MIX_AVG, MIX_NORM = 5, 7
LN_STEPS = 8

HH = HEADS // 2
SM = [unit for h in (0, HH)
      for unit in [(0, h, HH, 4), (1, h, 4, 2), (1, h + 4, 4, 2)] + [(2, h + 2 * i, 2, 1) for i in range(4)]]
SMH = len(SM) // 2


def build(nc, x_mix, x_flat, tokens, pos, wkv, wq, bq, bk, bv, wbt, maskt, outw, rows3,
          emb, convw, spos, wqkv_t, wo_t, rmask, wgu, wd, out):
    f32, bf16, f16 = mybir.dt.float32, mybir.dt.bfloat16, mybir.dt.float16
    i32, u8 = mybir.dt.int32, mybir.dt.uint8
    ALU, ACT, AX = mybir.AluOpType, mybir.ActivationFunctionType, mybir.AxisListType

    ctx = ExitStack()
    with ctx:
        def sb(name, shape, dt=f32):
            return ctx.enter_context(nc.sbuf_tensor(name, shape, dt))

        def sem(name):
            return ctx.enter_context(nc.semaphore(name))

        resid = sb("resid", [P, B, 3, MODEL])
        ident = sb("ident", [P, P])
        identb = sb("identb", [P, P], bf16)
        causal = sb("causal", [P, P], bf16)
        tok_sb = sb("tok_sb", [T, B], i32)
        nhalf = sb("nhalf", [P, 3])
        one = sb("one", [P, 1])
        arena = sb("arena", [P, ARENA])

        def carver():
            at = [0]

            def take(*dims, dt=f32, rows=P):
                words = int(np.prod(dims)) // (1 if dt == f32 else 2)
                part = arena[0:rows, at[0]:at[0] + words]
                at[0] += words
                assert at[0] <= ARENA
                part = part if dt == f32 else part.bitcast(dt)
                names = "abcd"[:len(dims)]
                return part.rearrange(f"p ({' '.join(names)}) -> p {' '.join(names)}", **dict(zip(names, dims)))
            return take

        early, late = carver(), carver()
        pos_sb = early(F, rows=T)
        emb_sb = early(B, F, rows=T)
        conv_sb = early(3, F, rows=F + 1)
        spos_sb = early(2, F)
        xcT = early(B, T + 2, rows=F + 1)
        selx = early(2, B, F, rows=T)
        smx = early(2, B, rows=T)
        ssum = early(2, B, rows=T)
        srec = early(2, B, rows=T)
        selT = early(2, B // 2, T)
        wkv_sb = early(4 * F)
        wq_sb = early(P)
        bq_sb, bqh, bk_sb, ebk, ebk2, bv_sb, bvh = (early(1) for _ in range(7))
        wb_sb = early(2, L)
        wbm = early(2, L)
        ew = early(2, L)
        outw_sb = early(CH, MODEL)
        rows_sb = early(3, MODEL)
        xs = early(2, 2, L)
        xf = early(2, MODEL)
        xfb = early(2, MODEL)
        ekv = early(2, 2, MODEL)
        tq = early(CH, L)
        sg = early(2, CH, L)
        rden = early(CH, L)
        yr = early(CH, L)
        yT = early(CH, L)
        hpre = early(2, MODEL)
        hn = early(2, MODEL)
        hg = early(2, MODEL)
        st_m = early(2, 6)
        mv_m = early(2, 2)
        ve_m = early(2)
        nm_m = early(2)
        rs_m = early(2)
        nb_m = early(2)
        mask_sb = sb("mask_sb", [P, 2, L], u8)
        wqkv_sb = sb("wqkv_sb", [P, 3, CH, MODEL])
        wo_sb = sb("wo_sb", [P, 2, MODEL])
        st_a = sb("st_a", [P, 3, 6])
        mv_a = sb("mv_a", [P, 3, 2])
        ve_a = sb("ve_a", [P, 3])
        nm_a = sb("nm_a", [P, 3])
        rs_a = sb("rs_a", [P, 3])
        nb_a = sb("nb_a", [P, 3])
        xln = sb("xln", [P, 3, MODEL])
        xlnT = sb("xlnT", [P, CH, S])
        parts = sb("parts", [P, 3, 4, S], bf16)
        rest = sb("rest", [P, 4, S])
        qstack = [sb(f"qstack{p}", [P, HEADS * S], bf16) for p in range(2)]
        kstack = [sb(f"kstack{p}", [P, HEADS * S], bf16) for p in range(2)]
        QS, KS = ([x[:, :].rearrange("p (h t) -> p h t", h=HEADS) for x in xs2] for xs2 in (qstack, kstack))
        V = [sb(f"V{p}", [P, 3, HEADS, 32])[:, :, :, :] for p in range(2)]
        mx = sb("mx", [P, 3, HEADS])
        mhl = sb("mhl", [P, 3, 2, 2, HH], bf16)
        mT = [sb(f"mT{p}", [2 * HH, S], bf16) for p in range(2)]
        probs = sb("probs", [P, 4, 2, PW])
        denT = sb("denT", [P, SB * 32])
        denr = sb("denr", [P, SB])
        scale = sb("scale", [P, SB * 32])
        oh = sb("oh", [P, 4, S])
        OT = sb("OT", [P, 2, S])
        row_mask = sb("row_mask", [P, 2])
        st_f = sb("st_f", [P, 3, 6])
        mv_f = sb("mv_f", [P, 3, 2])
        ve_f = sb("ve_f", [P, 3])
        nm_f = sb("nm_f", [P, 3])
        rs_f = sb("rs_f", [P, 3])
        nb_f = sb("nb_f", [P, 3])
        xlnf = late(3, MODEL)
        xfh = late(CH, S, dt=f16)
        xfl = late(CH, S, dt=f16)
        tg = late(2, S)
        ag = late(2, S)
        hh = late(2, S)
        hTh = late(HC, S, dt=f16)
        hTl = late(HC, S, dt=f16)
        ost = late(3, MODEL)
        wgu_sb = sb("wgu_sb", [P, 2, CH, HIDDEN], f16)
        wd_sb = sb("wd_sb", [P, HC, MODEL], f16)
        stage = probs[:, :, :, :].rearrange("p a b c -> p (a b c)")
        stage_gu = stage[:, 0:2 * CH * HIDDEN].bitcast(i32).rearrange("p (a c n) -> p a c n", a=2, c=CH)
        stage_d = stage[:, 2 * CH * HIDDEN:2 * CH * HIDDEN + HC * MODEL].bitcast(i32) \
            .rearrange("p (c n) -> p c n", c=HC)

        bank = [ctx.enter_context(nc.psum_tensor(f"bank{i}", [P, 1024], f32)) for i in range(4)]
        half = [bank[0], bank[1]]
        PB = [bank[2][:, 0:512], bank[2][:, 512:1024]]
        TAIL = [(PB[0], PB[1]), (bank[0][:, 0:512], bank[0][:, 512:1024])]
        OB, MB = bank[3][:, 0:512], bank[3][:, 512:1024]
        RING_DOWN = [bank[1][:, MODEL * t:MODEL * t + MODEL] for t in range(3)]
        TAIL_DOWN = [x[:, 0:MODEL] for x in (MB, OB, bank[1])]             

        qk_dram = [nc.dram_tensor(f"qk_parts{p}", [2, CH, 3, P, S], bf16).ap() for p in range(2)]
        m_dram = [nc.dram_tensor(f"max_rows{p}", [2 * HH, S], bf16).ap() for p in range(2)]

        names = """loaded_tok loaded_text loaded_wkv loaded_mixw loaded_outw loaded_wb loaded_rows loaded_attw
        loaded_ffw consts_ready gathered text_dve text_tr text_act text_mm ffw_cast mix_consts ew_ready
        x_loaded0 x_loaded1 xf_loaded xfb_ready den_ready hn_ready kv_mm q_mm ek_ready tq_ready ekv_ready
        sg_ready nd_mm mixout_mm mix_avg mix_norm mix_rstd att_rstd ffn_rstd hg_ready resid_ready packed
        att_ln xt_tr xt_copied qk_mm part1 rest_ready part2 part3 v_mm v_copied stack_ones parts_stored
        stacked0 stacked1 row_max_mm row_max maxima_ready mt_tr mt_copied m_stored m_loaded0 m_loaded1 st_mm
        exp_done selected pv_mm norm_steps normed oproj_mm attn_added ffn_ln att_applied ffn_applied fxt_tr
        fx_hi fx_lo gate_mm up_mm tanh_done a_ready h_ready h_hi h_lo down_mm final_ready out_stored
        held_pool held_dve held_sync held_act""".split()
        s = {n: sem(n) for n in names}

        block = ctx.enter_context(nc.Block())
        def since(n, k):
            return not isinstance(n, int) or n >= k

        def before(n, k):
            return not isinstance(n, int) or n < k

        def prep_banks(n):
            return PB if since(n, 1) else [PB[1], MB]

        @block.sync
        def _(sp):
            def load(dst, src, name):
                sp.dma_start(dst, src).then_inc(s[name], 16)

            def load_x(n):
                load(xs[:, n % 2, :, :], x_mix[bass.ds(n, 1)].rearrange("a p h l -> (a p) h l"), f"x_loaded{n % 2}")

            load(wkv_sb[:, :], wkv, "loaded_wkv")
            load_x(0)
            for dst, src in ((bk_sb, bk), (bq_sb, bq), (bv_sb, bv)):
                load(dst[:, :], src, "loaded_mixw")
            load(outw_sb[:, :, :], outw, "loaded_outw")
            load(rows_sb[:, :, :], rows3, "loaded_rows")
            weights = [[(wqkv_sb[:, :, :, :], wqkv_t, "loaded_attw"), (wo_sb[:, :, :], wo_t, "loaded_attw"),
                        (row_mask[:, :], rmask, "loaded_attw")],
                       [(stage_gu[:, 0], wgu[:, 0], "loaded_ffw")], [(stage_gu[:, 1], wgu[:, 1], "loaded_ffw")],
                       [(stage_d, wd, "loaded_ffw")]]

            def next_batch(n):
                if n > 1:
                    sp.wait_ge(s["q_mm"], n - 1)
                load_x(n)

            for n in range(1, 5):
                next_batch(n)
                for dst, src, name in weights[n - 1]:
                    load(dst, src, name)
            for n in range(5, B):
                next_batch(n)

            def store_parts(n, par):
                for part in range(3):
                    sp.wait_ge(s[f"part{part + 1}"], 4 * n + 4)
                    for qk, slot in enumerate((part, 2 - part)):
                        sp.dma_start(qk_dram[par][qk, :, slot].rearrange("c p t -> p c t"),
                                     parts[:, part, 2 * qk:2 * qk + 2, :]).then_inc(s["parts_stored"], 16)

            def load_stacks(n, par, reused=True):
                sp.wait_ge(s["parts_stored"], 96 * (n + 1))
                sp.sem_inc(s["held_sync"], 1)
                if reused:
                    sp.wait_ge(s["st_mm"], 16 * (n - 1))
                for qk, (dst, runs) in enumerate([(qstack[par], RUNS_Q), (kstack[par], RUNS_K)]):
                    rows = qk_dram[par][qk].rearrange("c r (i h) t -> (r i) c (h t)", i=HD)
                    r = 0
                    for first, count in runs:
                        sp.dma_start(dst[HD * r:HD * (r + count), :].rearrange("p (c w) -> p c w", c=CH),
                                     rows[HD * first:HD * (first + count)]).then_inc(s[f"stacked{par}"], 16)
                        r += count

            def max_rows(n, par, hf):
                sp.wait_ge(s["mt_copied"], 2 * n + hf + 1)
                sp.dma_start(m_dram[hf], mT[hf][:, :]).then_inc(s["m_stored"], 16)
                sp.wait_ge(s["m_stored"], 16 * (2 * n + hf + 1))
                sp.dma_start(QS[par][STK:STK + 2, HH * hf:HH * hf + HH, :],
                             m_dram[hf].rearrange("(r h) t -> r h t", r=2)).then_inc(s[f"m_loaded{hf}"], 16)

            def store_out(n):
                sp.wait_ge(s["final_ready"], 3 * n + 3)
                sp.sem_inc(s["held_sync"], 1)
                for dst, src in ((out[bass.ds(n, 1), 0:L, :].rearrange("a (t p) m -> p (a t) m", p=P),
                                  ost[:, 0:2, :]),
                                 (out[bass.ds(n, 1), L:S, :].rearrange("a p m -> (a p) m"), ost[0:T, 2, :])):
                    sp.dma_start(dst, src).then_inc(s["out_stored"], 16)

            def step(n, par):
                max_rows(n, par, 0)
                if before(n, LAST):
                    store_parts(n + 1, 1 - par)
                if since(n, 2):
                    store_out(n - 2)
                max_rows(n, par, 1)
                if before(n, LAST):
                    load_stacks(n + 1, 1 - par, since(n, 1))

            store_parts(0, 0)
            load_stacks(0, 0, False)
            step(0, 0)
            step(1, 1)
            with sp.Fori(1, PAIRS) as i:
                step(2 * i, 0)
                step(2 * i + 1, 1)
            step(B - 2, 0)
            step(LAST, 1)
            store_out(B - 2)
            store_out(B - 1)
            sp.wait_ge(s["out_stored"], 32 * B)
            for hf in range(2):
                sp.wait_ge(s[f"m_loaded{hf}"], 16 * B)

        @block.gpsimd
        def _(pool):
            g = nc.gpsimd
            pool.dma_start(tok_sb[:, :], tokens).then_inc(s["loaded_tok"], 16)
            def load_xf(n):
                pool.dma_start(xf[:, :, :], x_flat[bass.ds(n, 1)].rearrange("a p t m -> (a p) t m")) \
                    .then_inc(s["xf_loaded"], 16)

            g.memset(ident[:, :], 0.0).then_inc(s["consts_ready"], 1)
            g.memset(identb[:, :], 0.0).then_inc(s["consts_ready"], 1)
            g.memset(causal[:, :], 0.0).then_inc(s["consts_ready"], 1)
            g.memset(nhalf[:, :], -0.5).then_inc(s["consts_ready"], 1)
            g.memset(one[:, :], 1.0).then_inc(s["consts_ready"], 1)
            pool.wait_ge(s["consts_ready"], 5)
            for m in (ident, identb):
                g.affine_select(out=m[:, :], in_=m[:, :], compare_op=ALU.not_equal, fill=1.0, base=0,
                                pattern=[[-1, P]], channel_multiplier=1).then_inc(s["consts_ready"], 1)
            g.affine_select(out=causal[:, :], in_=causal[:, :], compare_op=ALU.is_ge, fill=MASKED, base=0,
                            pattern=[[-1, P]], channel_multiplier=1).then_inc(s["consts_ready"], 1)
            pool.wait_ge(s["loaded_tok"], 16)
            for n in range(B):
                g.indirect_dma_start(emb_sb[:, n, :], None, emb,
                                     bass.IndirectOffsetOnAxis(tok_sb[:, n:n + 1], 0)) \
                    .then_inc(s["gathered"], 16)
            load_xf(0)
            for p in range(2):
                g.memset(V[p][:, :, :, :], 0.0).then_inc(s["stack_ones"], 1)
            for p in range(2):
                pool.wait_ge(s["stack_ones"], 2 + p)
                g.memset(KS[p][STK:P, :, :], 1.0).then_inc(s["stack_ones"], 1)
            pool.wait_ge(s["stack_ones"], 4)
            for p in range(2):
                for b in range(2):
                    g.memset(V[p].rearrange("p t (c b j) w -> p t c b j w", b=2, j=4)[:, :, :, b, :, HD * (1 - b)],
                             1.0).then_inc(s["stack_ones"], 1)

            pool.wait_ge(s["loaded_rows"], 16)
            bias_row, gain_row, shift_row = (rows_sb[:, r:r + 1, :].to_broadcast([P, 2, MODEL]) for r in range(3))

            def residual_in(n):
                pool.wait_ge(s["xf_loaded"], 16 * (n + 1))
                if since(n, 1):
                    pool.wait_ge(s["mix_norm"], MIX_NORM * (n - 1) + 1)
                g.tensor_tensor(xfb[:, :, :], xf[:, :, :], bias_row, ALU.add).then_inc(s["xfb_ready"], 1)
                if before(n, LAST):
                    pool.wait_ge(s["xfb_ready"], n + 1)
                    pool.sem_inc(s["held_pool"], 1)
                    load_xf(n + 1)

            def inverse_root(n, counted, count, dst, src, done):
                pool.wait_ge(s[counted], count)
                g.tensor_tensor(dst[:, :], src[:, :], nhalf[:, 0:src.shape[1]], ALU.pow).then_inc(s[done], 1)

            def norm_scales(n, ln, nm, ve, rs, nb, rstd, steps=LN_STEPS):
                inverse_root(n, ln, steps * (n + 1), rs, ve, rstd)
                pool.wait_ge(s[rstd], 2 * n + 1)
                g.tensor_tensor(nb[:, :], nm[:, :], rs[:, :], ALU.mult).then_inc(s[rstd], 1)

            def mix_scales(n):
                norm_scales(n, "mix_norm", nm_m, ve_m, rs_m, nb_m, "mix_rstd", MIX_NORM)

            def gain(n):
                pool.wait_ge(s["hn_ready"], 2 * (n + 1))
                g.tensor_tensor(hg[:, :, :], hn[:, :, :], gain_row, ALU.mult).then_inc(s["hg_ready"], 1)
                pool.wait_ge(s["hg_ready"], n + 1)
                g.tensor_tensor(resid[:, bass.ds(n, 1), 0:2, :].rearrange("p a t m -> p (a t) m"), hg[:, :, :],
                                shift_row, ALU.add).then_inc(s["resid_ready"], 1)

            def att_inverse_root(n):
                norm_scales(n, "att_ln", nm_a, ve_a, rs_a, nb_a, "att_rstd")

            def third_part(n, c):
                pool.wait_ge(s["part2"], 4 * n + c + 1)
                g.tensor_tensor(parts[:, 2, c, :], rest[:, c, :], parts[:, 1, c, :], ALU.subtract) \
                    .then_inc(s["part3"], 1)

            def keep_past(n, k):
                for kt, (_, rows) in enumerate(TILES):
                    pool.wait_ge(s["exp_done"], 24 * n + 3 * k + kt + 1)
                    pool.sem_inc(s["held_pool"], 1)
                    blk = probs[0:rows, k % 4, :, QOFF[kt]:QOFF[kt] + rows]
                    g.affine_select(out=blk, in_=blk, compare_op=ALU.is_ge, fill=0.0, base=0,
                                    pattern=[[0, 2], [1, rows]], channel_multiplier=-1) \
                        .then_inc(s["selected"], 1)

            def pack(n, c):
                pool.wait_ge(s["normed"], 4 * n + 2 * c + 2)
                if since(n, 1) and c == 0:
                    pool.wait_ge(s["oproj_mm"], 3 * n)
                g.tensor_tensor(OT[:, c, :], oh[:, 2 * c, :], oh[:, 2 * c + 1, :], ALU.add) \
                    .then_inc(s["packed"], 1)

            def low_half(n, c):
                pool.wait_ge(s["h_hi"], HC * n + c + 1)
                g.tensor_tensor(hTl[:, c, :], hh[:, c % 2, :], hTh[:, c, :], ALU.subtract) \
                    .then_inc(s["h_lo"], 1)

            def ffn_inverse_root(n):
                norm_scales(n, "ffn_ln", nm_f, ve_f, rs_f, nb_f, "ffn_rstd")

            residual_in(0)
            residual_in(1)
            mix_scales(0)

            def mix_step(n):
                gain(n - 2)
                residual_in(n)
                mix_scales(n - 1)

            mix_step(2)
            mix_step(3)
            att_inverse_root(0)
            mix_step(4)
            for c in range(4):
                third_part(0, c)
            mix_step(5)
            mix_step(6)
            att_inverse_root(1)
            mix_step(LAST)
            gain(LAST - 1)
            mix_scales(LAST)
            gain(LAST)

            def step(n):
                for item in POOL_MAX_ORDER:
                    kind, k = item[0], int(item[1])
                    if kind == "w" and since(n, 1):
                        ffn_inverse_root(n - 1)
                    elif kind == "q" and before(n, LAST):
                        if k == 0:
                            pool.wait_ge(s["parts_stored"], 96 * (n + 1))
                        third_part(n + 1, k)
                for item in POOL_ORDER:
                    kind, k = item[0], int(item[1])
                    if kind == "s":
                        keep_past(n, k)
                    elif kind == "p":
                        pack(n, k)
                    elif kind == "a" and before(n, LAST - 1):
                        att_inverse_root(n + 2)
                    elif kind == "h" and since(n, 1):
                        low_half(n - 1, k)

            step(0)
            step(1)
            with pool.Fori(2, B - 2) as n:
                step(n)
            step(B - 2)
            step(LAST)
            ffn_inverse_root(LAST)
            for c in range(HC):
                low_half(LAST, c)

        @block.scalar
        def _(act):
            a = nc.scalar
            act.dma_start(wq_sb[:, :], wq).then_inc(s["loaded_mixw"], 16)
            act.dma_start(wb_sb[:, :, :], wbt).then_inc(s["loaded_wb"], 16)
            act.dma_start(mask_sb[:, :, :], maskt).then_inc(s["loaded_wb"], 16)
            act.dma_start(pos_sb[:, :], pos).then_inc(s["loaded_text"], 16)
            act.dma_start(conv_sb[:, :, :], convw).then_inc(s["loaded_text"], 16)
            for b in range(2):
                act.dma_start(spos_sb[F * b:F * b + F, :, :], spos).then_inc(s["loaded_text"], 16)
            act.wait_ge(s["loaded_mixw"], 64)
            a.activation(ebk[:, :], bk_sb[:, :], ACT.Exp).then_inc(s["ew_ready"], 1)
            a.mul(bqh[:, :], bq_sb[:, :], 0.5).then_inc(s["ew_ready"], 1)
            act.wait_ge(s["mix_consts"], 1)
            a.activation(ew[:, :, :], wbm[:, :, :], ACT.Exp).then_inc(s["ew_ready"], 1)
            act.wait_ge(s["ew_ready"], 3)
            a.mul(ebk2[:, :], ebk[:, :], 2.0).then_inc(s["ew_ready"], 1)

            def key_exps(n):
                for t in range(2):
                    act.wait_ge(s["kv_mm"], 2 * n + t + 1)
                    if since(n, 1) and t == 0:
                        act.wait_ge(s["nd_mm"], 2 * n)
                    kv = half[0][:, 512 * t:512 * t + 512].rearrange("p (h w) -> p h w", h=2)
                    a.activation(ekv[:, t, 1, :].rearrange("p (h w) -> p h w", h=2), kv[:, :, 0:P], ACT.Exp) \
                        .then_inc(s["ek_ready"], 1)

            def query_gate(n):
                act.wait_ge(s["q_mm"], n + 1)
                if since(n, 1):
                    act.wait_ge(s["sg_ready"], n)
                a.activation(tq[:, :, :], PB[0].rearrange("p (c l) -> p c l", c=CH), ACT.Tanh, scale=0.5,
                             bias=bqh[:, 0:1]).then_inc(s["tq_ready"], 1)
                act.wait_ge(s["tq_ready"], n + 1)
                if since(n, 2):
                    act.wait_ge(s["mix_avg"], MIX_AVG * (n - 1))
                a.activation(sg[:, n % 2, :, :], tq[:, :, :], ACT.Identity, bias=one[:, 0:1]) \
                    .then_inc(s["sg_ready"], 1)

            def denominators(n):
                for c in range(CH):
                    act.wait_ge(s["nd_mm"], 2 * n + c + 1)
                    if since(n, 1) and c == 0:
                        act.wait_ge(s["mix_avg"], MIX_AVG * n)
                    a.activation(rden[:, c, :], half[1][:, 512 * c + L:512 * c + 2 * L], ACT.Copy,
                                 scale=ebk2[:, 0:1]).then_inc(s["den_ready"], 1)

            def mix_apply(n):
                act.wait_ge(s["mix_rstd"], 2 * (n + 1))
                if since(n, 1):
                    act.wait_ge(s["hg_ready"], n)
                for t in range(2):
                    a.activation(hn[:, t, :], hpre[:, t, :], ACT.Identity, bias=nb_m[:, t:t + 1],
                                 scale=rs_m[:, t:t + 1]).then_inc(s["hn_ready"], 1)

            def mix_step(n):
                denominators(n)
                key_exps(n + 1)
                if since(n, 2):
                    mix_apply(n - 2)
                query_gate(n + 1)

            act.wait_ge(s["consts_ready"], 8)
            def cast_ffn_weights(k):
                act.wait_ge(s["loaded_ffw"], 48)
                dst, src = ((wgu_sb[:, 0], stage_gu[:, 0]), (wgu_sb[:, 1], stage_gu[:, 1]),
                            (wd_sb[:, :, :], stage_d))[k]
                a.copy(dst, src).then_inc(s["ffw_cast"], 1)

            key_exps(0)
            query_gate(0)
            for n in range(2):
                mix_step(n)
            act.wait_ge(s["text_dve"], 11)
            a.activation(selx[:, :, :, :], selx[:, :, :, :], ACT.Exp).then_inc(s["text_act"], 1)
            mix_step(2)

            def xt_copy(n):
                act.wait_ge(s["xt_tr"], n + 1)
                if since(n, 1):
                    act.wait_ge(s["v_mm"], 3 * n)
                for c in range(CH):
                    a.copy(xlnT[:, c, :], prep_banks(n)[c][:, 0:S]).then_inc(s["xt_copied"], 1)

            def first_parts(n, c):
                act.wait_ge(s["qk_mm"], 4 * n + c + 1)
                if since(n, 1) and c == 0:
                    act.wait_ge(s["parts_stored"], 96 * n)
                a.copy(parts[:, 0, c, :], prep_banks(n)[c % 2][:, 0:S]).then_inc(s["part1"], 1)

            def second_parts(n, c):
                act.wait_ge(s["rest_ready"], 4 * n + c + 1)
                a.copy(parts[:, 1, c, :], rest[:, c, :]).then_inc(s["part2"], 1)

            def v_copy(n, par, t):
                r = TILES[t][1]
                act.wait_ge(s["v_mm"], 3 * n + t + 1)
                if since(n, 2) and t == 0:
                    act.wait_ge(s["pv_mm"], 4 * (n - 1))
                for b in range(2):
                    a.copy(V[par].rearrange("p t (c b j) w -> p t c b j w", b=2, j=4)
                           [0:r, t, :, b, :, HD * b:HD * b + HD],
                           prep_banks(n)[t % 2][0:r, 0:MODEL]
                           .rearrange("p (c b j w) -> p c b j w", c=2, b=2, j=4)[:, :, b]) \
                        .then_inc(s["v_copied"], 1)

            def chunk(n, c):
                first_parts(n, c)
                second_parts(n, c)

            def mt_copy(n, hf):
                act.wait_ge(s["mt_tr"], 2 * n + hf + 1)
                if since(n, 1):
                    act.wait_ge(s["m_stored"], 16 * (2 * n + hf - 1))
                a.copy(mT[hf][:, :], OB[0:2 * HH, :].bitcast(bf16)[:, 0:S]).then_inc(s["mt_copied"], 1)

            def norm_apply(n, tiles, rs, nb, rstd, applied, dst):
                act.wait_ge(s[rstd], 2 * n + 2)
                act.sem_inc(s["held_act"], 1)
                for t in tiles:
                    a.activation(dst[:, t, :], resid[:, bass.ds(n, 1), t, :].rearrange("p a m -> p (a m)"),
                                 ACT.Identity, bias=nb[:, t:t + 1], scale=rs[:, t:t + 1]).then_inc(s[applied], 1)

            def att_apply(n, tiles=range(3)):
                if since(n, 1):
                    act.wait_ge(s["xt_tr"], n)
                norm_apply(n, tiles, rs_a, nb_a, "att_rstd", "att_applied", xln)

            def ffn_apply(n):
                if since(n, 1):
                    act.wait_ge(s["fxt_tr"], n)
                norm_apply(n, range(3), rs_f, nb_f, "ffn_rstd", "ffn_applied", xlnf)

            def exps(n, k):
                if since(n, 1) or k >= 4:
                    act.wait_ge(s["pv_mm"], 4 * n + k // 2 - 1)
                for kt, (_, rows) in enumerate(TILES):
                    act.wait_ge(s["st_mm"], 16 * n + 2 * k + (1 if kt == 0 else 2))
                    off = 0 if kt < 2 else QW[1]
                    src = half[min(kt, 1)][0:rows, :].rearrange("p (h w) -> p h w", h=2)[:, :, off:off + QW[kt]]
                    a.activation(probs[0:rows, k % 4, :, QOFF[kt]:QOFF[kt] + QW[kt]], src, ACT.Exp,
                                 scale=HD ** -0.5).then_inc(s["exp_done"], 1)

            def fx_high(n):
                act.wait_ge(s["fxt_tr"], n + 1)
                if since(n, 1):
                    act.wait_ge(s["up_mm"], HC * n)
                a.copy(xfh[:, :, :], bank[2][:, :].rearrange("p (c w) -> p c w", c=2)[:, :, 0:S]) \
                    .then_inc(s["fx_hi"], 1)

            def gate_tanh(n, c, src=PB[0]):
                act.wait_ge(s["gate_mm"], HC * n + c + 1)
                if since(n, 1) or c >= 2:
                    act.wait_ge(s["a_ready"], HC * n + c - 1)
                a.activation(tg[:, c % 2, :], src[:, 0:S], ACT.Tanh, scale=0.5 / 127.0).then_inc(s["tanh_done"], 1)

            def h_high(n, c):
                act.wait_ge(s["h_ready"], HC * n + c + 1)
                if since(n, 1) and c == 0:
                    act.wait_ge(s["down_mm"], 3 * n)
                a.copy(hTh[:, c, :], hh[:, c % 2, :]).then_inc(s["h_hi"], 1)

            def step(n, par):
                for item in ACT_MAX_ORDER:
                    kind, k = item[0], int(item[1])
                    if kind == "m":
                        mt_copy(n, k)
                    elif kind in "xqv" and before(n, LAST):
                        if kind == "x":
                            if since(n, 1):
                                xt_copy(n + 1)
                        elif kind == "q":
                            chunk(n + 1, k)
                        else:
                            v_copy(n + 1, 1 - par, k)
                    elif kind in "wf" and since(n, 1):
                        (ffn_apply if kind == "w" else fx_high)(n - 1)
                for item in ACT_ORDER:
                    kind, k = item[0], int(item[1])
                    if kind == "s":
                        exps(n, k)
                    elif kind == "a" and before(n, LAST - 1):
                        att_apply(n + 2, (k,))
                    elif kind in "th" and since(n, 1):
                        (gate_tanh if kind == "t" else h_high)(n - 1, k)

            mix_step(3)
            denominators(4)
            key_exps(5)
            att_apply(0)
            mix_apply(2)
            xt_copy(0)
            query_gate(5)
            chunk(0, 0)
            chunk(0, 1)
            denominators(5)
            key_exps(6)
            chunk(0, 2)
            chunk(0, 3)
            mix_apply(3)
            query_gate(6)
            denominators(6)
            key_exps(7)
            mix_apply(4)
            query_gate(7)
            cast_ffn_weights(0)
            denominators(7)
            act.wait_ge(s["stack_ones"], 8)
            mix_apply(5)
            for t in range(3):
                v_copy(0, 0, t)
            att_apply(1)
            cast_ffn_weights(1)
            mix_apply(6)
            cast_ffn_weights(2)
            xt_copy(1)
            mix_apply(7)
            act.wait_ge(s["ffw_cast"], 3)
            step(0, 0)
            step(1, 1)
            with act.Fori(1, PAIRS) as i:
                step(2 * i, 0)
                step(2 * i + 1, 1)
            step(B - 2, 0)
            step(LAST, 1)
            ffn_apply(LAST)
            fx_high(LAST)
            for c in range(HC + 1):
                if c < HC:
                    gate_tanh(LAST, c, TAIL[c % 2][0])
                if c:
                    h_high(LAST, c - 1)

        @block.vector
        def _(dve):
            v = nc.vector
            v.memset(resid[:, :, 2, :], 0.0).then_inc(s["text_dve"], 1)
            v.memset(xcT[0:F, :, 0:2], 0.0).then_inc(s["text_dve"], 1)
            v.memset(xcT[F:F + 1, :, :], 1.0).then_inc(s["text_dve"], 1)
            dve.wait_ge(s["loaded_wb"], 32)
            v.tensor_tensor(wbm[:, :, :], wb_sb[:, :, :], mask_sb[:, :, :], ALU.mult).then_inc(s["mix_consts"], 1)
            xe = resid[0:T, :, 2, 0:F]
            x1 = resid[0:T, :, 2, 2 * F:3 * F]

            def text_embed():
                dve.wait_ge(s["loaded_text"], 64)
                dve.wait_ge(s["gathered"], 16 * B)
                dve.wait_ge(s["text_dve"], 3)
                v.scalar_tensor_tensor(out=xe, in0=emb_sb[:, :, :], scalar=float(F) ** 0.5,
                                       in1=pos_sb[:, :].unsqueeze(1).to_broadcast([T, B, F]),
                                       op0=ALU.mult, op1=ALU.add).then_inc(s["text_dve"], 1)

            def text_columns():
                dve.wait_ge(s["text_tr"], 1)
                for k, b in enumerate((PB[1], MB)):
                    v.tensor_copy(xcT[0:F, 4 * k:4 * k + 4, 2:T + 2],
                                  b[0:F, 0:4 * T].rearrange("p (b t) -> p b t", b=4)) \
                        .then_inc(s["text_dve"], 1)

            def text_softmax_in():
                dve.wait_ge(s["text_mm"], 1)
                v.tensor_copy(x1, PB[1][0:T, :].rearrange("p (n f) -> p n f", n=B)).then_inc(s["text_dve"], 1)
                dve.wait_ge(s["text_dve"], 7)
                v.tensor_reduce(smx[:, 0, :], xe, axis=AX.X, op=ALU.max).then_inc(s["text_dve"], 1)
                v.tensor_reduce(smx[:, 1, :], x1, axis=AX.X, op=ALU.max).then_inc(s["text_dve"], 1)
                dve.wait_ge(s["text_dve"], 9)
                for k, src in enumerate((xe, x1)):
                    v.tensor_tensor(selx[:, k, :, :], src, smx[:, k, :].unsqueeze(2).to_broadcast([T, B, F]),
                                    ALU.subtract).then_inc(s["text_dve"], 1)

            def text_softmax_out():
                dve.wait_ge(s["text_act"], 1)
                v.tensor_reduce(ssum[:, :, :], selx[:, :, :, :], axis=AX.X, op=ALU.add) \
                    .then_inc(s["text_dve"], 1)
                dve.wait_ge(s["text_dve"], 12)
                v.reciprocal(srec[:, :, :], ssum[:, :, :]).then_inc(s["text_dve"], 1)

            def text_selectors():
                for k, b in enumerate((PB[1], MB)):
                    dve.wait_ge(s["text_tr"], 2 + k)
                    v.tensor_copy(selT[:, k, :, :], b[:, 0:4 * T].rearrange("p (b t) -> p b t", b=4)) \
                        .then_inc(s["text_dve"], 1)

            def text_positions():
                for odd, bank_ in enumerate((PB[1], MB)):
                    dve.wait_ge(s["text_mm"], 2 + odd)
                    v.tensor_tensor(resid[0:T, :, 2, :].rearrange("p (m o) (k w f) -> p o k m w f", o=2, k=2, w=2)
                                    [:, odd, :, :, 1, :],
                                    bank_[0:T, :].rearrange("p (k m f) -> p k m f", k=2, m=B // 2),
                                    srec[:, :, :].rearrange("p k (m o) -> p o k m", o=2)[:, odd]
                                    .unsqueeze(3).to_broadcast([T, 2, B // 2, F]), ALU.mult) \
                        .then_inc(s["text_dve"], 1)

            def mix_kv(n, t):
                dve.wait_ge(s["ek_ready"], 2 * n + t + 1)
                kv = half[0][:, 512 * t:512 * t + 512].rearrange("p (h w) -> p h w", h=2)
                v.tensor_tensor(ekv[:, t, 0, :].rearrange("p (h w) -> p h w", h=2),
                                ekv[:, t, 1, :].rearrange("p (h w) -> p h w", h=2), kv[:, :, P:2 * P],
                                ALU.mult).then_inc(s["ekv_ready"], 1)

            def mix_divide(n, c):
                dve.wait_ge(s["den_ready"], 2 * n + c + 1)
                v.reciprocal(rden[:, c, :], rden[:, c, :]).then_inc(s["mix_avg"], 1)

            def mix_average(n, c):
                dve.wait_ge(s["mix_avg"], MIX_AVG * n + 2 * c + 1)
                v.scalar_tensor_tensor(out=yr[:, c, :], in0=rden[:, c, :], scalar=ebk[:, 0:1],
                                       in1=half[1][:, 512 * c:512 * c + L],
                                       op0=ALU.mult, op1=ALU.mult).then_inc(s["mix_avg"], 1)

            def mix_gate(n):
                dve.wait_ge(s["mix_avg"], MIX_AVG * n + 4)
                dve.wait_ge(s["sg_ready"], n + 1)
                if since(n, 1):
                    dve.wait_ge(s["mixout_mm"], n)
                v.scalar_tensor_tensor(out=yT[:, :, :], in0=yr[:, :, :], scalar=bvh[:, 0:1], in1=sg[:, n % 2, :, :],
                                       op0=ALU.add, op1=ALU.mult).then_inc(s["mix_avg"], 1)

            def mix_norm(n):
                dve.wait_ge(s["mixout_mm"], n + 1)
                dve.wait_ge(s["xfb_ready"], n + 1)
                if since(n, 1):
                    dve.wait_ge(s["hn_ready"], 2 * n)
                v.tensor_tensor(hpre[:, :, :], OB.rearrange("p (t m) -> p t m", t=2), xfb[:, :, :], ALU.add) \
                    .then_inc(s["mix_norm"], 1)
                dve.wait_ge(s["mix_norm"], MIX_NORM * n + 1)
                for t in range(2):
                    v.bn_stats(st_m[:, t, :], hpre[:, t, :]).then_inc(s["mix_norm"], 1)
                dve.wait_ge(s["mix_norm"], MIX_NORM * n + 3)
                dve.sem_inc(s["held_dve"], 1)
                for t in range(2):
                    v.bn_aggr(mv_m[:, t, :], st_m[:, t, :]).then_inc(s["mix_norm"], 1)
                dve.wait_ge(s["mix_norm"], MIX_NORM * n + 5)
                v.tensor_scalar(nm_m[:, :], mv_m[:, :, 0], -1.0, None, ALU.mult).then_inc(s["mix_norm"], 1)
                v.tensor_scalar(ve_m[:, :], mv_m[:, :, 1], EPS, None, ALU.add).then_inc(s["mix_norm"], 1)

            dve.wait_ge(s["loaded_mixw"], 64)
            v.tensor_scalar(bvh[:, :], bv_sb[:, :], 0.5, None, ALU.mult).then_inc(s["mix_consts"], 1)
            v.memset(mx[:, :, :], 0.0).then_inc(s["mix_consts"], 1)
            v.memset(MB[:, S:32 * SB], 1.0).then_inc(s["mix_consts"], 1)
            dve.wait_ge(s["mix_consts"], 4)
            dve.wait_ge(s["ew_ready"], 4)

            def mix_step(n, text_first=None, text_last=None):
                for c in range(CH):
                    mix_divide(n, c)
                    if before(n, LAST):
                        mix_kv(n + 1, c)
                    mix_average(n, c)
                mix_gate(n)
                if text_first:
                    text_first()
                if since(n, 1):
                    mix_norm(n - 1)
                if text_last:
                    text_last()

            mix_kv(0, 0)
            mix_kv(0, 1)
            mix_step(0, text_embed)
            mix_step(1, text_columns, text_softmax_in)
            mix_step(2, text_softmax_out, text_selectors)

            def norm_stats(n, name, stats, mv, nm, ve):
                base = LN_STEPS * n
                for t in range(3):
                    v.bn_stats(stats[:, t, :], resid[:, bass.ds(n, 1), t, :].rearrange("p a m -> p (a m)")) \
                        .then_inc(s[name], 1)
                dve.wait_ge(s[name], base + 3)
                dve.sem_inc(s["held_dve"], 1)
                for t in range(3):
                    v.bn_aggr(mv[:, t, :], stats[:, t, :]).then_inc(s[name], 1)
                dve.wait_ge(s[name], base + 6)
                v.tensor_scalar(nm[:, :], mv[:, :, 0], -1.0, None, ALU.mult).then_inc(s[name], 1)
                v.tensor_scalar(ve[:, :], mv[:, :, 1], EPS, None, ALU.add).then_inc(s[name], 1)

            def att_stats(n):
                dve.wait_ge(s["resid_ready"], n + 1)
                dve.sem_inc(s["held_dve"], 1)
                if since(n, 1):
                    dve.wait_ge(s["att_applied"], 3 * n)
                dve.sem_inc(s["held_dve"], 1)
                norm_stats(n, "att_ln", st_a, mv_a, nm_a, ve_a)

            def take_rest(n, c):
                dve.wait_ge(s["part1"], 4 * n + c + 1)
                if since(n, 1):
                    dve.wait_ge(s["part3"], 4 * n + c - 3)
                v.tensor_tensor(rest[:, c, :], prep_banks(n)[c % 2][:, 0:S], parts[:, 0, c, :], ALU.subtract) \
                    .then_inc(s["rest_ready"], 1)

            def row_max(n, u):
                t, h0, nh, per = SM[u]
                rows = TILES[t][1]
                dve.wait_ge(s["row_max_mm"], len(SM) * n + u + 1)
                src = half[u % 2][0:rows, :].rearrange("p (h w) -> p h w", h=nh)[:, :, 0:KEND[t]]
                v.tensor_reduce(mx[0:rows, t, h0:h0 + nh], src, axis=AX.X, op=ALU.max).then_inc(s["row_max"], 1)

            def split_max(n, hf):
                dve.wait_ge(s["row_max"], len(SM) * n + SMH * (hf + 1))
                if since(n, 1):
                    dve.wait_ge(s["mt_tr"], 2 * n + hf - 1)
                m = mx[:, :, HH * hf:HH * hf + HH]
                v.tensor_scalar(mhl[:, :, hf, 0, :], m, -1.0, None, ALU.mult).then_inc(s["maxima_ready"], 1)
                dve.wait_ge(s["maxima_ready"], 4 * n + 2 * hf + 1)
                v.scalar_tensor_tensor(out=mhl[:, :, hf, 1, :], in0=m, scalar=-1.0, in1=mhl[:, :, hf, 0, :],
                                       op0=ALU.mult, op1=ALU.subtract).then_inc(s["maxima_ready"], 1)

            def add_attention(n, t):
                rows = TILES[t][1]
                dve.wait_ge(s["oproj_mm"], 3 * n + (2 if t < 2 else 3))
                src = (MB[:, 0:MODEL], MB[:, MODEL:2 * MODEL], OB[:, 0:MODEL])[t]
                r = resid[0:rows, bass.ds(n, 1), t, :].rearrange("p a m -> p (a m)")
                v.tensor_tensor(r, r, src[0:rows, :], ALU.add).then_inc(s["attn_added"], 1)

            def normalise(n, g):
                ob = (OB, MB)[g % 2]
                dve.wait_ge(s["pv_mm"], 4 * n + g + 1)
                v.transpose(denT[:, :], ob[:, 0:32 * SB]).then_inc(s["norm_steps"], 1)
                dve.wait_ge(s["norm_steps"], 12 * n + 3 * g + 1)
                v.reciprocal(denr[:, :], denT[:, :].rearrange("p (b c) -> p b c", c=32)[:, :, HD * (1 - g % 2)]) \
                    .then_inc(s["norm_steps"], 1)
                dve.wait_ge(s["norm_steps"], 12 * n + 3 * g + 2)
                v.transpose(scale[:, :], denr[:, :].unsqueeze(2).to_broadcast([P, SB, 32])) \
                    .then_inc(s["norm_steps"], 1)
                dve.wait_ge(s["norm_steps"], 12 * n + 3 * g + 3)
                if since(n, 1):
                    dve.wait_ge(s["packed"], 2 * (n - 1) + g // 2 + 1)
                v.scalar_tensor_tensor(out=oh[:, g, :], in0=scale[:, 0:S], scalar=row_mask[:, g % 2:g % 2 + 1],
                                       in1=ob[:, 0:S], op0=ALU.mult, op1=ALU.mult).then_inc(s["normed"], 1)

            def ffn_stats(n):
                dve.wait_ge(s["attn_added"], 3 * n + 3)
                dve.sem_inc(s["held_dve"], 1)
                if since(n, 1):
                    dve.wait_ge(s["ffn_applied"], 3 * n)
                dve.sem_inc(s["held_dve"], 1)
                norm_stats(n, "ffn_ln", st_f, mv_f, nm_f, ve_f)

            def fx_low(n):
                dve.wait_ge(s["fx_hi"], n + 1)
                if since(n, 1):
                    dve.wait_ge(s["up_mm"], HC * n)
                v.tensor_tensor(xfl[:, :, :], bank[2][:, :].rearrange("p (c w) -> p c w", c=2)[:, :, 0:S],
                                xfh[:, :, :], ALU.subtract).then_inc(s["fx_lo"], 1)

            def hidden(n, c, banks=PB):
                dve.wait_ge(s["tanh_done"], HC * n + c + 1)
                v.scalar_tensor_tensor(out=ag[:, c % 2, :], in0=tg[:, c % 2, :], scalar=1.0, in1=banks[0][:, 0:S],
                                       op0=ALU.add, op1=ALU.mult).then_inc(s["a_ready"], 1)
                dve.wait_ge(s["a_ready"], HC * n + c + 1)
                dve.wait_ge(s["up_mm"], HC * n + c + 1)
                if since(n, 1) or c >= 2:
                    dve.wait_ge(s["h_lo"], HC * n + c - 1)
                v.scalar_tensor_tensor(out=hh[:, c % 2, :], in0=ag[:, c % 2, :], scalar=HSCALE / (2 * 127.0 ** 2),
                                       in1=banks[1][:, 0:S], op0=ALU.mult, op1=ALU.mult).then_inc(s["h_ready"], 1)

            def finish(n, t, banks=None):
                if since(n, 1) and t == 0:
                    dve.wait_ge(s["out_stored"], 32 * n)
                rows = TILES[t][1]
                dve.wait_ge(s["down_mm"], 3 * n + (2 if t < 2 else 3))
                src = (banks or (MB[:, 0:MODEL], MB[:, MODEL:2 * MODEL], OB[:, 0:MODEL]))[t]
                v.scalar_tensor_tensor(out=ost[0:rows, t, :], in0=src[0:rows, :], scalar=1.0 / (127.0 * HSCALE),
                                       in1=resid[0:rows, bass.ds(n, 1), t, :].rearrange("p a m -> p (a m)"),
                                       op0=ALU.mult, op1=ALU.add).then_inc(s["final_ready"], 1)

            def step(n):
                for item in DVE_MAX_ORDER:
                    kind, k = item[0], int(item[1:])
                    if kind == "r":
                        row_max(n, k)
                    elif kind == "m":
                        split_max(n, k)
                    elif kind == "q" and before(n, LAST):
                        take_rest(n + 1, k)
                    elif kind == "o" and since(n, 1):
                        add_attention(n - 1, k)
                    elif kind == "w" and since(n, 1):
                        ffn_stats(n - 1)
                    elif kind == "f" and since(n, 1):
                        fx_low(n - 1)
                    elif kind == "d" and since(n, 2):
                        finish(n - 2, k)
                for item in DVE_ORDER:
                    kind, k = item[0], int(item[1])
                    if kind == "n":
                        normalise(n, k)
                    elif kind == "r" and before(n, LAST):
                        row_max(n + 1, k)
                    elif kind == "a" and before(n, LAST - 1):
                        att_stats(n + 2)
                    elif kind == "h" and since(n, 1):
                        hidden(n - 1, k)

            def text_out():
                text_positions()
                dve.wait_ge(s["text_dve"], 17)
                att_stats(0)

            mix_step(3, None, text_out)

            def rests(c0):
                take_rest(0, c0)
                take_rest(0, c0 + 1)

            mix_step(4, lambda: rests(0))
            mix_step(5, lambda: rests(2))
            mix_step(6, lambda: att_stats(1))
            mix_step(LAST)
            row_max(0, 0)
            row_max(0, 1)
            mix_norm(LAST)
            dve.wait_ge(s["loaded_attw"], 48)
            step(0)
            step(1)
            with dve.Fori(2, B - 2) as n:
                step(n)
            step(B - 2)
            step(LAST)
            for t in range(3):
                add_attention(LAST, t)
            ffn_stats(LAST)
            for t in range(3):
                finish(B - 2, t, RING_DOWN)
            fx_low(LAST)
            for c in range(HC):
                hidden(LAST, c, TAIL[c % 2])
            for t in range(3):
                finish(LAST, t, TAIL_DOWN)

        @block.tensor
        def _(pe):
            mm, tr = nc.tensor.matmul, nc.tensor.transpose
            def text_transpose():
                pe.wait_ge(s["consts_ready"], 8)
                pe.wait_ge(s["text_dve"], 4)
                for n in range(B):
                    last = tr((PB[1], MB)[n // 4][0:F, T * (n % 4):T * (n % 4) + T], resid[0:T, n, 2, 0:F],
                              ident[0:T, 0:T])
                last.then_inc(s["text_tr"], 1)

            def text_convolve():
                pe.wait_ge(s["loaded_text"], 64)
                pe.wait_ge(s["text_dve"], 6)
                for n in range(B):
                    for tap in range(3):
                        last = mm(PB[1][0:T, n * F:(n + 1) * F], xcT[:, n, tap:tap + T], conv_sb[:, tap, :],
                                  start=(tap == 0), stop=(tap == 2))
                last.then_inc(s["text_mm"], 1)

            def text_transpose_selectors():
                pe.wait_ge(s["text_act"], 1)
                for k, b in enumerate((PB[1], MB)):
                    for m in range(B // 2):
                        last = tr(b[:, T * m:T * m + T], selx[:, k, 2 * m:2 * m + 2, :].rearrange("p n f -> p (n f)"),
                                  ident[0:T, 0:T])
                    last.then_inc(s["text_tr"], 1)

            def text_soft_positions():
                pe.wait_ge(s["text_dve"], 15)
                for odd, bank_ in enumerate((PB[1], MB)):
                    r0 = F * odd
                    for k in range(2):
                        for m in range(B // 2):
                            o = F * (B // 2 * k + m)
                            last = mm(bank_[0:T, o:o + F], selT[r0:r0 + F, k, m, :], spos_sb[r0:r0 + F, k, :],
                                      start=True, stop=True)
                    last.then_inc(s["text_mm"], 1)

            def key_value(n):
                pe.wait_ge(s[f"x_loaded{n % 2}"], 16 * (n // 2 + 1))
                for t in range(2):
                    if since(n, 1):
                        pe.wait_ge(s["ekv_ready"], 2 * n)
                    for h in range(2):
                        last = mm(half[0][:, 512 * t + 256 * h:512 * t + 256 * h + 256],
                                  xs[:, n % 2, h, P * t:P * t + P], wkv_sb[:, :], start=True, stop=True)
                    last.then_inc(s["kv_mm"], 1)

            def queries(n):
                if since(n, 1):
                    pe.wait_ge(s["tq_ready"], n)
                for h in range(2):
                    last = mm(PB[0][:, L * h:L * h + L], wq_sb[:, :], xs[:, n % 2, h, :], start=True, stop=True)
                last.then_inc(s["q_mm"], 1)

            def averages(n):
                pe.wait_ge(s["ekv_ready"], 2 * n + 2)
                for c in range(CH):
                    if since(n, 1):
                        pe.wait_ge(s["mix_avg"], MIX_AVG * (n - 1) + 2 * c + 2)
                    for nd in range(2):
                        for t in range(2):
                            last = mm(half[1][:, 512 * c + L * nd:512 * c + L * nd + L],
                                      ekv[:, t, nd, P * c:P * c + P], ew[:, t, :], start=(t == 0), stop=(t == 1))
                    last.then_inc(s["nd_mm"], 1)

            def mix_project(n):
                pe.wait_ge(s["mix_avg"], MIX_AVG * (n + 1))
                if since(n, 1):
                    pe.wait_ge(s["mix_norm"], MIX_NORM * (n - 1) + 1)
                for t in range(2):
                    for c in range(CH):
                        last = mm(OB[:, MODEL * t:MODEL * t + MODEL], yT[:, c, P * t:P * t + P], outw_sb[:, c, :],
                                  start=(c == 0), stop=(c == CH - 1))
                last.then_inc(s["mixout_mm"], 1)

            def mix_step(n):
                averages(n)
                key_value(n + 1)
                if since(n, 1):
                    mix_project(n - 1)
                queries(n + 1)

            pe.wait_ge(s["loaded_wkv"], 16)
            key_value(0)
            pe.wait_ge(s["loaded_mixw"], 64)
            queries(0)
            pe.wait_ge(s["ew_ready"], 4)
            mix_step(0)
            averages(1)
            key_value(2)
            text_transpose()
            pe.wait_ge(s["loaded_outw"], 16)
            mix_project(0)
            queries(2)
            text_convolve()
            averages(2)
            key_value(3)
            text_transpose_selectors()
            mix_project(1)
            queries(3)

            def transpose_tokens(src, name, banks=PB):
                for t, (t0, rows) in enumerate(TILES):
                    for c in range(CH):
                        last = tr(banks[c][:, t0:t0 + rows], src[0:rows, t, P * c:P * c + P], ident[0:rows, 0:rows])
                last.then_inc(s[name], 1)

            def att_transpose(n):
                pe.wait_ge(s["att_applied"], 3 * (n + 1))
                if since(n, 3):
                    pe.wait_ge(s["h_ready"], HC * (n - 2))
                if since(n, 1):
                    pe.wait_ge(s["v_copied"], 6 * n)
                if not since(n, 2):
                    pe.wait_ge(s["text_dve"], 17)
                    pe.wait_ge(s["tq_ready"], B if n == 1 else 1)
                transpose_tokens(xln, "xt_tr", prep_banks(n))

            def query_key(n, c):
                if c < 2:
                    pe.wait_ge(s["xt_copied"], 2 * (n + 1))
                else:
                    pe.wait_ge(s["rest_ready"], 4 * n + c - 1)
                for kc in range(CH):
                    last = mm(prep_banks(n)[c % 2][:, 0:S],
                              wqkv_sb[:, c // 2, kc, P * (c % 2):P * (c % 2) + P], xlnT[:, kc, :],
                              start=(kc == 0), stop=(kc == CH - 1))
                last.then_inc(s["qk_mm"], 1)

            def values(n, t):
                if t < 2:
                    pe.wait_ge(s["rest_ready"], 4 * n + 3 + t)
                else:
                    pe.wait_ge(s["v_copied"], 6 * n + 2)
                t0, rows = TILES[t]
                for kc in range(CH):
                    last = mm(prep_banks(n)[t % 2][0:rows, 0:MODEL], xlnT[:, kc, t0:t0 + rows], wqkv_sb[:, 2, kc, :],
                              start=(kc == 0), stop=(kc == CH - 1))
                last.then_inc(s["v_mm"], 1)

            def scores_for_max(n, par, u):
                t, h0, nh, per = SM[u]
                t0, rows = TILES[t]
                if u >= 2:
                    pe.wait_ge(s["row_max"], len(SM) * n + u - 1)
                elif since(n, 1):
                    pe.wait_ge(s["exp_done"], 24 * n - (2 if u == 0 else 0))
                for i in range(nh):
                    h = h0 + i
                    o = 512 * (i // per) + KEND[t] * (i % per)
                    mm(half[u % 2][0:rows, o:o + KEND[t]], QS[par][0:STK, h, t0:t0 + rows],
                       KS[par][0:STK, h, 0:KEND[t]],
                       start=True, stop=False)
                    last = mm(half[u % 2][0:rows, o + t0:o + t0 + rows], identb[:, 0:rows], causal[:, 0:rows],
                              start=False, stop=True)
                last.then_inc(s["row_max_mm"], 1)

            def transpose_max(n, hf):
                pe.wait_ge(s["maxima_ready"], 4 * n + 2 * hf + 2)
                if hf == 0 and since(n, 1):
                    pe.wait_ge(s["attn_added"], 3 * n)
                elif hf == 0:
                    pe.wait_ge(s["mix_norm"], MIX_NORM * LAST + 1)
                if hf == 1 and since(n, 2):
                    pe.wait_ge(s["final_ready"], 3 * (n - 1))
                elif hf == 1:
                    pe.wait_ge(s["mt_copied"], 2 * n + 1)
                for t, (t0, rows) in enumerate(TILES):
                    last = tr(OB[0:2 * HH, :].bitcast(bf16)[:, t0:t0 + rows],
                              mhl[0:rows, t, hf, :, :].rearrange("p a h -> p (a h)"), identb[0:rows, 0:rows])
                last.then_inc(s["mt_tr"], 1)

            def scores_transposed(n, par, k):
                for kt, (t0, rows) in enumerate(TILES):
                    if kt < 2:
                        if k == 0:
                            pe.wait_ge(s["row_max"], len(SM) * n + 13 + kt)
                        else:
                            pe.wait_ge(s["exp_done"], 24 * n + 3 * (k - 1) + (1 if kt == 0 else 3))
                    off = 0 if kt < 2 else QW[1]
                    for i in range(2):
                        o = 512 * i + off
                        last = mm(half[min(kt, 1)][0:rows, o:o + QW[kt]], KS[par][0:STK + 2, 2 * k + i, t0:t0 + rows],
                                  QS[par][0:STK + 2, 2 * k + i, t0:S], start=True, stop=True)
                    if kt != 1:
                        last.then_inc(s["st_mm"], 1)

            def weighted_values(n, par, g):
                pe.wait_ge(s["selected"], 24 * n + 6 * (g + 1))
                if g >= 2:
                    pe.wait_ge(s["normed"], 4 * n + g - 1)
                elif g == 0:
                    pe.wait_ge(s["mt_copied"], 2 * n + 2)
                for kt, (t0, rows) in enumerate(TILES):
                    for j in range(4):
                        h = 4 * g + j
                        last = mm((OB, MB)[g % 2][32 * j:32 * j + 32, t0:S], V[par][0:rows, kt, h, :],
                                  probs[0:rows, (h // 2) % 4, h % 2, QOFF[kt]:QOFF[kt] + QW[kt]],
                                  start=(kt == 0), stop=(kt == 2))
                last.then_inc(s["pv_mm"], 1)

            def out_project(n, t):
                t0, rows = TILES[t]
                pe.wait_ge(s["normed"], 4 * n + 4)
                pe.wait_ge(s["packed"], 2 * n + 2)
                dst = (MB[:, 0:MODEL], MB[:, MODEL:2 * MODEL], OB[:, 0:MODEL])[t]
                for c in range(2):
                    last = mm(dst[0:rows, :], OT[:, c, t0:t0 + rows], wo_sb[:, c, :], start=(c == 0), stop=(c == 1))
                last.then_inc(s["oproj_mm"], 1)

            def ffn_transpose(n):
                pe.wait_ge(s["ffn_applied"], 3 * (n + 1))
                if not before(n, LAST):
                    pe.wait_ge(s["h_ready"], HC * n)
                else:
                    pe.wait_ge(s["v_copied"], 6 * B if isinstance(n, int) and n == B - 2 else 6 * (n + 3))
                transpose_tokens(xlnf, "fxt_tr")

            def ffn_product(n, c, gu, dst):
                for kc in range(CH):
                    for x in (xfh, xfl):
                        last = mm(dst[:, 0:S], wgu_sb[:, gu, kc, P * c:P * c + P], x[:, kc, :],
                                  start=(kc == 0 and x is xfh), stop=(kc == CH - 1 and x is xfl))
                last.then_inc(s[("gate_mm", "up_mm")[gu]], 1)

            def gate(n, c):
                if c == 0:
                    pe.wait_ge(s["fx_lo"], n + 1)
                else:
                    pe.wait_ge(s["a_ready"], HC * n + c)
                ffn_product(n, c, 0, PB[0])

            def up(n, c):
                if c:
                    pe.wait_ge(s["h_ready"], HC * n + c)
                ffn_product(n, c, 1, PB[1])

            def down_products(dst, t, c):
                t0, rows = TILES[t]
                for x in (hTh, hTl):
                    last = mm(dst[0:rows, :], x[:, c, t0:t0 + rows], wd_sb[:, c, :],
                              start=(c == 0 and x is hTh), stop=(c == HC - 1 and x is hTl))
                return last

            def down(n, t, banks=None):
                if t == 0:
                    pe.wait_ge(s["h_hi"], HC * (n + 1))
                    pe.wait_ge(s["h_lo"], HC * (n + 1))
                    if banks:
                        pe.wait_ge(s["exp_done"], 24 * B)
                    else:
                        pe.wait_ge(s["attn_added"], 3 * (n + 2))
                if t == 2 and not banks:
                    pe.wait_ge(s["mt_copied"], 2 * (n + 2) + 1)
                dst = (banks or (MB[:, 0:MODEL], MB[:, MODEL:2 * MODEL], OB[:, 0:MODEL]))[t]
                for c in range(HC):
                    last = down_products(dst, t, c)
                last.then_inc(s["down_mm"], 1)

            def stacks_loaded(par, turns):
                pe.wait_ge(s[f"stacked{par}"], 16 * (len(RUNS_Q) + len(RUNS_K)) * turns)

            def step(n, par, next_turns):
                for item in PE_MAX_ORDER:
                    kind, k = item[0], int(item[1:])
                    if kind == "r":
                        scores_for_max(n, par, k)
                    elif kind == "m":
                        transpose_max(n, k)
                    elif kind in "xqv" and before(n, LAST):
                        if kind == "x":
                            att_transpose(n + 1)
                        elif kind == "q":
                            query_key(n + 1, k)
                        else:
                            values(n + 1, k)
                    elif kind == "o" and since(n, 1):
                        out_project(n - 1, k)
                    elif kind == "f" and since(n, 1):
                        ffn_transpose(n - 1)
                    elif kind == "d" and since(n, 2):
                        down(n - 2, k)
                for item in PE_ORDER:
                    kind, k = item[0], int(item[1])
                    if kind == "s":
                        if k in (0, 4):
                            pe.wait_ge(s[f"m_loaded{k // 4}"], 16 * (n + 1))
                        scores_transposed(n, par, k)
                    elif kind == "w":
                        weighted_values(n, par, k)
                    elif kind == "r" and before(n, LAST):
                        if k == 0:
                            stacks_loaded(1 - par, next_turns)
                        scores_for_max(n + 1, 1 - par, k)
                    elif kind in "gu" and since(n, 1):
                        (gate if kind == "g" else up)(n - 1, k)

            averages(3)
            key_value(4)
            mix_project(2)
            text_soft_positions()
            queries(4)
            averages(4)
            key_value(5)
            mix_project(3)
            queries(5)
            att_transpose(0)
            pe.wait_ge(s["loaded_attw"], 48)
            query_key(0, 0)
            query_key(0, 1)
            averages(5)
            key_value(6)
            query_key(0, 2)
            query_key(0, 3)
            mix_project(4)
            queries(6)
            averages(6)
            key_value(7)
            mix_project(5)
            queries(7)
            averages(LAST)
            mix_project(LAST - 1)
            for t in range(3):
                values(0, t)
            pe.wait_ge(s["ekv_ready"], 2 * B)
            pe.wait_ge(s["mix_avg"], MIX_AVG * LAST + 4)
            stacks_loaded(0, 1)
            scores_for_max(0, 0, 0)
            scores_for_max(0, 0, 1)
            mix_project(LAST)
            pe.wait_ge(s["stack_ones"], 8)
            step(0, 0, 1)
            step(1, 1, 2)
            with pe.Fori(1, PAIRS) as i:
                step(2 * i, 0, i + 1)
                step(2 * i + 1, 1, i + 2)
            step(B - 2, 0, B // 2)
            step(LAST, 1, None)
            down(B - 2, 0, RING_DOWN)
            for t in range(3):
                out_project(LAST, t)
            down(B - 2, 1, RING_DOWN)
            down(B - 2, 2, RING_DOWN)
            ffn_transpose(LAST)
            for c in range(HC + 2):
                if c < HC:
                    if c == 0:
                        pe.wait_ge(s["fx_lo"], B)
                    elif c >= 2:
                        pe.wait_ge(s["a_ready"], HC * LAST + c - 1)
                    ffn_product(LAST, c, 0, TAIL[c % 2][0])
                    if c >= 2:
                        pe.wait_ge(s["h_ready"], HC * LAST + c - 1)
                    ffn_product(LAST, c, 1, TAIL[c % 2][1])
                if c == 2:
                    pe.wait_ge(s["final_ready"], 3 * LAST)
                    pe.wait_ge(s["attn_added"], 3 * B)
                if c >= 2:
                    pe.wait_ge(s["h_hi"], HC * LAST + c - 1)
                    pe.wait_ge(s["h_lo"], HC * LAST + c - 1)
                    for t in range(3):
                        last = down_products(TAIL_DOWN[t], t, c - 2)
                        if c == HC + 1:
                            last.then_inc(s["down_mm"], 1)


def kernel(**inputs):
    import concourse.bacc as bacc
    from concourse import mybir as mb
    from concourse.bass_utils import run_bass_kernel_spmd

    x = {k: np.asarray(v) for k, v in inputs.items()}
    z = np.zeros((F, F), np.float32)

    def halves(w):
        return w.T.reshape(-1, P, w.shape[0]).transpose(1, 0, 2)

    def two_heads(*ws):
        top = [m for w in ws for m in (w.T, z)]
        low = [m for w in ws for m in (z, w.T)]
        return np.concatenate([np.concatenate(top, 1), np.concatenate(low, 1)], 0)

    def by_column(w):
        return w.reshape(CH, HH, HD, MODEL).transpose(0, 2, 1, 3).reshape(MODEL, MODEL)

    def column(b):
        return np.concatenate([b, b]).reshape(P, 1)

    depth = F // 2
    angle = np.arange(T, dtype=np.float32)[:, None] * \
        (np.float32(1.0) / np.float32(2500) ** (np.arange(depth, dtype=np.float32)[None, :] / np.float32(depth)))
    pos = np.concatenate([np.sin(angle), np.cos(angle)], -1).astype(np.float32)

    conv = np.concatenate([x["L0_txt_conv_w"].transpose(1, 0, 2), np.zeros((1, 3, F), np.float32)], 0)
    conv[F, 2, :] = x["L0_txt_conv_b"]
    wo = x["L0_attn_o_proj_weight"].T.reshape(2, 2, 4, HD, MODEL).transpose(2, 1, 3, 0, 4)
    rmask = (np.arange(P)[:, None] // HD % 2 == np.arange(2)[None, :]).astype(np.float32)
    xm = x["x"]
    arrays = dict(
        x_mix=xm.transpose(0, 3, 1, 2).reshape(B, 2, 2, F, L).transpose(0, 2, 3, 1, 4).reshape(B, P, 2, L),
        x_flat=xm.transpose(0, 2, 3, 1).reshape(B, 2, P, MODEL).transpose(0, 2, 1, 3),
        tokens=x["x_txt"].T, pos=pos,
        wkv=two_heads(x["L0_tok_Wk_w"], x["L0_tok_Wv_w"]), wq=two_heads(x["L0_tok_Wq_w"]),
        bq=column(x["L0_tok_Wq_b"]), bk=column(x["L0_tok_Wk_b"]), bv=column(x["L0_tok_Wv_b"]),
        wbt=halves(x["L0_tok_w_bias"]), maskt=halves(x["L0_tok_local_mask"]),
        outw=x["L0_tok_out_w"].reshape(CH, P, MODEL).transpose(1, 0, 2),
        rows3=np.broadcast_to(np.stack([x["L0_tok_out_b"], x["L0_tok_ln_g"], x["L0_tok_ln_b"]])[None],
                              (P, 3, MODEL)),
        emb=x["L0_txt_emb_table"], convw=conv,
        spos=np.stack([x["L0_txt_spos0"], x["L0_txt_spos1"]], 1),
        wqkv=np.stack([halves(by_column(x["L0_attn_q_proj_weight"])), halves(by_column(x["L0_attn_k_proj_weight"])),
                       halves(x["L0_attn_v_proj_weight"])], 1),
        wo=wo.reshape(P, 2, MODEL), rmask=rmask,
        wgu=np.stack([halves(x["L0_ffn_w_gate"]), halves(x["L0_ffn_w_up"])], 1),
        wd=halves(x["L0_ffn_w_down"]),
    )
    nc = bacc.Bacc("TRN2", target_bir_lowering=False, num_devices=1)
    sent, args = {}, []
    for name, a in arrays.items():
        a = np.ascontiguousarray(a)
        sent[f"in_{name}"] = a
        dt = mb.dt.uint8 if a.dtype == bool else mb.dt.from_np(a.dtype)
        args.append(nc.dram_tensor(f"in_{name}", a.shape, dt, kind="ExternalInput").ap())
    args.append(nc.dram_tensor("out", (B, S, MODEL), mb.dt.float32, kind="ExternalOutput").ap())
    build(nc, *args)
    r = run_bass_kernel_spmd(nc, [sent], core_ids=[0])
    return r.results[0]["out"]
```
